# Optimizing a Trainium2 kernel written in Bass

```python
import numpy as np
import jax
import jax.numpy as jnp

def _softmax(x, axis=-1):
    return jax.nn.softmax(x, axis=axis)

def _gelu(x):
    return jax.nn.gelu(x, approximate=True)

def _silu(x):
    return jax.nn.silu(x)

def _sigmoid(x):
    return jax.nn.sigmoid(x)

def _layernorm(x, axis=-1, eps=1e-05):
    m = jnp.mean(x, axis=axis, keepdims=True)
    v = jnp.var(x, axis=axis, keepdims=True)
    return (x - m) / jnp.sqrt(v + eps)

def _scatter_add(tgt, idx, src, axis=0):
    return tgt.at[idx].add(src)

def _segment_sum(src, seg, n):
    return jax.ops.segment_sum(src, seg, n)
kernel_name = 'mk_seq_preln_d2_jaxref_r4_528761'

def setup_inputs(seed: int=0):
    np.random.seed(seed)
    _w = jnp.asarray

    def _L0_attn_setup():
        import math
        import jax, jax.numpy as jnp
        import numpy as np
        B, N, D = (4, 1024, 256)
        H, M = (16, 64)
        HD = D // H
        EPS = 1e-06

        def favor_features(data, proj):
            hd = data.shape[-1]
            m = proj.shape[0]
            dn = data / math.sqrt(hd)
            norm_sq = 0.5 * jnp.sum(dn * dn, axis=-1, keepdims=True)
            comb = jnp.einsum('bhnd,md->bhnm', dn, proj) - norm_sq
            comb = comb - jnp.max(comb, axis=-1, keepdims=True)
            return jnp.exp(comb) / math.sqrt(m) + EPS
        key = jax.random.key(seed)
        ks = jax.random.split(key, 6)
        x = jax.random.normal(ks[0], (B, N, D), dtype=jnp.float32)
        qkv_w = jax.random.normal(ks[1], (3 * D, D), dtype=jnp.float32) * (1.0 / math.sqrt(D))
        qkv_b = jnp.zeros((3 * D,), dtype=jnp.float32)
        proj_w = jax.random.normal(ks[2], (D, D), dtype=jnp.float32) * (1.0 / math.sqrt(D))
        proj_b = jnp.zeros((D,), dtype=jnp.float32)
        pm = jax.random.normal(ks[3], (M, HD), dtype=jnp.float32)
        pm = pm / jnp.linalg.norm(pm, axis=-1, keepdims=True)
        return {'x': x, 'qkv_w': qkv_w, 'qkv_b': qkv_b, 'proj_w': proj_w, 'proj_b': proj_b, 'projection_matrix': pm}
    _L0_attn_in = _L0_attn_setup()

    def _L0_ffn_setup():
        import jax, jax.numpy as jnp
        import numpy as np
        LN_EPS = 1e-05
        NORM_EPS = 1e-12

        def _layernorm(x, gamma, beta):
            mu = x.mean(axis=-1, keepdims=True)
            var = ((x - mu) ** 2).mean(axis=-1, keepdims=True)
            return (x - mu) * jax.lax.rsqrt(var + LN_EPS) * gamma + beta

        def _l2norm(x, axis):
            n = jnp.sqrt((x ** 2).sum(axis=axis, keepdims=True))
            return x / jnp.maximum(n, NORM_EPS)
        key = jax.random.key(seed)
        ks = jax.random.split(key, 4)
        B, N, D, E, S, H = (64, 64, 256, 16, 16, 64)
        x = jax.random.normal(ks[0], (B, N, D), dtype=jnp.float32)
        mu = jax.random.normal(ks[1], (D, E, S), dtype=jnp.float32) / np.sqrt(D)
        w1 = jax.random.normal(ks[2], (E, D, H), dtype=jnp.float32) * np.sqrt(2.0 / D)
        w2 = jax.random.normal(ks[3], (E, H, D), dtype=jnp.float32) * np.sqrt(2.0 / (H + D))
        return {'x': x, 'ln_gamma': jnp.ones((D,), jnp.float32), 'ln_beta': jnp.zeros((D,), jnp.float32), 'mu': mu, 'scale': jnp.ones((1,), jnp.float32), 'w1': w1, 'b1': jnp.zeros((E, H), jnp.float32), 'w2': w2, 'b2': jnp.zeros((E, D), jnp.float32)}
    _L0_ffn_in = _L0_ffn_setup()

    def _L1_attn_setup():
        import jax, jax.numpy as jnp
        import numpy as np
        D_MODEL = 256
        N_HEADS = 16
        HEAD_DIM = D_MODEL // N_HEADS
        ROPE_BASE = 10000.0

        def _rope_tables(T, dtype=jnp.float32):
            half = HEAD_DIM // 2
            inv_freq = 1.0 / ROPE_BASE ** (jnp.arange(0, HEAD_DIM, 2, dtype=jnp.float32) / HEAD_DIM)
            t = jnp.arange(T, dtype=jnp.float32)
            freqs = jnp.einsum('i,j->ij', t, inv_freq)
            return (jnp.cos(freqs).astype(dtype), jnp.sin(freqs).astype(dtype))

        def _apply_rotary(x, cos, sin):
            B, T, H, D = x.shape
            xr = x.reshape(B, T, H, D // 2, 2)
            x0, x1 = (xr[..., 0], xr[..., 1])
            c = cos[None, :, None, :]
            s = sin[None, :, None, :]
            out = jnp.stack([x0 * c - x1 * s, x0 * s + x1 * c], axis=-1)
            return out.reshape(B, T, H, D)
        key = jax.random.key(seed)
        ks = jax.random.split(key, 5)
        x = jax.random.normal(ks[0], (4, 256, D_MODEL), dtype=jnp.float32)
        init = 1.0 / np.sqrt(D_MODEL)
        Wq = jax.random.uniform(ks[1], (D_MODEL, D_MODEL), jnp.float32, -init, init)
        Wk = jax.random.uniform(ks[2], (D_MODEL, D_MODEL), jnp.float32, -init, init)
        Wv = jax.random.uniform(ks[3], (D_MODEL, D_MODEL), jnp.float32, -init, init)
        Wo = jax.random.uniform(ks[4], (D_MODEL, D_MODEL), jnp.float32, -init, init)
        return {'x': x, 'Wq': Wq, 'Wk': Wk, 'Wv': Wv, 'Wo': Wo}
    _L1_attn_in = _L1_attn_setup()

    def _L1_ffn_setup():
        import jax, jax.numpy as jnp
        import numpy as np
        TOP_K = 2
        key = jax.random.key(seed)
        k1, k2, k3 = jax.random.split(key, 3)
        B, S, H, E, D = (4, 256, 256, 32, 256)
        x = jax.random.normal(k1, (B, S, H), dtype=jnp.float32)
        router_w = jax.random.normal(k2, (E, H), dtype=jnp.float32) * (1.0 / np.sqrt(H))
        bound = float(np.sqrt(6.0 / ((1.0 + 0.01 ** 2) * H)))
        expert_weights = jax.random.uniform(k3, (E, H, D), dtype=jnp.float32, minval=-bound, maxval=bound)
        return {'x': x, 'router_w': router_w, 'expert_weights': expert_weights}
    _L1_ffn_in = _L1_ffn_setup()
    _d = {'L0_attn_x': _L0_attn_in['x'], 'L0_attn_qkv_w': _L0_attn_in['qkv_w'], 'L0_attn_qkv_b': _L0_attn_in['qkv_b'], 'L0_attn_proj_w': _L0_attn_in['proj_w'], 'L0_attn_proj_b': _L0_attn_in['proj_b'], 'L0_attn_projection_matrix': _L0_attn_in['projection_matrix'], 'L0_ffn_ln_gamma': _L0_ffn_in['ln_gamma'], 'L0_ffn_ln_beta': _L0_ffn_in['ln_beta'], 'L0_ffn_mu': _L0_ffn_in['mu'], 'L0_ffn_scale': _L0_ffn_in['scale'], 'L0_ffn_w1': _L0_ffn_in['w1'], 'L0_ffn_b1': _L0_ffn_in['b1'], 'L0_ffn_w2': _L0_ffn_in['w2'], 'L0_ffn_b2': _L0_ffn_in['b2'], 'L1_attn_Wq': _L1_attn_in['Wq'], 'L1_attn_Wk': _L1_attn_in['Wk'], 'L1_attn_Wv': _L1_attn_in['Wv'], 'L1_attn_Wo': _L1_attn_in['Wo'], 'L1_ffn_router_w': _L1_ffn_in['router_w'], 'L1_ffn_expert_weights': _L1_ffn_in['expert_weights']}
    _x0 = _d['L0_attn_x']
    _d['L0_attn_x'] = jax.random.normal(jax.random.fold_in(jax.random.key(seed), 1), (4, 2048, 256), dtype=_x0.dtype)
    del _x0
    return _d

def reference(L0_attn_x, L0_attn_qkv_w, L0_attn_qkv_b, L0_attn_proj_w, L0_attn_proj_b, L0_attn_projection_matrix, L0_ffn_ln_gamma, L0_ffn_ln_beta, L0_ffn_mu, L0_ffn_scale, L0_ffn_w1, L0_ffn_b1, L0_ffn_w2, L0_ffn_b2, L1_attn_Wq, L1_attn_Wk, L1_attn_Wv, L1_attn_Wo, L1_ffn_router_w, L1_ffn_expert_weights):

    def _L0_attn_ref(x, qkv_w, qkv_b, proj_w, proj_b, projection_matrix):
        import math
        import jax, jax.numpy as jnp
        import numpy as np
        B, N, D = (4, 1024, 256)
        H, M = (16, 64)
        HD = D // H
        EPS = 1e-06

        def favor_features(data, proj):
            hd = data.shape[-1]
            m = proj.shape[0]
            dn = data / math.sqrt(hd)
            norm_sq = 0.5 * jnp.sum(dn * dn, axis=-1, keepdims=True)
            comb = jnp.einsum('bhnd,md->bhnm', dn, proj) - norm_sq
            comb = comb - jnp.max(comb, axis=-1, keepdims=True)
            return jnp.exp(comb) / math.sqrt(m) + EPS
        b, n, d = x.shape
        qkv = x @ qkv_w.T + qkv_b
        qkv = qkv.reshape(b, n, 3, H, HD)
        qkv = jnp.transpose(qkv, (2, 0, 3, 1, 4))
        q, k, v = (qkv[0], qkv[1], qkv[2])
        q_p = favor_features(q, projection_matrix)
        k_p = favor_features(k, projection_matrix)
        kv = jnp.einsum('bhnm,bhnv->bhmv', k_p, v)
        out = jnp.einsum('bhnm,bhmv->bhnv', q_p, kv)
        k_sum = jnp.sum(k_p, axis=2)
        normalizer = jnp.einsum('bhnm,bhm->bhn', q_p, k_sum)[..., None]
        out = out / (normalizer + EPS)
        out = jnp.transpose(out, (0, 2, 1, 3)).reshape(b, n, d)
        return out @ proj_w.T + proj_b

    def _L0_ffn_ref(x, ln_gamma, ln_beta, mu, scale, w1, b1, w2, b2):
        import jax, jax.numpy as jnp
        import numpy as np
        LN_EPS = 1e-05
        NORM_EPS = 1e-12

        def _layernorm(x, gamma, beta):
            mu = x.mean(axis=-1, keepdims=True)
            var = ((x - mu) ** 2).mean(axis=-1, keepdims=True)
            return (x - mu) * jax.lax.rsqrt(var + LN_EPS) * gamma + beta

        def _l2norm(x, axis):
            n = jnp.sqrt((x ** 2).sum(axis=axis, keepdims=True))
            return x / jnp.maximum(n, NORM_EPS)
        B, N, D = x.shape
        _, E, S = mu.shape
        xn = _layernorm(x, ln_gamma, ln_beta)
        x_unit = _l2norm(xn, axis=-1)
        mu_unit = _l2norm(mu, axis=0)
        logits = jnp.einsum('bnd,des->bnes', x_unit * scale, mu_unit)
        dispatch = jax.nn.softmax(logits, axis=1)
        combine = jax.nn.softmax(logits.reshape(B, N, E * S), axis=-1).reshape(B, N, E, S)
        slot_in = jnp.einsum('bnd,bnes->besd', xn, dispatch)
        h = jax.nn.gelu(jnp.einsum('besd,edh->besh', slot_in, w1) + b1[None, :, None, :], approximate=False)
        slot_out = jnp.einsum('besh,ehd->besd', h, w2) + b2[None, :, None, :]
        out = jnp.einsum('besd,bnes->bnd', slot_out, combine)
        return out

    def _L1_attn_ref(x, Wq, Wk, Wv, Wo):
        import jax, jax.numpy as jnp
        import numpy as np
        D_MODEL = 256
        N_HEADS = 16
        HEAD_DIM = D_MODEL // N_HEADS
        ROPE_BASE = 10000.0

        def _rope_tables(T, dtype=jnp.float32):
            half = HEAD_DIM // 2
            inv_freq = 1.0 / ROPE_BASE ** (jnp.arange(0, HEAD_DIM, 2, dtype=jnp.float32) / HEAD_DIM)
            t = jnp.arange(T, dtype=jnp.float32)
            freqs = jnp.einsum('i,j->ij', t, inv_freq)
            return (jnp.cos(freqs).astype(dtype), jnp.sin(freqs).astype(dtype))

        def _apply_rotary(x, cos, sin):
            B, T, H, D = x.shape
            xr = x.reshape(B, T, H, D // 2, 2)
            x0, x1 = (xr[..., 0], xr[..., 1])
            c = cos[None, :, None, :]
            s = sin[None, :, None, :]
            out = jnp.stack([x0 * c - x1 * s, x0 * s + x1 * c], axis=-1)
            return out.reshape(B, T, H, D)
        B, T, C = x.shape
        H, Dh = (N_HEADS, HEAD_DIM)
        scale = Dh ** (-0.5)
        q = (x @ Wq.T).reshape(B, T, H, Dh)
        k = (x @ Wk.T).reshape(B, T, H, Dh)
        v = (x @ Wv.T).reshape(B, T, H, Dh)
        cos, sin = _rope_tables(T, x.dtype)
        q = _apply_rotary(q, cos, sin)
        k = _apply_rotary(k, cos, sin)
        q = q.transpose(0, 2, 1, 3).astype(jnp.float32)
        k = k.transpose(0, 2, 1, 3).astype(jnp.float32)
        v = v.transpose(0, 2, 1, 3)
        scores = jnp.einsum('bhqd,bhkd->bhqk', q, k) * scale
        causal = jnp.triu(jnp.ones((T, T), dtype=bool), k=1)
        scores = jnp.where(causal[None, None], -jnp.inf, scores)
        attn = jax.nn.softmax(scores, axis=-1).astype(v.dtype)
        out = jnp.einsum('bhqk,bhkd->bhqd', attn, v)
        out = out.transpose(0, 2, 1, 3).reshape(B, T, C)
        return out @ Wo.T

    def _L1_ffn_ref(x, router_w, expert_weights):
        import jax, jax.numpy as jnp
        import numpy as np
        TOP_K = 2
        B, S, H = x.shape
        E = router_w.shape[0]
        T = B * S
        logits = jnp.einsum('bsh,eh->bse', x, router_w)
        rw = jax.nn.softmax(logits, axis=-1).reshape(T, E)
        x_flat = x.reshape(T, H)
        vals, idx = jax.lax.top_k(rw, TOP_K)
        w_masked = jnp.zeros_like(rw).at[jnp.arange(T)[:, None], idx].set(vals)

        def body(acc, we):
            w_e, W_e = we
            return (acc + x_flat * w_e[:, None] @ W_e, None)
        out_flat, _ = jax.lax.scan(body, jnp.zeros((T, H), dtype=x.dtype), (w_masked.T, expert_weights))
        return out_flat.reshape(B, S, H)
    x = L0_attn_x
    x = x + _L0_attn_ref(_layernorm(x, axis=-1), L0_attn_qkv_w, L0_attn_qkv_b, L0_attn_proj_w, L0_attn_proj_b, L0_attn_projection_matrix)
    x = x + _L0_ffn_ref(_layernorm(x, axis=-1), L0_ffn_ln_gamma, L0_ffn_ln_beta, L0_ffn_mu, L0_ffn_scale, L0_ffn_w1, L0_ffn_b1, L0_ffn_w2, L0_ffn_b2)
    x = x + _L1_attn_ref(_layernorm(x, axis=-1), L1_attn_Wq, L1_attn_Wk, L1_attn_Wv, L1_attn_Wo)
    x = x + _L1_ffn_ref(_layernorm(x, axis=-1), L1_ffn_router_w, L1_ffn_expert_weights)
    return x

_drawn_inputs = setup_inputs


def setup_inputs(seed=0):
    import zlib

    import numpy as np

    out = dict(_drawn_inputs(seed))
    spreads = {'L0_attn_qkv_b': (0.0, 0.1),
     'L0_attn_proj_b': (0.0, 0.1),
     'L0_ffn_ln_gamma': (1.0, 0.6),
     'L0_ffn_ln_beta': (0.0, 0.281),
     'L0_ffn_b1': (0.0, 0.298),
     'L0_ffn_b2': (0.0, 0.1)}
    factors = {'L0_attn_projection_matrix': 5.805,
     'L0_ffn_mu': 8.0,
     'L1_attn_Wq': 3.165,
     'L1_attn_Wk': 2.969}
    for name, (base, spread) in spreads.items():
        noise = np.random.default_rng([zlib.crc32(name.encode()), seed]).standard_normal(out[name].shape)
        drawn = base * np.exp(spread * noise) if base else spread * noise
        out[name] = jnp.asarray(drawn.astype(out[name].dtype))
    for name, factor in factors.items():
        out[name] = (out[name] * factor).astype(out[name].dtype)
    return out
```

```python
import concourse.bass as bass
from concourse import mybir
from contextlib import ExitStack
import numpy as np

fp32 = mybir.dt.float32
bf16 = mybir.dt.bfloat16
ALU = mybir.AluOpType
ACT = mybir.ActivationFunctionType
AX = mybir.AxisListType.X
ds = bass.ds

B, N, D = 4, 2048, 256
P = 128
TPB = N // P
NT = B * TPB
H, HD = 16, 16
M = 64
DC = D // P
VW = 32
G = H // 4
E0, S0, HID = 16, 16, 64
NS = E0 * S0
E1 = 32
LN_EPS = 1e-5
FEAT_EPS = 1e-6
MASKED = -1e30


class Memory:

    def __init__(self, nc, ctx, stage):
        self.nc, self.ctx, self.stage, self.sems = nc, ctx, stage, []

    def sb(self, name, shape, dt=fp32):
        return self.ctx.enter_context(self.nc.sbuf_tensor(f"{self.stage}_{name}", shape, dt))

    def ps(self, name, shape, dt=fp32):
        return self.ctx.enter_context(self.nc.psum_tensor(f"{self.stage}_{name}", shape, dt))

    def sem(self, name):
        self.sems.append(self.ctx.enter_context(self.nc.semaphore(f"{self.stage}_{name}")))
        return self.sems[-1]

    def clear(self):
        with self.nc.Block() as block:
            @block.gpsimd
            def _(pool):
                for s in self.sems:
                    pool.sem_clear(s)


def in_pairs(eng, front, back):
    front(0, 0)
    front(1, 1)
    back(0, 0)
    with eng.Fori(1, TPB // 4) as q:
        front(q * 2, 0)
        back(q * 2 - 1, 1)
        front(q * 2 + 1, 1)
        back(q * 2, 0)
    back(TPB // 2 - 1, 1)


def finish_rstd(nc, mem, keep, st, extra_norm):
    mean, rstd = keep["mean"], keep["rstd"]
    t1, t2, ve = mem.sb("ln_t1", [P, NT]), mem.sb("ln_t2", [P, NT]), mem.sb("ln_ve", [P, NT])
    var = mem.sb("ln_var", [P, NT])
    ve_ready, root_ready = mem.sem("ve_ready"), mem.sem("root_ready")
    rounds = 2 if extra_norm else 1
    with nc.Block() as block:
        @block.vector
        def _(dve):
            v = nc.vector
            v.tensor_tensor(mean[:, :], st[:, :, 1], st[:, :, 4], ALU.add)
            v.tensor_tensor(t1[:, :], st[:, :, 1], st[:, :, 4], ALU.subtract)
            v.tensor_tensor(var[:, :], st[:, :, 2], st[:, :, 5], ALU.add)
            dve.drain()
            v.tensor_scalar(mean[:, :], mean[:, :], 0.5, None, ALU.mult)
            v.tensor_tensor(t1[:, :], t1[:, :], t1[:, :], ALU.mult)
            v.tensor_scalar(var[:, :], var[:, :], 1.0 / D, None, ALU.mult)
            dve.drain()
            v.tensor_scalar(t1[:, :], t1[:, :], 0.25, None, ALU.mult)
            dve.drain()
            v.tensor_tensor(var[:, :], var[:, :], t1[:, :], ALU.add)
            dve.drain()
            for r in range(rounds):
                v.tensor_scalar(ve[:, :], var[:, :], LN_EPS, None, ALU.add).then_inc(ve_ready, 1)
                dve.wait_ge(root_ready, r + 1)
                v.reciprocal(t1[:, :], t2[:, :])
                dve.drain()
                v.tensor_tensor(t2[:, :], t1[:, :], t1[:, :], ALU.mult)
                dve.drain()
                v.tensor_tensor(t2[:, :], t2[:, :], ve[:, :], ALU.mult)
                dve.drain()
                v.tensor_scalar(t2[:, :], t2[:, :], -0.5, 1.5, ALU.mult, ALU.add)
                dve.drain()
                if r == 0:
                    v.tensor_tensor(rstd[:, :], t1[:, :], t2[:, :], ALU.mult)
                    dve.drain()
                    if extra_norm:
                        v.tensor_tensor(t1[:, :], rstd[:, :], rstd[:, :], ALU.mult)
                        dve.drain()
                        v.tensor_tensor(var[:, :], var[:, :], t1[:, :], ALU.mult)
                        dve.drain()
                else:
                    v.tensor_tensor(t1[:, :], t1[:, :], t2[:, :], ALU.mult)
                    dve.drain()
                    v.tensor_tensor(rstd[:, :], rstd[:, :], t1[:, :], ALU.mult)

        @block.scalar
        def _(act):
            for r in range(rounds):
                act.wait_ge(ve_ready, r + 1)
                nc.scalar.activation(t2[:, :], ve[:, :], ACT.Sqrt).then_inc(root_ready, 1)


def load_and_constants(nc, mem, io, keep, st):
    X = keep["X"]
    ident, identb = keep["ident"], keep["identb"]
    x_loaded = [mem.sem(f"x_loaded{b}") for b in range(B)]
    made = mem.sem("made")
    xv = io["x"].rearrange("b (t p) d -> b p t d", p=P)
    with nc.Block() as block:
        @block.sync
        def _(sp):
            for b in range(B):
                sp.dma_start(X[:, b * TPB:(b + 1) * TPB, :], xv[b]).then_inc(x_loaded[b], 16)

        @block.gpsimd
        def _(pool):
            nc.gpsimd.memset(ident[:, :], 0.0).then_inc(made, 1)
            pool.wait_ge(made, 1)
            nc.gpsimd.affine_select(out=ident[:, :], in_=ident[:, :], compare_op=ALU.not_equal, fill=1.0,
                                    base=0, pattern=[[-1, P]], channel_multiplier=1).then_inc(made, 1)
            pool.wait_ge(made, 2)
            nc.gpsimd.tensor_copy(identb[:, :], ident[:, :])

        @block.vector
        def _(dve):
            for b in range(B):
                dve.wait_ge(x_loaded[b], 16)
                with dve.Fori(0, TPB) as i:
                    nc.vector.bn_stats(st[:, ds(b * TPB + i, 1), :], X[:, ds(b * TPB + i, 1), :])


def tables():
    freq = 1.0 / 10000.0 ** (np.arange(0, HD, 2, dtype=np.float32) / HD)
    angle = np.arange(N, dtype=np.float32)[:, None] * freq.astype(np.float32)[None, :]
    return {"cos": np.cos(angle).astype(np.float32), "sin": np.sin(angle).astype(np.float32)}


def linear_attention(nc, mem, io, keep, st):
    X, mean, rstd, ident = keep["X"], keep["mean"], keep["rstd"], keep["ident"]
    W = mem.sb("qkv_w", [P, DC, 3 * D])
    PW = mem.sb("proj_w", [P, DC, D])
    FM = mem.sb("feature_w", [P, 8 * M])
    qb, kb = mem.sb("qb", [P, DC]), mem.sb("kb", [P, DC])
    vb, pb = mem.sb("vb", [P, D]), mem.sb("pb", [P, D])
    zeros = mem.sb("zeros", [P, D])
    z = [mem.sb(f"z{u}", [P, D]) for u in range(2)]
    zT = [mem.sb(f"zT{u}", [P, DC, P]) for u in range(2)]
    qkT = [mem.sb(f"qkT{u}", [P, DC, P]) for u in range(2)]
    ft = [mem.sb(f"ft{u}", [P, H * M]) for u in range(4)]
    mx = [mem.sb(f"mx{u}", [P, H]) for u in range(2)]
    vx = [mem.sb(f"vx{u}", [P, H, VW]) for u in range(4)]
    kvs = mem.sb("kvs", [P, G * M])
    KV = mem.sb("KV", [P, 8, 2 * (HD + 1)])
    qpT = [mem.sb(f"qpT{u}", [P, 8, P]) for u in range(2)]
    den = [mem.sb(f"den{u}", [P, 8, 2]) for u in range(2)]
    o = [mem.sb(f"o{u}", [P, H, HD]) for u in range(2)]
    oT = [mem.sb(f"oT{u}", [P, DC, P]) for u in range(2)]
    xb = [mem.sb(f"xb{u}", [P, D]) for u in range(2)]
    w_sem = mem.sem("weights")
    fm_sem = mem.sem("fm_loaded")
    fm_zero, set_up = mem.sem("fm_zero"), mem.sem("set_up")

    with nc.Block() as block:
        @block.vector
        def _(dve):
            nc.vector.memset(FM[:, :], 0.0).then_inc(fm_zero, 1)
            nc.vector.memset(zeros[:, :], 0.0)
            nc.vector.memset(KV[:, :, :], 0.0)
            for u in range(4):
                nc.vector.memset(vx[u][:, :, :], 0.0)
            dve.drain()
            for u in range(4):
                nc.vector.memset(vx[u][:, :, HD:HD + 1], 1.0)

        @block.sync
        def _(sp):
            n = 0
            for dst, src in ((W[:, :, :], io["qkvT"].rearrange("(c p) n -> p c n", p=P)),
                             (PW[:, :, :], io["projT"].rearrange("(c p) n -> p c n", p=P)),
                             (qb[:, :], io["qkv_b"][0:D].rearrange("(c p) -> p c", p=P)),
                             (kb[:, :], io["qkv_b"][D:2 * D].rearrange("(c p) -> p c", p=P)),
                             (vb[:, :], io["qkv_b"][2 * D:3 * D].partition_broadcast(P)),
                             (pb[:, :], io["proj_b"].partition_broadcast(P))):
                with nc.allow_non_contiguous_dma(reason="a bias as columns, once"):
                    sp.dma_start(dst, src).then_inc(w_sem, 16)
                n += 16
                sp.wait_ge(w_sem, n)
            sp.wait_ge(fm_zero, 1)
            for hl in range(8):
                pos = (hl % 4) * 2 + hl // 4
                sp.dma_start(FM[hl * HD:(hl + 1) * HD, pos * M:(pos + 1) * M], io["pmT"]).then_inc(fm_sem, 16)
            sp.wait_ge(fm_sem, 8 * 16)

    with ExitStack() as sub:
        m = Memory(nc, sub, "la")
        kv_names = ("z_ready", "tr_done", "zT_ready", "kp_done", "kT_ready", "v_ready", "w_done",
                    "max_done", "sub_done", "exp_done", "kf_ready", "kv_done")
        K = {n: m.sem("k_" + n) for n in kv_names}
        q_names = ("z_ready", "tr_done", "zT_ready", "qp_done", "qT_ready", "w_done", "sub_done", "exp_done",
                   "trE_done", "ev0_ready", "ev1_ready", "out_done", "o_ready", "trO_done", "oT_ready",
                   "proj_done", "x_done")
        Q = {n: m.sem("q_" + n) for n in q_names}
        kv_saved, kv_turned, kv_built, seen = (m.sem(n) for n in ("kv_saved", "kv_turned", "kv_built", "seen"))
        pT = m.ps("pT", [P, DC, P])
        pKQ = m.ps("pKQ", [P, 2, D])
        pW = m.ps("pW", [P, H * M])
        pE = [m.ps(f"pE{i}", [P, 4, P]) for i in range(2)]
        pO = m.ps("pO", [P, 512])
        pX = m.ps("pX", [P, 2, D])
        pKV = pO[:, 0:G * M]
        pOut = pO[:, 0:8 * 34].rearrange("p (c n) -> p c n", c=8)

        block = sub.enter_context(nc.Block())

        @block.vector
        def _(dve):
            v = nc.vector
            for name in ("v_ready", "sub_done"):
                dve.sem_inc(K[name], 1)
            for name in ("sub_done", "ev1_ready", "o_ready", "x_done"):
                dve.sem_inc(Q[name], 1)

            def normalise(S, t, u):
                dve.wait_ge(S["tr_done"], t + 1)
                v.tensor_scalar(z[u][:, :], X[:, ds(t, 1), :], mean[:, ds(t, 1)], rstd[:, ds(t, 1)],
                                ALU.subtract, ALU.mult).then_inc(S["z_ready"], 1)

            def values(t, f):
                dve.wait_ge(K["kT_ready"], t + 2)
                dve.wait_ge(K["kv_done"], t + 1)
                v.tensor_tensor(vx[f][:, :, 0:HD], pKQ[:, 1, :].rearrange("p (h e) -> p h e", h=H),
                                vb[:, :].rearrange("p (h e) -> p h e", h=H), ALU.add).then_inc(K["v_ready"], 1)

            def centre(S, free, t, u, f):
                dve.wait_ge(S["w_done"], t + 1)
                w3 = pW[:, :].rearrange("p (h m) -> p h m", h=H)
                v.tensor_reduce(mx[u][:, :], w3, AX, ALU.max)
                dve.drain()
                dve.wait_ge(free, t + 1)
                v.tensor_tensor(ft[f][:, :].rearrange("p (h m) -> p h m", h=H), w3,
                                mx[u][:, :].unsqueeze(2).broadcast_to([P, H, M]), ALU.subtract).then_inc(S["sub_done"], 1)

            def k_front(b, i, k):
                for u in range(2):
                    values(b * TPB + i * 2 + u, 2 * k + u)
                for u in range(2):
                    centre(K, K["kv_done"], b * TPB + i * 2 + u, u, 2 * k + u)

            def q_evict(t, u):
                dve.wait_ge(Q["trE_done"], t + 5)
                dve.wait_ge(Q["out_done"], t + 1)
                v.tensor_scalar(qpT[u][:, 4:8, :], pE[1][:, :, :], 0.125, FEAT_EPS, ALU.mult, ALU.add).then_inc(Q["ev1_ready"], 1)

            def q_divide(t, u):
                dve.wait_ge(Q["out_done"], t + 3)
                v.tensor_scalar(den[u][:, :, :], pOut.rearrange("p c (g e) -> p c g e", g=2)[:, :, :, HD], FEAT_EPS, None, ALU.add)
                dve.drain()
                v.reciprocal(den[u][:, :, :], den[u][:, :, :])
                dve.drain()
                dve.wait_ge(Q["trO_done"], t + 1)
                for blk in range(2):
                    src = pOut[:, blk * 4:blk * 4 + 4, :].rearrange("p j (g e) -> p j g e", g=2)[:, :, :, 0:HD]
                    last = v.tensor_tensor(o[u][:, blk * 8:blk * 8 + 8, :].rearrange("p (g j) e -> p j g e", g=2), src,
                                           den[u][:, blk * 4:blk * 4 + 4, :].unsqueeze(3).broadcast_to([P, 4, 2, HD]), ALU.mult)
                last.then_inc(Q["o_ready"], 1)

            def q_add(t, u):
                v.tensor_tensor(xb[u][:, :], X[:, ds(t, 1), :], pb[:, :], ALU.add)
                dve.drain()
                dve.wait_ge(Q["proj_done"], t + 1)
                v.tensor_tensor(X[:, ds(t, 1), :], xb[u][:, :], pX[:, 1, :], ALU.add).then_inc(Q["x_done"], 1)
                dve.drain()
                v.bn_stats(st[:, ds(t, 1), :], X[:, ds(t, 1), :])

            with dve.Fori(0, B) as b:
                def z_pair(S, i):
                    for u in range(2):
                        normalise(S, b * TPB + i * 2 + u, u)
                in_pairs(dve, lambda i, k: z_pair(K, i), lambda i, k: k_front(b, i, k))
                dve.wait_ge(kv_turned, b + 1)
                for g in range(2):
                    last = v.tensor_copy(KV[g * M:(g + 1) * M, :, g * 17:g * 17 + 17],
                                         pE[0][g * M:(g + 1) * M, 0:2, :].rearrange("p k (j e) -> p (k j) e", j=4)[:, :, 0:17])
                last.then_inc(kv_built, 1)

                def q_front(i, k):
                    z_pair(Q, i)
                    for u in range(2):
                        centre(Q, Q["trE_done"], b * TPB + i * 2 + u, u, 2 * k + u)

                def q_back(i, k):
                    for u in range(2):
                        t = b * TPB + i * 2 + u
                        q_evict(t, u)
                        q_divide(t, u)
                        q_add(t, u)
                in_pairs(dve, q_front, q_back)

        @block.scalar
        def _(act):
            s = nc.scalar
            for name in ("zT_ready", "kT_ready"):
                act.sem_inc(K[name], 1)
            for name in ("zT_ready", "qT_ready", "ev0_ready"):
                act.sem_inc(Q[name], 1)
            act.sem_inc(kv_saved, 1)

            def turn(S, user, t, u):
                act.wait_ge(S["tr_done"], t + 3)
                act.wait_ge(S[user], t + 1)
                s.activation(zT[u][:, :, :], pT[:, :, :], ACT.Copy).then_inc(S["zT_ready"], 1)

            def biased(S, done, ready, bias, t, u):
                act.wait_ge(S[done], t + 3)
                for c in range(DC):
                    last = s.activation(qkT[u][:, c, :], pKQ[:, 0, c * P:(c + 1) * P], ACT.Identity, bias=bias[:, c:c + 1])
                last.then_inc(S[ready], 1)

            def exponent(S, t, f):
                act.wait_ge(S["sub_done"], t + 2)
                s.activation(ft[f][:, :], ft[f][:, :], ACT.Exp, scale=0.25).then_inc(S["exp_done"], 1)

            with act.Fori(0, B) as b:
                def k_front(i, k):
                    for u in range(2):
                        turn(K, "kp_done", b * TPB + i * 2 + u, u)
                    for u in range(2):
                        t = b * TPB + i * 2 + u
                        biased(K, "kp_done", "kT_ready", kb, t, u)

                def k_back(i, k):
                    for u in range(2):
                        exponent(K, b * TPB + i * 2 + u, 2 * k + u)
                in_pairs(act, k_front, k_back)
                act.wait_ge(K["kv_done"], b * TPB + TPB + 4)
                s.activation(kvs[:, :], pKV, ACT.Copy).then_inc(kv_saved, 1)

                def q_front(i, k):
                    for u in range(2):
                        turn(Q, "qp_done", b * TPB + i * 2 + u, u)
                    for u in range(2):
                        biased(Q, "qp_done", "qT_ready", qb, b * TPB + i * 2 + u, u)

                def q_back(i, k):
                    for u in range(2):
                        exponent(Q, b * TPB + i * 2 + u, 2 * k + u)
                    for u in range(2):
                        t = b * TPB + i * 2 + u
                        act.wait_ge(Q["trE_done"], t + 5)
                        act.wait_ge(Q["out_done"], t + 1)
                        s.activation(qpT[u][:, 0:4, :], pE[0][:, :, :], ACT.Copy, scale=0.125, bias=FEAT_EPS).then_inc(Q["ev0_ready"], 1)
                        act.wait_ge(Q["trO_done"], t + 3)
                        s.activation(oT[u][:, :, :], pX[:, 0, :].rearrange("p (c q) -> p c q", c=DC), ACT.Copy).then_inc(Q["oT_ready"], 1)
                in_pairs(act, q_front, q_back)

        @block.gpsimd
        def _(pool):
            with pool.Fori(0, NT // 4) as i:
                for u in range(4):
                    pool.wait_ge(K["exp_done"], i * 4 + u + 1)
                    pool.sem_inc(seen, 1)
                    nc.gpsimd.tensor_scalar(ft[u][:, :], ft[u][:, :], 0.125, FEAT_EPS, ALU.mult, ALU.add).then_inc(K["kf_ready"], 1)

        @block.tensor
        def _(pe):
            mm = nc.tensor.matmul
            for S in (K, Q):
                pe.sem_inc(S["tr_done"], 2)
            pe.sem_inc(K["kp_done"], 2)
            pe.sem_inc(K["kv_done"], 4)
            pe.sem_inc(Q["qp_done"], 2)
            pe.sem_inc(Q["out_done"], 2)
            pe.sem_inc(Q["trE_done"], 4)
            pe.sem_inc(Q["trO_done"], 2)

            def turn(S, t, u):
                pe.wait_ge(S["z_ready"], t + 1)
                pe.wait_ge(S["zT_ready"], t + 1)
                for c in range(DC):
                    last = nc.tensor.transpose(pT[:, c, :], z[u][:, c * P:(c + 1) * P], ident[:, :])
                last.then_inc(S["tr_done"], 1)

            def project(S, done, ready, col, t, u):
                pe.wait_ge(S["zT_ready"], t + 2)
                pe.wait_ge(S[ready], t + 1)
                for j in range(DC):
                    for c in range(DC):
                        last = mm(pKQ[:, 0, j * P:(j + 1) * P], W[:, c, col + j * P:col + (j + 1) * P], zT[u][:, c, :],
                                  start=(c == 0), stop=(c == DC - 1))
                if S is K:
                    for c in range(DC):
                        last = mm(pKQ[:, 1, :], zT[u][:, c, :], W[:, c, 2 * D:3 * D], start=(c == 0), stop=(c == DC - 1))
                last.then_inc(S[done], 1)

            def exponents(S, ready, t, u):
                pe.wait_ge(S[ready], t + 2)
                pe.wait_ge(S["sub_done"], t + 1)
                for c in range(DC):
                    last = mm(pW[:, c * 512:(c + 1) * 512], qkT[u][:, c, :], FM[:, :], start=True, stop=True)
                last.then_inc(S["w_done"], 1)

            with pe.Fori(0, B) as b:
                tile = lambda i, u: b * TPB + i * 2 + u
                pe.wait_ge(kv_saved, b + 1)
                pe.wait_ge(Q["o_ready"], b * TPB + 1)
                mm(pKV, zeros[:, 0:P], zeros[:, :], start=True, stop=True)

                def k_front(i, k):
                    for u in range(2):
                        turn(K, tile(i, u), u)
                        pe.wait_ge(K["v_ready"], tile(i, u) + 1)
                        project(K, "kp_done", "kT_ready", D, tile(i, u), u)
                    for u in range(2):
                        exponents(K, "kT_ready", tile(i, u), u)

                def k_back(i, k):
                    for u in range(2):
                        pe.wait_ge(K["kf_ready"], tile(i, u) + 1)
                        pe.wait_ge(K["v_ready"], tile(i, u) + 2)
                        for blk in range(2):
                            for g in range(2):
                                for j in range(4):
                                    pos = (blk * 4 + j) * 2 + g
                                    last = mm(pKV[32 * j:32 * j + 32, (2 * blk + g) * M:(2 * blk + g + 1) * M],
                                              vx[2 * k + u][:, 8 * blk + 4 * g + j, :], ft[2 * k + u][:, pos * M:(pos + 1) * M],
                                              start=False, stop=True, skip_group_check=True)
                        last.then_inc(K["kv_done"], 1)
                in_pairs(pe, k_front, k_back)
                pe.wait_ge(kv_saved, b + 2)
                pe.wait_ge(Q["ev0_ready"], b * TPB + 1)
                for h in range(2):
                    last = nc.tensor.transpose(pE[0][:, h, :], kvs[:, h * P:(h + 1) * P], ident[:, :])
                last.then_inc(kv_turned, 1)

                def q_front(i, k):
                    for u in range(2):
                        turn(Q, tile(i, u), u)
                        project(Q, "qp_done", "qT_ready", 0, tile(i, u), u)
                    for u in range(2):
                        exponents(Q, "qT_ready", tile(i, u), u)

                def q_back(i, k):
                    for u in range(2):
                        t = tile(i, u)
                        pe.wait_ge(Q["exp_done"], t + 1)
                        pe.wait_ge(Q["ev0_ready"], t + 1)
                        pe.wait_ge(Q["ev1_ready"], t + 1)
                        pe.wait_ge(kv_built, b + 1)
                        for c in range(8):
                            last = nc.tensor.transpose(pE[c // 4][:, c % 4, :], ft[2 * k + u][:, c * P:(c + 1) * P], ident[:, :])
                        last.then_inc(Q["trE_done"], 1)
                        pe.wait_ge(Q["ev0_ready"], t + 2)
                        pe.wait_ge(Q["ev1_ready"], t + 2)
                        pe.wait_ge(Q["o_ready"], t + 1)
                        for c in range(8):
                            last = mm(pOut[:, c, :], qpT[u][:, c, :], KV[:, c, :], start=True, stop=True)
                        last.then_inc(Q["out_done"], 1)
                        pe.wait_ge(Q["o_ready"], t + 2)
                        pe.wait_ge(Q["x_done"], t + 1)
                        for c in range(DC):
                            last = nc.tensor.transpose(pX[:, 0, c * P:(c + 1) * P], o[u][:, 8 * c:8 * c + 8, :].rearrange("p h e -> p (h e)"), ident[:, :])
                        last.then_inc(Q["trO_done"], 1)
                        pe.wait_ge(Q["oT_ready"], t + 1)
                        for c in range(DC):
                            last = mm(pX[:, 1, :], oT[u][:, c, :], PW[:, c, :], start=(c == 0), stop=(c == DC - 1))
                        last.then_inc(Q["proj_done"], 1)
                in_pairs(pe, q_front, q_back)
    m.clear()


def soft_mixture(nc, mem, io, keep, st):
    X, mean, rstd, ident = keep["X"], keep["mean"], keep["rstd"], keep["ident"]
    QT = TPB // 4
    NP = E0 // 2
    gam, bet = mem.sb("gamma", [P, D]), mem.sb("beta", [P, D])
    scol = mem.sb("scale", [P, 1])
    mu = mem.sb("mu", [P, DC, NS])
    ones = mem.sb("ones", [P, P])
    w1 = mem.sb("w1", [P, DC, E0, HID])
    w2 = mem.sb("w2", [P, NP, D])
    b1 = mem.sb("b1", [P, NP])
    b2 = mem.sb("b2", [E0, D])
    pick = mem.sb("pick", [E0, NS])
    XN = mem.sb("XN", [P, NT, D + 2])
    ss, rn = mem.sb("ss", [P, NT]), mem.sb("rn", [P, NT])
    L = mem.sb("L", [P, TPB, NS])
    cm, mrow = mem.sb("cm", [P, NS]), mem.sb("mrow", [P, NS])
    ccol, dg = mem.sb("ccol", [P, 2]), mem.sb("dg", [P, 2, P])
    nrm = mem.sb("nrm", [P, TPB])
    rs, rr = mem.sb("rs", [P, NT]), mem.sb("rr", [P, NT])
    xnT = [mem.sb(f"xnT{f}", [P, DC, P]) for f in range(4)]
    Ed = [mem.sb(f"Ed{u}", [P, 4, NS]) for u in range(2)]
    si, siT = mem.sb("si", [P, 2, D]), mem.sb("siT", [P, DC, NS])
    rsi = mem.sb("rsi", [P, 2])
    sq, ty, tz = siT, cm, mrow
    Hp = mem.sb("Hp", [P, NP, P])
    SO = mem.sb("SO", [P, 2, D])
    C = [mem.sb(f"C{f}", [P, NS]) for f in range(4)]
    loads = mem.sem("loads")

    made, ss_ready, root_ready, sumd = (mem.sem(n) for n in ("made", "ss_ready", "root_ready", "sumd"))
    with ExitStack() as sub:
        m = Memory(nc, sub, "sm0")
        pSS = m.ps("pSS", [P, NS])
        block = sub.enter_context(nc.Block())

        @block.sync
        def _(sp):
            n = 0
            for dst, src in ((mu[:, :, :], io["mu"].rearrange("(c p) n -> p c n", p=P)),
                             (gam[:, :], io["gamma"].partition_broadcast(P)),
                             (bet[:, :], io["beta"].partition_broadcast(P)),
                             (scol[:, :], io["scale"].partition_broadcast(P)),
                             (w1[:, 0, :, :], io["w1"][:, 0:P, :].rearrange("e p h -> p e h")),
                             (w1[:, 1, :, :], io["w1"][:, P:D, :].rearrange("e p h -> p e h")),
                             (w2[0:HID, :, :], io["w2"].rearrange("(k a) h d -> a h k d", a=2)[0]),
                             (w2[HID:P, :, :], io["w2"].rearrange("(k a) h d -> a h k d", a=2)[1]),
                             (b1[0:HID, :], io["b1"].rearrange("(k a) h -> a h k", a=2)[0]),
                             (b1[HID:P, :], io["b1"].rearrange("(k a) h -> a h k", a=2)[1]),
                             (b2[:, :], io["b2"])):
                with nc.allow_non_contiguous_dma(reason="a bias as columns, once"):
                    sp.dma_start(dst, src).then_inc(loads, 16)
                n += 16
                sp.wait_ge(loads, n)

        @block.gpsimd
        def _(pool):
            nc.gpsimd.memset(pick[:, :], 1.0).then_inc(made, 1)
            pool.wait_ge(made, 1)
            nc.gpsimd.affine_select(out=pick[:, :], in_=pick[:, :], compare_op=ALU.is_ge, fill=0.0,
                                    base=0, pattern=[[1, NS]], channel_multiplier=-S0).then_inc(made, 1)
            pool.wait_ge(made, 2)
            nc.gpsimd.affine_select(out=pick[:, :], in_=pick[:, :], compare_op=ALU.is_ge, fill=0.0,
                                    base=S0 - 1, pattern=[[-1, NS]], channel_multiplier=S0)

        @block.vector
        def _(dve):
            v = nc.vector
            v.memset(ones[:, :], 1.0)
            v.memset(Hp[:, :, :], 0.0)
            v.memset(XN[:, :, D:D + 2], 1.0)
            dve.wait_ge(loads, 16)
            v.tensor_tensor(sq[:, :, :], mu[:, :, :], mu[:, :, :], ALU.mult).then_inc(ss_ready, 1)
            dve.wait_ge(sumd, 1)
            v.tensor_scalar(ty[:, :], pSS[:, :], 1e-24, None, ALU.max).then_inc(ss_ready, 1)
            dve.wait_ge(root_ready, 1)
            v.reciprocal(tz[:, :], sq[:, 0, :])
            dve.drain()
            v.tensor_tensor(sq[:, 0, :], tz[:, :], tz[:, :], ALU.mult)
            dve.drain()
            v.tensor_tensor(sq[:, 0, :], sq[:, 0, :], ty[:, :], ALU.mult)
            dve.drain()
            v.tensor_scalar(sq[:, 0, :], sq[:, 0, :], -0.5, 1.5, ALU.mult, ALU.add)
            dve.drain()
            v.tensor_tensor(tz[:, :], tz[:, :], sq[:, 0, :], ALU.mult)
            dve.drain()
            v.tensor_tensor(mu[:, :, :], mu[:, :, :], tz[:, :].unsqueeze(1).broadcast_to([P, DC, NS]), ALU.mult)

        @block.scalar
        def _(act):
            act.wait_ge(ss_ready, 2)
            nc.scalar.activation(sq[:, 0, :], ty[:, :], ACT.Sqrt).then_inc(root_ready, 1)

        @block.tensor
        def _(pe):
            pe.wait_ge(ss_ready, 1)
            for c in range(DC):
                last = nc.tensor.matmul(pSS[:, :], ones[:, :], sq[:, c, :], start=(c == 0), stop=(c == DC - 1))
            last.then_inc(sumd, 1)

    xn_ready, sqd, nroot, ssr = (mem.sem(n) for n in ("xn_ready", "sqd", "nroot", "ssr"))
    with ExitStack() as sub:
        block = sub.enter_context(nc.Block())

        @block.vector
        def _(dve):
            v = nc.vector
            with dve.Fori(0, NT // 4) as q:
                for j in range(4):
                    v.tensor_scalar(XN[:, ds(q * 4 + j, 1), 0:D], X[:, ds(q * 4 + j, 1), :], mean[:, ds(q * 4 + j, 1)],
                                    rstd[:, ds(q * 4 + j, 1)], ALU.subtract, ALU.mult)
                dve.drain()
                v.tensor_tensor(XN[:, ds(q * 4, 4), 0:D], XN[:, ds(q * 4, 4), 0:D],
                                gam[:, :].unsqueeze(1).broadcast_to([P, 4, D]), ALU.mult)
                dve.drain()
                v.tensor_tensor(XN[:, ds(q * 4, 4), 0:D], XN[:, ds(q * 4, 4), 0:D],
                                bet[:, :].unsqueeze(1).broadcast_to([P, 4, D]), ALU.add).then_inc(xn_ready, 1)
            dve.wait_ge(sqd, NT)
            v.tensor_scalar(ss[:, :], ss[:, :], 1e-24, None, ALU.max).then_inc(ssr, 1)
            dve.wait_ge(nroot, 1)
            v.reciprocal(rn[:, :], rs[:, :])
            dve.drain()
            v.tensor_tensor(rs[:, :], rn[:, :], rn[:, :], ALU.mult)
            dve.drain()
            v.tensor_tensor(rs[:, :], rs[:, :], ss[:, :], ALU.mult)
            dve.drain()
            v.tensor_scalar(rs[:, :], rs[:, :], -0.5, 1.5, ALU.mult, ALU.add)
            dve.drain()
            v.tensor_tensor(rn[:, :], rn[:, :], rs[:, :], ALU.mult)
            dve.drain()
            v.tensor_scalar(rn[:, :], rn[:, :], scol[:, 0:1], None, ALU.mult)

        @block.scalar
        def _(act):
            with act.Fori(0, NT // 4) as q:
                act.drain()
                act.wait_ge(xn_ready, q + 1)
                for j in range(4):
                    nc.scalar.activation(C[j][:, :], XN[:, ds(q * 4 + j, 1), 0:D], ACT.Square,
                                         accum_out=ss[:, ds(q * 4 + j, 1)]).then_inc(sqd, 1)
            act.wait_ge(ssr, 1)
            nc.scalar.activation(rs[:, :], ss[:, :], ACT.Sqrt).then_inc(nroot, 1)

    with ExitStack() as sub:
        m = Memory(nc, sub, "sm2")
        xs_ready, seen = m.sem("xs_ready"), m.sem("seen")
        XS = [m.sb(f"XS{f}", [P, D]) for f in range(4)]
        trB, xnT_ready, lgB, L_ready = (m.sem(n) for n in ("trB", "xnT_ready", "lgB", "L_ready"))
        cm_ready, cmT, dg_ready, mr_ready = (m.sem(n) for n in ("cm_ready", "cmT", "dg_ready", "mr_ready"))
        sub_done, ed_ready, ed_used = (m.sem(n) for n in ("sub_done", "ed_ready", "ed_used"))
        si_ready, siT_done, siT_ready, h_done, hp_ready, so_done, so_ready = (m.sem(n) for n in (
            "si_ready", "siT_done", "siT_ready", "h_done", "hp_ready", "so_done", "so_ready"))
        C_ready, trD, CT_ready, mmD, x_ready = (m.sem(n) for n in ("C_ready", "trD", "CT_ready", "mmD", "x_ready"))
        pT = [m.ps(f"pT{u}", [P, DC, P]) for u in range(2)]
        pL = [m.ps(f"pL{u}", [P, 2, NS]) for u in range(2)]
        pA = [m.ps(f"pA{h}", [P, 512]) for h in range(2)]
        pM = m.ps("pM", [P, 2, NS])
        pH = m.ps("pH", [P, NP, S0])
        block = sub.enter_context(nc.Block())

        @block.vector
        def _(dve):
            v = nc.vector
            dve.sem_inc(L_ready, 2)
            dve.sem_inc(x_ready, 2)
            with dve.Fori(0, B) as b:
                v.memset(cm[:, :], -3.0e38)

                def logits(i, k):
                    for u in range(2):
                        t = b * TPB + i * 2 + u
                        dve.wait_ge(lgB, t + 5)
                        v.tensor_scalar(L[:, ds(i * 2 + u, 1), :], pL[u][:, 0, :], rn[:, ds(t, 1)], None,
                                        ALU.mult).then_inc(L_ready, 1)
                        dve.drain()
                        v.tensor_tensor(cm[:, :], cm[:, :], L[:, ds(i * 2 + u, 1), :].rearrange("p a n -> p (a n)"), ALU.max)
                dve.drain()
                in_pairs(dve, lambda i, k: None, logits)
                dve.drain().then_inc(cm_ready, 1)
                v.tensor_reduce(nrm[:, :], L[:, :, :], AX, ALU.max, negate=True)
                dve.wait_ge(cmT, b + 1)
                v.tensor_reduce(ccol[:, :], pM[:, 0, :].rearrange("p (h q) -> p h q", h=2), AX, ALU.max)
                dve.drain()
                for h in range(2):
                    last = v.tensor_scalar(dg[:, h, :], ident[:, :], ccol[:, h:h + 1], None, ALU.mult)
                last.then_inc(dg_ready, 1)
                dve.wait_ge(mr_ready, b + 1)
                v.tensor_copy(mrow[:, :], pM[:, 1, :])
                dve.drain()
                for q in range(QT):
                    dve.wait_ge(ed_used, b * QT + q + 1)
                    v.tensor_tensor(Ed[q % 2][:, :, :], L[:, q * 4:q * 4 + 4, :],
                                    mrow[:, :].unsqueeze(1).broadcast_to([P, 4, NS]), ALU.subtract).then_inc(sub_done, 1)
                dve.wait_ge(ed_used, b * QT + QT + 2)
                for h in range(2):
                    v.reciprocal(rsi[:, h:h + 1], pA[h][:, D:D + 1])
                dve.drain()
                for h in range(2):
                    last = v.tensor_scalar(si[:, h, :], pA[h][:, 0:D], rsi[:, h:h + 1], None, ALU.mult)
                last.then_inc(si_ready, 1)
                dve.wait_ge(so_done, b + 1)
                for h in range(2):
                    last = v.tensor_copy(SO[:, h, :], pA[h][:, 0:D])
                last.then_inc(so_ready, 1)

                def add(i, k):
                    for u in range(2):
                        t = b * TPB + i * 2 + u
                        dve.wait_ge(mmD, t + 5)
                        v.reciprocal(rr[:, ds(t, 1)], rs[:, ds(t, 1)])
                        dve.drain()
                        v.scalar_tensor_tensor(X[:, ds(t, 1), :], pL[u][:, 0, :].unsqueeze(1), rr[:, ds(t, 1)],
                                               X[:, ds(t, 1), :], ALU.mult, ALU.add).then_inc(x_ready, 1)
                        dve.drain()
                        v.bn_stats(st[:, ds(t, 1), :], X[:, ds(t, 1), :])
                in_pairs(dve, lambda i, k: None, add)

        @block.scalar
        def _(act):
            s = nc.scalar
            act.sem_inc(xnT_ready, 2)
            act.sem_inc(CT_ready, 2)
            with act.Fori(0, B) as b:
                def turn_in(i, k):
                    for u in range(2):
                        t = b * TPB + i * 2 + u
                        act.wait_ge(trB, t + 5)
                        act.wait_ge(lgB, t + 1)
                        s.activation(xnT[2 * k + u][:, :, :], pT[u][:, :, :], ACT.Copy).then_inc(xnT_ready, 1)
                in_pairs(act, turn_in, lambda i, k: None)
                for q in range(QT):
                    act.wait_ge(sub_done, b * QT + q + 1)
                    s.activation(Ed[q % 2][:, :, :], Ed[q % 2][:, :, :], ACT.Exp).then_inc(ed_ready, 1)
                act.wait_ge(siT_done, b + 1)
                s.activation(siT[:, :, :], pL[0][:, :, :], ACT.Copy).then_inc(siT_ready, 1)
                act.wait_ge(h_done, b + 1)
                for e in range(E0):
                    k, a = e // 2, e % 2
                    col = (e % 8) * S0
                    last = s.activation(Hp[a * HID:(a + 1) * HID, k, col:col + S0], pH[a * HID:(a + 1) * HID, k, :],
                                        ACT.Gelu, bias=b1[a * HID:(a + 1) * HID, k:k + 1])
                last.then_inc(hp_ready, 1)

                def mix(i, k):
                    for u in range(2):
                        t = b * TPB + i * 2 + u
                        act.wait_ge(trD, t + 1)
                        s.activation(C[2 * k + u][:, :].unsqueeze(1), L[:, ds(i * 2 + u, 1), :], ACT.Exp,
                                     bias=nrm[:, ds(i * 2 + u, 1)], accum_out=rs[:, ds(t, 1)]).then_inc(C_ready, 1)

                def turn_out(i, k):
                    for u in range(2):
                        t = b * TPB + i * 2 + u
                        act.wait_ge(trD, t + 5)
                        act.wait_ge(mmD, t + 1)
                        s.activation(xnT[2 * k + u][:, :, :], pT[u][:, :, :], ACT.Copy).then_inc(CT_ready, 1)
                in_pairs(act, mix, turn_out)

        @block.gpsimd
        def _(pool):
            with pool.Fori(0, NT // 4) as q:
                for f in range(4):
                    pool.wait_ge(trB, q * 4 + f + 1)
                    pool.sem_inc(seen, 1)
                    nc.gpsimd.tensor_copy(XS[f][:, :].unsqueeze(1), XN[:, ds(q * 4 + f, 1), 0:D]).then_inc(xs_ready, 1)

        @block.tensor
        def _(pe):
            mm = nc.tensor.matmul
            for sem_, n in ((trB, 4), (lgB, 4), (ed_used, 2), (trD, 4), (mmD, 4)):
                pe.sem_inc(sem_, n)
            with pe.Fori(0, B) as b:
                pe.wait_ge(x_ready, b * TPB + 2)

                def turn(i, k):
                    for u in range(2):
                        t = b * TPB + i * 2 + u
                        pe.wait_ge(xs_ready, t + 1)
                        pe.wait_ge(xnT_ready, t + 1)
                        for c in range(DC):
                            last = nc.tensor.transpose(pT[u][:, c, :], XS[2 * k + u][:, c * P:(c + 1) * P], ident[:, :])
                        last.then_inc(trB, 1)

                def logits(i, k):
                    for u in range(2):
                        t = b * TPB + i * 2 + u
                        pe.wait_ge(xnT_ready, t + 3)
                        pe.wait_ge(L_ready, t + 1)
                        for c in range(DC):
                            last = mm(pL[u][:, 0, :], xnT[2 * k + u][:, c, :], mu[:, c, :], start=(c == 0), stop=(c == DC - 1))
                        last.then_inc(lgB, 1)
                in_pairs(pe, turn, logits)

                pe.wait_ge(cm_ready, b + 1)
                for h in range(2):
                    last = nc.tensor.transpose(pM[:, 0, h * P:(h + 1) * P], cm[:, h * P:(h + 1) * P], ident[:, :])
                last.then_inc(cmT, 1)
                pe.wait_ge(dg_ready, b + 1)
                for h in range(2):
                    last = mm(pM[:, 1, h * P:(h + 1) * P], ones[:, :], dg[:, h, :], start=True, stop=True)
                last.then_inc(mr_ready, 1)
                for q in range(QT):
                    pe.wait_ge(ed_ready, b * QT + q + 1)
                    for j in range(4):
                        for h in range(2):
                            first, end = q + j == 0, q * 4 + j == TPB - 1
                            last = mm(pA[h][:, 0:D + 1].unsqueeze(1), Ed[q % 2][:, j, h * P:(h + 1) * P],
                                      XN[:, ds(b * TPB + q * 4 + j, 1), 0:D + 1], start=first, stop=end)
                    last.then_inc(ed_used, 1)
                pe.wait_ge(si_ready, b + 1)
                for h in range(2):
                    for c in range(DC):
                        last = nc.tensor.transpose(pL[0][:, c, h * P:(h + 1) * P], si[:, h, c * P:(c + 1) * P], ident[:, :])
                last.then_inc(siT_done, 1)
                pe.wait_ge(siT_ready, b + 1)
                for e in range(E0):
                    k, a = e // 2, e % 2
                    for c in range(DC):
                        last = mm(pH[a * HID:(a + 1) * HID, k, :], w1[:, c, e, :], siT[:, c, e * S0:(e + 1) * S0],
                                  start=(c == 0), stop=(c == DC - 1))
                last.then_inc(h_done, 1)
                pe.wait_ge(hp_ready, b + 1)
                for h in range(2):
                    for k in range(4):
                        mm(pA[h][:, 0:D], Hp[:, h * 4 + k, :], w2[:, h * 4 + k, :], start=(k == 0), stop=False)
                    last = mm(pA[h][:, 0:D], pick[:, h * P:(h + 1) * P], b2[:, :], start=False, stop=True)
                last.then_inc(so_done, 1)

                def turn_mix(i, k):
                    for u in range(2):
                        t = b * TPB + i * 2 + u
                        pe.wait_ge(C_ready, t + 1)
                        pe.wait_ge(CT_ready, t + 1)
                        for c in range(2):
                            last = nc.tensor.transpose(pT[u][:, c, :], C[2 * k + u][:, c * P:(c + 1) * P], ident[:, :])
                        last.then_inc(trD, 1)

                def mix(i, k):
                    for u in range(2):
                        t = b * TPB + i * 2 + u
                        pe.wait_ge(CT_ready, t + 3)
                        pe.wait_ge(so_ready, b + 1)
                        pe.wait_ge(x_ready, t + 1)
                        for c in range(2):
                            last = mm(pL[u][:, 0, :], xnT[2 * k + u][:, c, :], SO[:, c, :], start=(c == 0), stop=(c == 1))
                        last.then_inc(mmD, 1)
                in_pairs(pe, turn_mix, mix)
    m.clear()


def project_qkv(nc, mem, io, keep, nn):
    X, mean, rstd, ident = keep["X"], keep["mean"], keep["rstd"], keep["ident"]
    W = mem.sb("W", [P, DC, 3 * D])
    cos, sin = mem.sb("cos", [P, NT, HD // 2]), mem.sb("sin", [P, NT, HD // 2])
    z = [mem.sb(f"z{f}", [P, D]) for f in range(4)]
    zT = [mem.sb(f"zT{f}", [P, DC, P]) for f in range(4)]
    xc = [mem.sb(f"xc{u}", [P, 2 * D]) for u in range(2)]
    xs = [mem.sb(f"xs{u}", [P, 2 * D]) for u in range(2)]
    rqk = [mem.sb(f"rqk{f}", [P, G, 2, 4 * HD]) for f in range(4)]
    rv = [mem.sb(f"rv{f}", [P, G, 4, VW]) for f in range(4)]
    sq = [mem.sb(f"sq{f}", [P, 3, D]) for f in range(4)]
    z_ready, turned, zT_ready, qk_done, v_done, rot_ready, v_ready, rec_ready, sq_ready, summed = (mem.sem(n) for n in (
        "z_ready", "turned", "zT_ready", "qk_done", "v_done", "rot_ready", "v_ready", "rec_ready", "sq_ready", "summed"))
    seen = mem.sem("seen")
    w_loaded = mem.sem("w_loaded")
    qk_stored = [mem.sem(f"qk_stored{f}") for f in range(4)]
    v_stored = [mem.sem(f"v_stored{f}") for f in range(4)]
    pT = [mem.ps(f"pT{u}", [P, DC, P]) for u in range(2)]
    pQK = [mem.ps(f"pQK{u}", [P, 2 * D]) for u in range(2)]
    pV = [mem.ps(f"pV{u}", [P, D]) for u in range(2)]
    qk_d = keep["qk"].rearrange("(b g) t p e -> b g t p e", g=G)
    v_d = keep["v"].rearrange("(b g) t p e -> b g t p e", g=G)
    with nc.Block() as block:
        @block.sync
        def _(sp):
            n = 0
            for c in range(3):
                sp.dma_start(W[:, :, c * D:(c + 1) * D],
                             io[("WqT", "WkT", "WvT")[c]].rearrange("(c p) n -> p c n", p=P)).then_inc(w_loaded, 16)
                n += 16
                sp.wait_ge(w_loaded, n)
            for b in range(B):
                for dst, src in ((cos, io["cos"]), (sin, io["sin"])):
                    sp.dma_start(dst[:, b * TPB:(b + 1) * TPB, :], src.rearrange("(t p) j -> p t j", p=P)).then_inc(w_loaded, 16)
                    n += 16
                    sp.wait_ge(w_loaded, n)
            for f in range(4):
                sp.sem_inc(qk_stored[f], 16)
                sp.sem_inc(v_stored[f], 16)
            with sp.Fori(0, B) as b:
                with sp.Fori(0, TPB // 4) as q:
                    for f in range(4):
                        t = b * TPB + q * 4 + f
                        for ready, buf, dram, done in ((rec_ready, rqk[f], qk_d, qk_stored[f]), (v_ready, rv[f], v_d, v_stored[f])):
                            sp.wait_ge(ready, t + 3)
                            sp.dma_start(dram[ds(b, 1), :, ds(q * 4 + f, 1), :, :].rearrange("b g t p e -> p (b g t) e"),
                                         buf[:, :, :, :].rearrange("p g a e -> p g (a e)")).then_inc(done, 16)
            for f in range(4):
                sp.wait_ge(qk_stored[f], 16 + 16 * (NT // 4))
                sp.wait_ge(v_stored[f], 16 + 16 * (NT // 4))

        @block.vector
        def _(dve):
            v = nc.vector
            for f in range(4):
                v.memset(rv[f][:, :, :, :], 0.0)
            dve.drain()
            for f in range(4):
                v.memset(rv[f][:, :, :, HD:HD + 1], 1.0)
            dve.drain().then_inc(z_ready, 1)
            dve.sem_inc(rot_ready, 2)
            dve.wait_ge(w_loaded, 16 * 11)

            def normalise(t, f):
                dve.wait_ge(turned, t + 1)
                v.tensor_scalar(z[f][:, :].unsqueeze(1), X[:, ds(t, 1), :], mean[:, ds(t, 1)], rstd[:, ds(t, 1)],
                                ALU.subtract, ALU.mult).then_inc(z_ready, 1)

            def rotate(t, f):
                u = f % 2
                src = pQK[u][:, :].rearrange("p (h i a) -> p h i a", h=2 * H, a=2)
                dve.wait_ge(qk_done, t + 1)
                for table, dst in ((cos, xc), (sin, xs)):
                    tab = table[:, ds(t, 1), :].unsqueeze(3).broadcast_to([P, 2 * H, HD // 2, 2])
                    last = v.tensor_tensor(dst[u][:, :].rearrange("p (h i a) -> p h i a", h=2 * H, a=2), src, tab, ALU.mult)
                last.then_inc(rot_ready, 1)
            dve.sem_inc(summed, 4)

            def sums(t, f):
                dve.wait_ge(sq_ready, t + 1)
                v.tensor_reduce(nn[:, ds(t, 1), :], sq[f][:, :, :].rearrange("p a (h e) -> p (a h) e", h=H), AX, ALU.add)\
                 .then_inc(summed, 1)

            def quad(q, sums_too):
                for f in range(4):
                    normalise(q * 4 + f, f)
                    if sums_too:
                        sums(q * 4 + f - 4, f)
                for f in range(4):
                    dve.wait_ge(rec_ready, q * 4 + f + 1)
                    rotate(q * 4 + f, f)
            quad(0, False)
            with dve.Fori(1, NT // 4) as q:
                quad(q, True)
            for f in range(4):
                sums(NT - 4 + f, f)

        @block.gpsimd
        def _(pool):
            pool.sem_inc(rec_ready, 2)
            with pool.Fori(0, NT // 4) as q:
                for f in range(4):
                    u = f % 2
                    pool.wait_ge(rot_ready, q * 4 + f + 3)
                    pool.wait_ge(qk_stored[f], q * 16 + 16)
                    pool.sem_inc(seen, 1)
                    c4 = xc[u][:, :].rearrange("p (q g r a) -> p q g r a", q=2, g=G, a=2)
                    s4 = xs[u][:, :].rearrange("p (q g r a) -> p q g r a", q=2, g=G, a=2)
                    for qk in range(2):
                        out = rqk[f][:, :, qk, :].rearrange("p g (r a) -> p g r a", a=2)
                        nc.gpsimd.tensor_tensor(out[:, :, :, 0], c4[:, qk, :, :, 0], s4[:, qk, :, :, 1], ALU.subtract)
                        last = nc.gpsimd.tensor_tensor(out[:, :, :, 1], s4[:, qk, :, :, 0], c4[:, qk, :, :, 1], ALU.add)
                    last.then_inc(rec_ready, 1)
                    pool.wait_ge(summed, q * 4 + f + 1)
                    pool.wait_ge(rec_ready, q * 4 + f + 3)
                    pool.sem_inc(seen, 1)
                    for n, (x, y) in enumerate(((0, 0), (1, 1), (0, 1))):
                        last = nc.gpsimd.tensor_tensor(sq[f][:, n, :].rearrange("p (g e) -> p g e", g=G), rqk[f][:, :, x, :],
                                                       rqk[f][:, :, y, :], ALU.mult)
                    last.then_inc(sq_ready, 1)

        @block.scalar
        def _(act):
            act.sem_inc(zT_ready, 2)
            act.sem_inc(v_ready, 2)
            with act.Fori(0, NT // 4) as q:
                def turn(f):
                    act.wait_ge(turned, q * 4 + f + 5)
                    nc.scalar.activation(zT[f][:, :, :], pT[f % 2][:, :, :], ACT.Copy).then_inc(zT_ready, 1)

                def value(f):
                    act.wait_ge(v_done, q * 4 + f + 1)
                    act.wait_ge(v_stored[f], q * 16 + 16)
                    nc.scalar.activation(rv[f][:, :, :, 0:HD].rearrange("p g h e -> p (g h) e"),
                                         pV[f % 2][:, :].rearrange("p (h e) -> p h e", h=H), ACT.Copy).then_inc(v_ready, 1)
                for f in (0, 1, 2, 3):
                    turn(f)
                    if f:
                        value(f - 1)
                value(3)

        @block.tensor
        def _(pe):
            mm = nc.tensor.matmul
            pe.sem_inc(turned, 4)
            pe.wait_ge(w_loaded, 48)
            with pe.Fori(0, NT // 4) as q:
                def turn(f):
                    pe.wait_ge(z_ready, q * 4 + f + 2)
                    pe.wait_ge(zT_ready, q * 4 + f + 1)
                    for c in range(DC):
                        last = nc.tensor.transpose(pT[f % 2][:, c, :], z[f][:, c * P:(c + 1) * P], ident[:, :])
                    last.then_inc(turned, 1)

                def project(f):
                    pe.wait_ge(zT_ready, q * 4 + f + 3)
                    pe.wait_ge(rot_ready, q * 4 + f + 1)
                    for c in range(DC):
                        last = mm(pQK[f % 2][:, :], zT[f][:, c, :], W[:, c, 0:2 * D], start=(c == 0), stop=(c == DC - 1))
                    last.then_inc(qk_done, 1)
                    pe.wait_ge(v_ready, q * 4 + f + 1)
                    for c in range(DC):
                        last = mm(pV[f % 2][:, :], zT[f][:, c, :], W[:, c, 2 * D:3 * D], start=(c == 0), stop=(c == DC - 1))
                    last.then_inc(v_done, 1)
                for f in range(4):
                    turn(f)
                    if f:
                        project(f - 1)
                project(3)


ROOM = 55.0 / HD ** -0.5
LOOSE = 124.0 / HD ** -0.5


def bound_scores(nc, mem, io, keep, nn):
    ident, nmax, need_max = keep["ident"], keep["nmax"], keep["need_max"]
    BH = B * H
    km, kcol, dg = mem.sb("km", [P, BH]), mem.sb("kcol", [BH, 1]), mem.sb("dg", [BH, BH])
    ones = mem.sb("ones", [BH, P])
    bd = mem.sb("bd", [P, NT, H])
    gap, worst, over = mem.sb("gap", [P, 1]), mem.sb("worst", [1, 1]), mem.sb("over", [1, 1])
    km_ready, km_turned, dg_ready, spread, squared, rooted, gap_ready, gap_turned = (mem.sem(n) for n in (
        "km_ready", "km_turned", "dg_ready", "spread", "squared", "rooted", "gap_ready", "gap_turned"))
    pK, pM, pG = mem.ps("pK", [BH, P]), mem.ps("pM", [P, BH]), mem.ps("pG", [1, P])
    q2, k2, own = (nn[:, :, n * H:(n + 1) * H] for n in range(3))
    with nc.Block() as block:
        @block.vector
        def _(dve):
            v = nc.vector
            v.memset(ones[:, :], 1.0)
            for b in range(B):
                v.tensor_reduce(km[:, b * H:(b + 1) * H], k2[:, b * TPB:(b + 1) * TPB, :].rearrange("p t h -> p h t"), AX, ALU.max)
            dve.drain().then_inc(km_ready, 1)
            dve.wait_ge(km_turned, 1)
            v.tensor_reduce(kcol[:, :], pK[:, :], AX, ALU.max)
            dve.drain()
            v.tensor_scalar(dg[:, :], ident[0:BH, 0:BH], kcol[:, 0:1], None, ALU.mult).then_inc(dg_ready, 1)
            dve.wait_ge(spread, 1)
            for b in range(B):
                last = v.tensor_tensor(bd[:, b * TPB:(b + 1) * TPB, :], q2[:, b * TPB:(b + 1) * TPB, :],
                                       pM[:, b * H:(b + 1) * H].unsqueeze(1).broadcast_to([P, TPB, H]), ALU.mult)
            last.then_inc(squared, 1)
            dve.wait_ge(rooted, 1)
            for b in range(B):
                for g in range(G):
                    v.tensor_scalar(nmax[:, b * G + g, :].rearrange("p (t h) -> p t h", h=4),
                                    bd[:, b * TPB:(b + 1) * TPB, g * 4:g * 4 + 4], -1.0, ROOM, ALU.mult, ALU.add)
            dve.drain()
            v.tensor_tensor(bd[:, :, :], bd[:, :, :], own, ALU.subtract)
            dve.drain()
            v.tensor_reduce(gap[:, :], bd[:, :, :].rearrange("p t h -> p (t h)"), AX, ALU.max).then_inc(gap_ready, 1)
            dve.wait_ge(gap_turned, 1)
            v.tensor_reduce(worst[:, :], pG[:, :], AX, ALU.max)
            dve.drain()
            v.tensor_scalar(over[:, :], worst[:, :], LOOSE, None, ALU.is_lt)
            dve.drain()
            v.tensor_scalar(over[:, :], over[:, :], -1.0, 1.0, ALU.mult, ALU.add)
            dve.drain()
            v.tensor_copy(need_max[:, :], over[:, :])

        @block.scalar
        def _(act):
            act.wait_ge(squared, 1)
            nc.scalar.activation(bd[:, :, :], bd[:, :, :], ACT.Sqrt).then_inc(rooted, 1)

        @block.tensor
        def _(pe):
            pe.wait_ge(km_ready, 1)
            nc.tensor.transpose(pK[:, :], km[:, :], ident[:, :]).then_inc(km_turned, 1)
            pe.wait_ge(dg_ready, 1)
            nc.tensor.matmul(pM[:, :], ones[:, :], dg[:, :], start=True, stop=True).then_inc(spread, 1)
            pe.wait_ge(gap_ready, 1)
            nc.tensor.transpose(pG[:, :], gap[:, :], ident[:, :]).then_inc(gap_turned, 1)


TERMS_Q = (0, 0, 0, 1, 1, 2)
TERMS_K = (0, 1, 2, 0, 1, 0)
KR = 6 * HD
KS = KR + 3


class Turner:

    def __init__(self, nc, m, keep, rqk, QT, KT, shifted):
        self.nc, self.keep, self.rqk, self.dst, self.shifted = nc, keep, rqk, (QT, KT), shifted
        self.rep = [[m.sb(f"{x}r{w}", [P, 16, 100], bf16) for w in range(2)] for x in "qk"]
        self.hi, self.mid = m.sb("hi", [P, 4, P], bf16), m.sb("mid", [P, 4, P], bf16)
        self.r1 = m.sb("r1", [P, 4, P])
        self.sh, self.shr = m.sb("sh", [P, 3, 16], bf16), m.sb("shr", [P, 16])
        self.pG = m.ps("pG", [P, 8, P], bf16)
        self.split_done, self.turned, self.evicted = m.sem("split_done"), m.sem("group_turned"), m.sem("group_evicted")

    def begin_dve(self, dve):
        for w in range(2):
            self.nc.vector.memset(self.rep[0][w][:, :, KR:100], 0.0)
            self.nc.vector.memset(self.rep[1][w][:, :, KR:100], 1.0)
        dve.sem_inc(self.evicted, 1)

    def split(self, dve, n, qd):
        v, hi, mid, r1 = self.nc.vector, self.hi, self.mid, self.r1
        src = self.rqk[:, qd * 4:qd * 4 + 4, :]
        v.tensor_copy(hi[:, :, :], src)
        if self.shifted:
            cur = self.keep["nmax"][:, ds(n, 1), qd * 16:qd * 16 + 16]
            sh, shr = self.sh, self.shr
            v.tensor_copy(sh[:, 0:1, :], cur)
        dve.drain()
        v.tensor_tensor(r1[:, :, :], src, hi[:, :, :], ALU.subtract)
        if self.shifted:
            v.tensor_tensor(shr[:, :].unsqueeze(1), cur, sh[:, 0:1, :], ALU.subtract)
        dve.drain()
        v.tensor_copy(mid[:, :, :], r1[:, :, :])
        if self.shifted:
            v.tensor_copy(sh[:, 1, :], shr[:, :])
        dve.drain()
        v.tensor_tensor(r1[:, :, :], r1[:, :, :], mid[:, :, :], ALU.subtract)
        if self.shifted:
            v.tensor_tensor(sh[:, 2, :], shr[:, :], sh[:, 1, :], ALU.subtract)
        for x, terms in enumerate((TERMS_Q, TERMS_K)):
            rep = self.rep[x][qd % 2]
            for part, from_ in ((0, hi), (1, mid), (2, r1)):
                s = from_[:, :, x * 64:(x + 1) * 64].rearrange("p t (h e) -> p t h e", h=4)
                if part == 2:
                    dve.drain()
                for slot in [n for n, w in enumerate(terms) if w == part]:
                    d = rep[:, :, slot * HD:(slot + 1) * HD].rearrange("p (t h) e -> p t h e", t=4)
                    last = v.tensor_copy(d, s)
        if self.shifted:
            for n in range(3):
                last = v.tensor_copy(self.rep[0][qd % 2][:, :, KR + n:KR + n + 1], self.sh[:, n, :].unsqueeze(2))
        dve.drain().then_inc(self.split_done, 1)

    def turn(self, pe, n, qd, gi):
        x, half = gi % 2, gi // 2
        rows = 100 if self.shifted else KR
        pe.wait_ge(self.split_done, n * 4 + qd + 1)
        pe.wait_ge(self.evicted, n * 16 + qd * 4 + gi + 1)
        for h in range(4):
            for t in range(2):
                last = self.nc.tensor.transpose(self.pG[0:rows, h * 2 + t, :],
                                                self.rep[x][qd % 2][:, (half * 2 + t) * 4 + h, 0:rows],
                                                self.keep["identb"][:, :])
        last.then_inc(self.turned, 1)

    def evict(self, dve, n, qd, gi, par):
        x, half = gi % 2, gi // 2
        rows = 100 if self.shifted else KR
        col = (qd * 4 + half * 2) * P
        dve.wait_ge(self.turned, n * 16 + qd * 4 + gi + 1)
        self.nc.vector.tensor_copy(self.dst[x][par][0:rows, :, col:col + 2 * P],
                                   self.pG[0:rows, :, :].rearrange("p (h t) q -> p h (t q)", t=2)).then_inc(self.evicted, 1)


def row_maxima(nc, mem, io, keep):
    nmax, identb, need_max = keep["nmax"], keep["identb"], keep["need_max"]
    rqk = mem.sb("rqk", [P, TPB, P])
    QT, KT = [mem.sb("QT", [P, 4, N], bf16)], [mem.sb("KT", [P, 4, N], bf16)]
    mask = mem.sb("mask", [P, P], bf16)
    pm = mem.sb("pm", [P, TPB, 4, 2])
    T = Turner(nc, mem, keep, rqk, QT, KT, False)
    made, loaded, scored, reduced, mx_done = (mem.sem(n) for n in ("made", "loaded", "scored", "reduced", "mx_done"))
    pS = [mem.ps(f"pS{s}", [P, 1024]) for s in range(3)]
    units = [(t, h, k) for t in range(TPB) for h in range(4) for k in range(1 + t // 8)]
    U = len(units)
    assert U % 3 == 0
    with nc.Block() as block:
        @block.gpsimd
        def _(pool):
            nc.gpsimd.memset(mask[:, :], 0.0).then_inc(made, 1)
            pool.wait_ge(made, 1)
            nc.gpsimd.affine_select(out=mask[:, :], in_=mask[:, :], compare_op=ALU.is_ge, fill=MASKED,
                                    base=0, pattern=[[-1, P]], channel_multiplier=1).then_inc(made, 1)

        @block.sync
        def _(sp):
            need = sp.value_load(need_max[0:1, 0:1], min_val=0, max_val=1)
            with sp.If(need > 0):
                with sp.Fori(0, B) as b:
                    for g in range(G):
                        n = b * G + g
                        sp.wait_ge(mx_done, n + 1)
                        for half in (slice(0, TPB // 2), slice(TPB // 2, TPB)):
                            sp.dma_start(rqk[:, half, :], keep["qk"][ds(n, 1), half, :, :].rearrange("i t p e -> p (i t) e")).then_inc(loaded, 16)

        @block.vector
        def _(dve):
            need = dve.value_load(need_max[0:1, 0:1], min_val=0, max_val=1)
            with dve.If(need > 0):
                v = nc.vector
                T.begin_dve(dve)
                dve.sem_inc(reduced, 3)
                dve.sem_inc(mx_done, 1)
                with dve.Fori(0, B) as b:
                    for g in range(G):
                        n = b * G + g
                        dve.wait_ge(loaded, n * 32 + 32)
                        for qd in range(4):
                            T.split(dve, n, qd)
                            for gi in range(4):
                                T.evict(dve, n, qd, gi, 0)
                        for i, (t, h, k) in enumerate(units):
                            width = min(1024, (t + 1) * P - k * 1024)
                            dve.wait_ge(scored, n * U + i + 1)
                            v.tensor_reduce(pm[:, t, h, k:k + 1], pS[i % 3][:, 0:width], AX, ALU.max).then_inc(reduced, 1)
                        dve.drain()
                        v.tensor_tensor(pm[:, 8:16, :, 0], pm[:, 8:16, :, 0], pm[:, 8:16, :, 1], ALU.max)
                        dve.drain()
                        v.tensor_scalar(nmax[:, ds(n, 1), :].rearrange("p i (t h) -> p (i t) h", h=4), pm[:, :, :, 0], -1.0, None, ALU.mult).then_inc(mx_done, 1)

        @block.tensor
        def _(pe):
            need = pe.value_load(need_max[0:1, 0:1], min_val=0, max_val=1)
            with pe.If(need > 0):
                pe.wait_ge(made, 2)
                with pe.Fori(0, B) as b:
                    for g in range(G):
                        n = b * G + g
                        for qd in range(4):
                            for gi in range(4):
                                T.turn(pe, n, qd, gi)
                        pe.wait_ge(T.evicted, n * 16 + 17)
                        for i, (t, h, k) in enumerate(units):
                            width = min(1024, (t + 1) * P - k * 1024)
                            pe.wait_ge(reduced, n * U + i + 1)
                            for c in range(0, width, 512):
                                w = min(512, width - c)
                                key = k * 1024 + c
                                diag = key + w == (t + 1) * P
                                last = nc.tensor.matmul(pS[i % 3][:, c:c + w], QT[0][0:KR, h, t * P:(t + 1) * P],
                                                        KT[0][0:KR, h, key:key + w], start=True, stop=not diag)
                                if diag:
                                    last = nc.tensor.matmul(pS[i % 3][:, c + w - P:c + w], identb[:, :], mask[:, :], start=False, stop=True)
                            last.then_inc(scored, 1)


def attention(nc, mem, io, keep):
    ident, identb = keep["ident"], keep["identb"]
    QC = N // 512
    STEPS = [(c, kb) for c in range(QC) for kb in range(4 * c + 4)]
    NST = len(STEPS)
    LAST = [STEPS.index((c, 4 * c + 3)) for c in range(QC)]
    rqk = mem.sb("rqk", [P, TPB, P])
    V = [mem.sb(f"V{k}", [P, TPB, P]) for k in range(2)]
    QT = [mem.sb(f"QT{k}", [P, 4, N], bf16) for k in range(2)]
    KT = [mem.sb(f"KT{k}", [P, 4, N], bf16) for k in range(2)]
    PT = [mem.sb(f"PT{s}", [P, 2, 512]) for s in range(4)]
    mask = mem.sb("mask", [P, P], bf16)
    zero = mem.sb("zero", [P, D])
    zeroed = mem.sem("zeroed")
    OT = [mem.sb(f"OT{s}", [P, 512]) for s in range(2)]
    rc = mem.sb("rc", [P, 4, 4])
    ob = [mem.sb(f"ob{s}", [P, 4, 4, HD]) for s in range(2)]
    T = Turner(nc, mem, keep, rqk, QT, KT, True)
    made, qk_loaded, scored, exp_done, pv_done, out_copied, out_turned, divided = (mem.sem(n) for n in (
        "made", "qk_loaded", "scored", "exp_done", "pv_done", "out_copied", "out_turned", "divided"))
    v_loaded = [mem.sem(f"v_loaded{k}") for k in range(2)]
    stored = [mem.sem(f"stored{s}") for s in range(2)]
    pS = [mem.ps(f"pS{s}", [P, 2, 512]) for s in range(2)]
    pO = [mem.ps(f"pO{s}", [P, 512]) for s in range(2)]
    pY = mem.ps("pY", [P, 4, P])
    NIT = B * G

    def iterations(eng, first, body):
        first()
        with eng.Fori(0, NIT // 2 - 1) as j:
            body(j * 2, 0, j, True)
            body(j * 2 + 1, 1, j, True)
        body(NIT - 2, 0, NIT // 2 - 1, True)
        body(NIT - 1, 1, NIT // 2 - 1, False)

    with nc.Block() as block:
        @block.gpsimd
        def _(pool):
            nc.gpsimd.memset(mask[:, :], 0.0).then_inc(made, 1)
            pool.wait_ge(made, 1)
            nc.gpsimd.affine_select(out=mask[:, :], in_=mask[:, :], compare_op=ALU.is_ge, fill=MASKED,
                                    base=0, pattern=[[1, P]], channel_multiplier=-1).then_inc(made, 1)
            nc.gpsimd.memset(zero[:, :], 0.0).then_inc(made, 1)
            pool.wait_ge(made, 3)
            rows = keep["xg"].rearrange("(q n p) d -> q p n d", n=20, p=P)
            for n in range(8):
                pool.dma_start(rows[n], zero[:, :].unsqueeze(1).broadcast_to([P, 20, D])).then_inc(zeroed, 16)
                pool.wait_ge(zeroed, n * 16 + 16)

        @block.sync
        def _(sp):
            for s in range(2):
                sp.sem_inc(stored[s], 16)

            def load(it, par):
                for dst, src, done in ((rqk, keep["qk"], qk_loaded), (V[par], keep["v"], v_loaded[par])):
                    for half in (slice(0, TPB // 2), slice(TPB // 2, TPB)):
                        sp.dma_start(dst[:, half, :], src[ds(it, 1), half, :, :].rearrange("i t p e -> p (i t) e")).then_inc(done, 16)

            def body(it, par, j, more):
                if more:
                    sp.wait_ge(T.split_done, it * 4 + 4)
                    sp.wait_ge(pv_done, it * NST + 2)
                    load(it + 1, 1 - par)
                for c in range(QC):
                    sp.wait_ge(divided, it * QC + c + 2)
                    sp.dma_start(keep["ao"][ds(it * QC + c, 1), :, :, :].rearrange("n q p e -> p (n q) e"),
                                 ob[c % 2][:, :, :, :].rearrange("p q h e -> p q (h e)")).then_inc(stored[c % 2], 16)
            iterations(sp, lambda: load(0, 0), body)
            for s in range(2):
                sp.wait_ge(stored[s], 16 + 16 * NIT * QC // 2)

        @block.vector
        def _(dve):
            v = nc.vector
            T.begin_dve(dve)
            dve.sem_inc(out_copied, 2)
            dve.sem_inc(divided, 1)

            def finish(it, c):
                s = c % 2
                dve.wait_ge(pv_done, it * NST + LAST[c] + 3)
                v.tensor_copy(OT[s][:, :], pO[s][:, :]).then_inc(out_copied, 1)
                dve.wait_ge(out_turned, it * QC + c + 1)
                y = pY[:, :, :].rearrange("p q (h e) -> p q h e", h=4)
                v.reciprocal(rc[:, :, :], y[:, :, :, HD])
                dve.drain()
                dve.wait_ge(stored[s], (it * 2 + c // 2) * 16 + 16)
                v.tensor_tensor(ob[s][:, :, :, :], y[:, :, :, 0:HD], rc[:, :, :].unsqueeze(3).broadcast_to([P, 4, 4, HD]),
                                ALU.mult).then_inc(divided, 1)

            def evict(n, qd, par):
                for gi in range(4):
                    T.evict(dve, n, qd, gi, par)

            def first():
                dve.wait_ge(qk_loaded, 32)
                for qd in range(4):
                    T.split(dve, 0, qd)
                    evict(0, qd, 0)

            def body(it, par, j, more):
                if more:
                    n = it + 1
                    dve.wait_ge(qk_loaded, it * 32 + 64)
                    T.split(dve, n, 0)
                    T.split(dve, n, 1)
                finish(it, 0)
                if more:
                    dve.wait_ge(pv_done, it * NST + 2)
                    evict(n, 0, 1 - par)
                    T.split(dve, n, 2)
                finish(it, 1)
                if more:
                    evict(n, 1, 1 - par)
                    T.split(dve, n, 3)
                    evict(n, 2, 1 - par)
                finish(it, 2)
                if more:
                    evict(n, 3, 1 - par)
                finish(it, 3)
            iterations(dve, first, body)

        @block.scalar
        def _(act):
            act.sem_inc(exp_done, 2)

            def body(it, par, j, more):
                for n, (c, kb) in enumerate(STEPS):
                    off = max(0, kb - 4 * c) * P
                    for p in range(2):
                        unit = n * 2 + p
                        act.wait_ge(scored, it * (2 * NST) + unit + 1)
                        if p == 0:
                            act.wait_ge(pv_done, it * NST + n + 1)
                        nc.scalar.activation(PT[unit % 4][:, :, off:512], pS[p][:, :, off:512], ACT.Exp, scale=HD ** -0.5).then_inc(exp_done, 1)
            iterations(act, lambda: None, body)

        @block.tensor
        def _(pe):
            mm = nc.tensor.matmul
            pe.sem_inc(pv_done, 2)
            pe.wait_ge(made, 2)

            def scores(it, par, n):
                c, kb = STEPS[n]
                off = max(0, kb - 4 * c) * P
                for p in range(2):
                    pe.wait_ge(exp_done, it * (2 * NST) + n * 2 + p + 1)
                    for a in range(2):
                        h = 2 * p + a
                        last = mm(pS[p][:, a, off:512], KT[par][0:KS, h, kb * P:(kb + 1) * P],
                                  QT[par][0:KS, h, c * 512 + off:(c + 1) * 512], start=True, stop=kb < 4 * c)
                        if kb >= 4 * c:
                            last = mm(pS[p][:, a, off:off + P], identb[:, :], mask[:, :], start=False, stop=True)
                    last.then_inc(scored, 1)

            def values(it, par, n):
                c, kb = STEPS[n]
                off = max(0, kb - 4 * c) * P
                if kb == 0:
                    pe.wait_ge(out_copied, it * QC + c + 1)
                pe.wait_ge(exp_done, it * (2 * NST) + n * 2 + 4)
                for h in range(4):
                    last = mm(pO[c % 2][32 * h:32 * h + 32, off:512], V[par][:, kb, 32 * h:32 * h + 32],
                              PT[(n * 2 + h // 2) % 4][:, h % 2, off:512], start=(kb == 0), stop=(kb == 4 * c + 3))
                last.then_inc(pv_done, 1)

            def turn_out(it, c):
                pe.wait_ge(out_copied, it * QC + c + 3)
                pe.wait_ge(divided, it * QC + c + 1)
                for q in range(4):
                    last = nc.tensor.transpose(pY[:, q, :], OT[c % 2][:, q * P:(q + 1) * P], ident[:, :])
                last.then_inc(out_turned, 1)

            def first():
                for qd in range(4):
                    for gi in range(4):
                        T.turn(pe, 0, qd, gi)

            extra = {}
            for c in range(1, QC):
                extra.setdefault((c, 2), []).append(("out", c - 1))
            for qd, (c, kb) in enumerate(((1, 3), (2, 3), (2, 7), (3, 4))):
                for gi in range(4):
                    extra.setdefault((c, kb + gi), []).append((qd, gi))

            def body(it, par, j, more):
                pe.wait_ge(T.evicted, it * 16 + 17)
                pe.wait_ge(v_loaded[par], j * 32 + 32)
                for n, (c, kb) in enumerate(STEPS):
                    scores(it, par, n)
                    if n:
                        values(it, par, n - 1)
                    for what, x in extra.get((c, kb), []):
                        if what == "out":
                            turn_out(it, x)
                        elif more:
                            T.turn(pe, it + 1, what, x)
                values(it, par, NST - 1)
                turn_out(it, QC - 1)
            iterations(pe, first, body)


def project_out(nc, mem, io, keep, st):
    X, ident = keep["X"], keep["ident"]
    W = mem.sb("W", [P, DC, D])
    a = [mem.sb(f"a{k}", [P, 4, G, 4 * HD]) for k in range(2)]
    aT = [mem.sb(f"aT{f}", [P, DC, P]) for f in range(4)]
    w_loaded, a_ready, turned, aT_ready, projected, x_ready = (mem.sem(n) for n in (
        "w_loaded", "a_ready", "turned", "aT_ready", "projected", "x_ready"))
    a_loaded = [mem.sem(f"a_loaded{k}") for k in range(2)]
    pT = [mem.ps(f"pT{u}", [P, DC, P]) for u in range(2)]
    pP = [mem.ps(f"pP{u}", [P, D]) for u in range(2)]
    with nc.Block() as block:
        @block.sync
        def _(sp):
            sp.dma_start(W[:, :, :], io["WoT"].rearrange("(c p) n -> p c n", p=P)).then_inc(w_loaded, 16)
            with sp.Fori(0, B) as b:
                for c in range(4):
                    k = c % 2
                    sp.wait_ge(turned, (b * 4 + c) * 4 + 4)
                    for g in range(G):
                        sp.dma_start(a[k][:, :, g, :], keep["ao"][ds(b * 16 + g * 4 + c, 1), :, :, :].rearrange("n q p e -> p (n q) e"))\
                          .then_inc(a_loaded[k], 16)

        @block.vector
        def _(dve):
            dve.sem_inc(x_ready, 2)
            with dve.Fori(0, NT // 4) as q:
                for f in range(4):
                    t = q * 4 + f
                    dve.wait_ge(projected, t + 1)
                    nc.vector.tensor_tensor(X[:, ds(t, 1), :], X[:, ds(t, 1), :], pP[f % 2][:, :].unsqueeze(1), ALU.add).then_inc(x_ready, 1)
                    dve.drain()
                    nc.vector.bn_stats(st[:, ds(t, 1), :], X[:, ds(t, 1), :])

        @block.scalar
        def _(act):
            act.sem_inc(aT_ready, 2)
            with act.Fori(0, NT // 4) as q:
                for f in range(4):
                    act.wait_ge(turned, q * 4 + f + 9)
                    nc.scalar.activation(aT[f][:, :, :], pT[f % 2][:, :, :], ACT.Copy).then_inc(aT_ready, 1)

        @block.tensor
        def _(pe):
            pe.sem_inc(turned, 8)
            pe.wait_ge(w_loaded, 16)
            with pe.Fori(0, NT // 8) as q:
                for k in range(2):
                    def turn(f):
                        pe.wait_ge(aT_ready, q * 8 + k * 4 + f + 1)
                        av = a[k][:, f, :, :].rearrange("p g e -> p (g e)")
                        for c in range(DC):
                            last = nc.tensor.transpose(pT[f % 2][:, c, :], av[:, c * P:(c + 1) * P], ident[:, :])
                        last.then_inc(turned, 1)

                    def project(f):
                        pe.wait_ge(aT_ready, q * 8 + k * 4 + f + 3)
                        pe.wait_ge(x_ready, q * 8 + k * 4 + f + 1)
                        for c in range(DC):
                            last = nc.tensor.matmul(pP[f % 2][:, :], aT[f][:, c, :], W[:, c, :], start=(c == 0), stop=(c == DC - 1))
                        last.then_inc(projected, 1)
                    pe.wait_ge(a_loaded[k], q * (16 * G) + 16 * G)
                    for f in range(4):
                        turn(f)
                        if f:
                            project(f - 1)
                    project(3)


NPT = 2 * NT + E1


def route(nc, mem, io, keep):
    X, mean, rstd, ident = keep["X"], keep["mean"], keep["rstd"], keep["ident"]
    wt, dest, which = keep["wt"], keep["dest"], keep["which"]
    R = mem.sb("R", [P, DC, E1])
    z = [mem.sb(f"z{f}", [P, D]) for f in range(4)]
    zT = [mem.sb(f"zT{f}", [P, DC, P]) for f in range(4)]
    rw = mem.sb("rw", [P, NT, E1])
    M1, M2 = mem.sb("M1", [P, NT, E1]), mem.sb("M2", [P, NT, E1])
    t1, t2 = mem.sb("t1", [P, NT, E1]), mem.sb("t2", [P, NT, E1])
    Mb = mem.sb("Mb", [P, NT, E1], bf16)
    before, onesb = mem.sb("before", [P, P], bf16), mem.sb("onesb", [P, P], bf16)
    code = mem.sb("code", [P, E1])
    row = mem.sb("row", [P, NPT])
    s1, s2 = mem.sb("s1", [P, NT]), mem.sb("s2", [P, NT])
    n1, n2, nt, ni = mem.sb("n1", [P, E1]), mem.sb("n2", [P, E1]), mem.sb("nt", [P, E1]), mem.sb("ni", [P, E1], mybir.dt.int32)
    wf = mem.sb("wf", [1, NPT])
    codei, rowi = mem.sb("codei", [P, E1], mybir.dt.int32), mem.sb("rowi", [P, NPT], mybir.dt.int32)
    z_ready, turned, zT_ready, l_done, l_ready, made, w_loaded = (mem.sem(n) for n in (
        "z_ready", "turned", "zT_ready", "l_done", "l_ready", "made", "w_loaded"))
    less_max, exps, chosen, ranked = (mem.sem(n) for n in ("less_max", "exps", "chosen", "ranked"))

    with ExitStack() as sub:
        m = Memory(nc, sub, "rt1")
        pT = [m.ps(f"pT{u}", [P, DC, P]) for u in range(2)]
        pR = [m.ps(f"pR{u}", [P, E1]) for u in range(2)]
        block = sub.enter_context(nc.Block())

        @block.sync
        def _(sp):
            sp.dma_start(R[:, :, :], io["routerT"].rearrange("(c p) n -> p c n", p=P)).then_inc(w_loaded, 16)

        @block.gpsimd
        def _(pool):
            g = nc.gpsimd
            g.memset(before[:, :], 1.0).then_inc(made, 1)
            g.memset(onesb[:, :], 1.0)
            pool.wait_ge(made, 1)
            g.affine_select(out=before[:, :], in_=before[:, :], compare_op=ALU.is_gt, fill=0.0,
                            base=0, pattern=[[1, P]], channel_multiplier=-1)
            g.iota(codei[:, :], pattern=[[-1, E1]], base=E1, channel_multiplier=0)
            g.iota(rowi[:, :], pattern=[[1, NPT]], base=0, channel_multiplier=0)

        @block.vector
        def _(dve):
            dve.sem_inc(l_ready, 2)
            with dve.Fori(0, NT // 4) as q:
                for f in range(4):
                    dve.wait_ge(turned, q * 4 + f + 1)
                    nc.vector.tensor_scalar(z[f][:, :].unsqueeze(1), X[:, ds(q * 4 + f, 1), :], mean[:, ds(q * 4 + f, 1)],
                                            rstd[:, ds(q * 4 + f, 1)], ALU.subtract, ALU.mult).then_inc(z_ready, 1)
                for f in range(4):
                    dve.wait_ge(l_done, q * 4 + f + 1)
                    nc.vector.tensor_copy(rw[:, ds(q * 4 + f, 1), :], pR[f % 2][:, :].unsqueeze(1)).then_inc(l_ready, 1)

        @block.scalar
        def _(act):
            act.sem_inc(zT_ready, 2)
            with act.Fori(0, NT // 4) as q:
                for f in range(4):
                    act.wait_ge(turned, q * 4 + f + 5)
                    nc.scalar.activation(zT[f][:, :, :], pT[f % 2][:, :, :], ACT.Copy).then_inc(zT_ready, 1)

        @block.tensor
        def _(pe):
            pe.sem_inc(turned, 4)
            pe.wait_ge(w_loaded, 16)
            with pe.Fori(0, NT // 4) as q:
                def turn(f):
                    pe.wait_ge(z_ready, q * 4 + f + 1)
                    pe.wait_ge(zT_ready, q * 4 + f + 1)
                    for c in range(DC):
                        last = nc.tensor.transpose(pT[f % 2][:, c, :], z[f][:, c * P:(c + 1) * P], ident[:, :])
                    last.then_inc(turned, 1)

                def logits(f):
                    pe.wait_ge(zT_ready, q * 4 + f + 3)
                    pe.wait_ge(l_ready, q * 4 + f + 1)
                    for c in range(DC):
                        last = nc.tensor.matmul(pR[f % 2][:, :], zT[f][:, c, :], R[:, c, :], start=(c == 0), stop=(c == DC - 1))
                    last.then_inc(l_done, 1)
                for f in range(4):
                    turn(f)
                    if f:
                        logits(f - 1)
                logits(3)

    with ExitStack() as sub:
        m = Memory(nc, sub, "rt2")
        pB = m.ps("pB", [P, NT * E1])
        pC = m.ps("pC", [P, NT * E1])
        block = sub.enter_context(nc.Block())
        wide = lambda a: a.unsqueeze(2).broadcast_to([P, NT, E1])
        per = lambda a: a.unsqueeze(1).broadcast_to([P, NT, E1])

        @block.vector
        def _(dve):
            v = nc.vector

            def step(*ops):
                for op in ops:
                    op()
                dve.drain()
            A = lambda t: t[:, :, :]
            tt = lambda o, a, b, op: (lambda: v.tensor_tensor(o, a, b, op))
            ts = lambda o, a, s, op, s2=None, op2=ALU.bypass: (lambda: v.tensor_scalar(o, a, s, s2, op, op2))
            red = lambda o, a, op: (lambda: v.tensor_reduce(o, a, AX, op))
            step(red(s1[:, :], A(rw), ALU.max), lambda: v.tensor_copy(code[:, :], codei[:, :]), lambda: v.tensor_copy(row[:, :], rowi[:, :]))
            step(tt(A(rw), A(rw), wide(s1[:, :]), ALU.subtract))
            dve.drain().then_inc(less_max, 1)
            dve.wait_ge(exps, 1)
            step(red(s1[:, :], A(rw), ALU.add))
            step(lambda: v.reciprocal(s1[:, :], s1[:, :]))
            step(tt(A(rw), A(rw), wide(s1[:, :]), ALU.mult))
            for k, Mk in enumerate((M1, M2)):
                src = rw if k == 0 else t2
                best = wt[:, k, :]
                step(red(best, A(src), ALU.max))
                step(tt(A(t1), A(src), wide(best), ALU.is_equal))
                step(tt(A(t1), A(t1), per(code[:, :]), ALU.mult))
                step(red(s1[:, :], A(t1), ALU.max))
                step(tt(A(Mk), per(code[:, :]), wide(s1[:, :]), ALU.is_equal))
                if k == 0:
                    step(ts(A(t1), A(M1), 2.0, ALU.mult))
                    step(tt(A(t2), A(rw), A(t1), ALU.subtract))
            step(tt(A(Mb), A(M1), A(M2), ALU.add))
            dve.drain().then_inc(chosen, 1)
            dve.wait_ge(ranked, 1)
            pc = pC[:, :].rearrange("p (t e) -> p t e", e=E1)
            pb = pB[:, :].rearrange("p (t e) -> p t e", e=E1)
            step(lambda: v.tensor_copy(A(t1), pc))
            a, c = t1, t2
            n = 1
            while n < NT:
                step(tt(c[:, n:, :], a[:, n:, :], a[:, :NT - n, :], ALU.add), lambda n=n, a=a, c=c: v.tensor_copy(c[:, :n, :], a[:, :n, :]))
                a, c = c, a
                n *= 2
            step(ts(nt[:, :], a[:, NT - 1, :], float(P - 1), ALU.add))
            step(lambda: v.tensor_copy(ni[:, :], nt[:, :]))
            step(ts(ni[:, :], ni[:, :], 7, ALU.arith_shift_right))
            step(lambda: v.tensor_copy(nt[:, :], ni[:, :]), lambda: v.tensor_copy(n1[:, :], ni[:, :]))
            x, y = n1, n2
            n = 1
            while n < E1:
                step(tt(y[:, n:], x[:, n:], x[:, :E1 - n], ALU.add), lambda n=n, x=x, y=y: v.tensor_copy(y[:, :n], x[:, :n]))
                x, y = y, x
                n *= 2
            step(tt(nt[:, :], x[:, :], nt[:, :], ALU.subtract))
            step(ts(nt[:, :], nt[:, :], float(P), ALU.mult))
            step(tt(A(a), A(a), pc, ALU.subtract))
            step(tt(A(a), A(a), pb, ALU.add))
            step(tt(A(a), A(a), per(nt[:, :]), ALU.add))
            for k, Mk in enumerate((M1, M2)):
                step(tt(A(c), A(a), A(Mk), ALU.mult))
                step(red(s2[:, :], A(c), ALU.add))
                step(lambda: v.tensor_copy(dest[:, k, :], s2[:, :]))
            cnt = t1[0:1, :, :].rearrange("p t e -> p (t e)")
            for lo in range(0, NPT, 64):
                w = min(64, NPT - lo)
                sl = cnt[:, 0:w * E1].rearrange("p (t e) -> p t e", e=E1)
                step(tt(sl, row[0:1, lo:lo + w].unsqueeze(2).broadcast_to([1, w, E1]),
                        x[0:1, :].unsqueeze(1).broadcast_to([1, w, E1]), ALU.is_ge))
                step(red(wf[:, lo:lo + w], sl, ALU.add))
            step(ts(wf[:, :], wf[:, :], float(E1 - 1), ALU.min))
            v.tensor_copy(which[:, :], wf[:, :])

        @block.scalar
        def _(act):
            act.wait_ge(less_max, 1)
            nc.scalar.activation(rw[:, :, :], rw[:, :, :], ACT.Exp).then_inc(exps, 1)

        @block.tensor
        def _(pe):
            pe.wait_ge(chosen, 1)
            flat = Mb[:, :, :].rearrange("p t e -> p (t e)")
            for src, dst in ((before, pB), (onesb, pC)):
                for c in range(0, NT * E1, 512):
                    last = nc.tensor.matmul(dst[:, c:c + 512], src[:, :], flat[:, c:c + 512], start=True, stop=True)
            last.then_inc(ranked, 1)


def experts(nc, mem, io, keep):
    X, mean, rstd, ident = keep["X"], keep["mean"], keep["rstd"], keep["ident"]
    wt, dest, which = keep["wt"], keep["dest"], keep["which"]
    xg, yg = keep["xg"], keep["yg"]
    i32 = mybir.dt.int32
    W = mem.sb("W", [P, DC, E1, D])
    w_loaded = [mem.sem(f"w_loaded{c}") for c in range(2)]

    with ExitStack() as sub:
        m = Memory(nc, sub, "ex1")
        z = [m.sb(f"z{f}", [P, D]) for f in range(4)]
        zw = [[m.sb(f"zw{k}{f}", [P, D]) for f in range(4)] for k in range(2)]
        ix = [[m.sb(f"ix{k}{f}", [P, 1], i32) for f in range(4)] for k in range(2)]
        sent = [[m.sem(f"sent{k}{f}") for f in range(4)] for k in range(2)]
        ready, seen = m.sem("ready"), m.sem("seen")
        block = sub.enter_context(nc.Block())

        @block.sync
        def _(sp):
            for c in range(DC):
                sp.dma_start(W[:, c, :, :], io["we"][:, c * P:(c + 1) * P, :].rearrange("e p d -> p e d")).then_inc(w_loaded[c], 16)

        @block.vector
        def _(dve):
            v = nc.vector

            def copies(q):
                for f in range(4):
                    t = q * 4 + f
                    v.tensor_scalar(z[f][:, :].unsqueeze(1), X[:, ds(t, 1), :], mean[:, ds(t, 1)], rstd[:, ds(t, 1)], ALU.subtract, ALU.mult)
                    dve.drain()
                    for k in range(2):
                        if not (isinstance(q, int) and q == 0):
                            dve.wait_ge(sent[k][f], q * 16)
                        v.tensor_copy(ix[k][f][:, :], dest[:, k, ds(t, 1)])
                        v.tensor_scalar(zw[k][f][:, :], z[f][:, :], wt[:, k, ds(t, 1)], None, ALU.mult)
                    dve.drain().then_inc(ready, 1)
            copies(0)
            with dve.Fori(1, NT // 4) as q:
                copies(q)

        @block.gpsimd
        def _(pool):
            with pool.Fori(0, NT // 4) as q:
                for f in range(4):
                    pool.wait_ge(ready, q * 4 + f + 1)
                    pool.sem_inc(seen, 1)
                    for k in range(2):
                        nc.gpsimd.indirect_dma_start(out=xg, out_offset=bass.IndirectOffsetOnAxis(ap=ix[k][f][:, 0:1], axis=0),
                                                     in_=zw[k][f][:, :], in_offset=None).then_inc(sent[k][f], 16)
            for k in range(2):
                for f in range(4):
                    pool.wait_ge(sent[k][f], 16 * (NT // 4))

    with ExitStack() as sub:
        m = Memory(nc, sub, "ex2")
        NB = 4
        xin = [m.sb(f"xin{k}", [P, NB, D]) for k in range(2)]
        xT = [m.sb(f"xT{f}", [P, DC, P]) for f in range(4)]
        yout = [m.sb(f"yout{k}", [P, NB, D]) for k in range(2)]
        x_in = [m.sem(f"x_in{k}") for k in range(2)]
        y_out = [m.sem(f"y_out{k}") for k in range(2)]
        turned, xT_ready, multiplied, y_ready = (m.sem(n) for n in ("turned", "xT_ready", "multiplied", "y_ready"))
        pT = [m.ps(f"pT{u}", [P, DC, P]) for u in range(2)]
        pY = [m.ps(f"pY{u}", [P, D]) for u in range(2)]
        xgv = xg.rearrange("(q n p) d -> q n p d", n=NB, p=P)
        ygv = yg.rearrange("(q n p) d -> q n p d", n=NB, p=P)
        block = sub.enter_context(nc.Block())

        @block.sync
        def _(sp):
            for k in range(2):
                sp.sem_inc(y_out[k], 16)

            def load(r, k):
                sp.wait_ge(turned, (r * 2 + k) * NB + NB)
                sp.dma_start(xin[k][:, :, :], xgv[ds(r * 2 + k, 1), :, :, :].rearrange("q n p d -> p (q n) d")).then_inc(x_in[k], 16)

            def keep_y(r, k):
                sp.wait_ge(y_ready, (r * 2 + k) * NB + NB + 2)
                sp.dma_start(ygv[ds(r * 2 + k, 1), :, :, :].rearrange("q n p d -> p (q n) d"), yout[k][:, :, :]).then_inc(y_out[k], 16)
            load(0, 0)
            load(0, 1)
            with sp.Fori(1, NPT // NB // 2) as r:
                for k in range(2):
                    load(r, k)
                    keep_y(r - 1, k)
            for k in range(2):
                keep_y(NPT // NB // 2 - 1, k)
            for k in range(2):
                sp.wait_ge(y_out[k], 16 + 16 * (NPT // NB // 2))

        @block.vector
        def _(dve):
            dve.sem_inc(y_ready, 2)
            with dve.Fori(0, NPT // NB // 2) as r:
                for k in range(2):
                    dve.wait_ge(y_out[k], r * 16 + 16)
                    for f in range(NB):
                        dve.wait_ge(multiplied, r * 8 + k * 4 + f + 1)
                        nc.vector.tensor_copy(yout[k][:, f, :], pY[f % 2][:, :]).then_inc(y_ready, 1)

        @block.scalar
        def _(act):
            act.sem_inc(xT_ready, 2)
            with act.Fori(0, NPT // NB) as q:
                for f in range(NB):
                    act.wait_ge(turned, q * 4 + f + 9)
                    nc.scalar.activation(xT[f][:, :, :], pT[f % 2][:, :, :], ACT.Copy).then_inc(xT_ready, 1)

        @block.tensor
        def _(pe):
            pe.sem_inc(turned, 2 * NB)
            for c in range(DC):
                pe.wait_ge(w_loaded[c], 16)
            with pe.Fori(0, NPT // NB // 2) as r:
                for k in range(2):
                    def turn(f):
                        pe.wait_ge(xT_ready, r * 8 + k * 4 + f + 1)
                        for c in range(DC):
                            last = nc.tensor.transpose(pT[f % 2][:, c, :], xin[k][:, f, c * P:(c + 1) * P], ident[:, :])
                        last.then_inc(turned, 1)

                    def multiply(f):
                        e = pe.value_load(which[0:1, ds(r * 8 + k * 4 + f, 1)], min_val=0, max_val=E1 - 1)
                        pe.wait_ge(xT_ready, r * 8 + k * 4 + f + 3)
                        pe.wait_ge(y_ready, r * 8 + k * 4 + f + 1)
                        for c in range(DC):
                            last = nc.tensor.matmul(pY[f % 2][:, :].unsqueeze(1), xT[f][:, c, :], W[:, c, ds(e, 1), :],
                                                    start=(c == 0), stop=(c == DC - 1))
                        last.then_inc(multiplied, 1)
                    pe.wait_ge(x_in[k], r * 16 + 16)
                    for f in range(NB):
                        turn(f)
                        if f:
                            multiply(f - 1)
                    multiply(NB - 1)

    with ExitStack() as sub:
        m = Memory(nc, sub, "ex3")
        y = [[m.sb(f"y{k}{f}", [P, D]) for f in range(4)] for k in range(2)]
        ix = [[m.sb(f"ix{k}{f}", [P, 1], i32) for f in range(4)] for k in range(2)]
        res = [m.sb(f"res{f}", [P, D]) for f in range(4)]
        got = [[m.sem(f"got{k}{f}") for f in range(4)] for k in range(2)]
        stored = [m.sem(f"stored{f}") for f in range(4)]
        named, added, seen = m.sem("named"), m.sem("added"), m.sem("seen")
        ov = io["out"].rearrange("b (t p) d -> (b t) p d", p=P)
        block = sub.enter_context(nc.Block())

        @block.vector
        def _(dve):
            v = nc.vector
            dve.sem_inc(added, 4)
            for f in range(4):
                dve.sem_inc(stored[f], 16)

            def name(q, f):
                for k in range(2):
                    v.tensor_copy(ix[k][f][:, :], dest[:, k, ds(q * 4 + f, 1)])
                dve.drain().then_inc(named, 1)

            def add(q, f):
                t = q * 4 + f
                for k in range(2):
                    dve.wait_ge(got[k][f], q * 16 + 16)
                dve.wait_ge(stored[f], q * 16 + 16)
                v.tensor_tensor(res[f][:, :].unsqueeze(1), X[:, ds(t, 1), :], y[0][f][:, :].unsqueeze(1), ALU.add)
                dve.drain()
                v.tensor_tensor(res[f][:, :], res[f][:, :], y[1][f][:, :], ALU.add).then_inc(added, 1)
            for f in range(4):
                name(0, f)
            with dve.Fori(1, NT // 4) as q:
                for f in range(4):
                    add(q - 1, f)
                    name(q, f)
            for f in range(4):
                add(NT // 4 - 1, f)

        @block.gpsimd
        def _(pool):
            with pool.Fori(0, NT // 4) as q:
                for f in range(4):
                    pool.wait_ge(named, q * 4 + f + 1)
                    pool.sem_inc(seen, 1)
                    for k in range(2):
                        nc.gpsimd.indirect_dma_start(out=y[k][f][:, :], out_offset=None, in_=yg,
                                                     in_offset=bass.IndirectOffsetOnAxis(ap=ix[k][f][:, 0:1], axis=0)).then_inc(got[k][f], 16)

        @block.sync
        def _(sp):
            with sp.Fori(0, NT // 4) as q:
                for f in range(4):
                    sp.wait_ge(added, q * 4 + f + 5)
                    sp.dma_start(ov[ds(q * 4 + f, 1), :, :].rearrange("n p d -> p n d"), res[f][:, :].unsqueeze(1)).then_inc(stored[f], 16)
            for f in range(4):
                sp.wait_ge(stored[f], 16 + 16 * (NT // 4))


def store(nc, mem, io, keep):
    X = keep["X"]
    stored = [mem.sem(f"stored{b}") for b in range(B)]
    ov = io["out"].rearrange("b (t p) d -> b p t d", p=P)
    with nc.Block() as block:
        @block.sync
        def _(sp):
            for b in range(B):
                sp.dma_start(ov[b], X[:, b * TPB:(b + 1) * TPB, :]).then_inc(stored[b], 16)
            for b in range(B):
                sp.wait_ge(stored[b], 16)


def build(nc, io):
    with ExitStack() as ctx:
        mem = Memory(nc, ctx, "all")
        keep = {"X": mem.sb("X", [P, NT, D]), "ident": mem.sb("ident", [P, P]), "identb": mem.sb("identb", [P, P], bf16),
                "mean": mem.sb("mean", [P, NT]), "rstd": mem.sb("rstd", [P, NT])}
        st = mem.sb("stats", [P, NT, 6])
        def stage(name, f, *args):
            with ExitStack() as sub:
                own = Memory(nc, sub, name)
                f(nc, own, *args)
                if name in ("in", "n1", "n2", "bd"):
                    own.clear()
        stage("in", load_and_constants, io, keep, st)
        stage("n1", finish_rstd, keep, st, False)
        stage("la", linear_attention, io, keep, st)
        stage("n2", finish_rstd, keep, st, True)
        stage("sm", soft_mixture, io, keep, st)
        keep["qk"] = nc.dram_tensor("rotated_qk", (B * G, TPB, P, P), fp32).ap()
        keep["v"] = nc.dram_tensor("values", (B * G, TPB, P, 4 * VW), fp32).ap()
        keep["ao"] = nc.dram_tensor("head_outputs", (B * G * (N // 512), 4, P, 4 * HD), fp32).ap()
        keep["xg"] = nc.dram_tensor("rows_in", (NPT * P, D), fp32).ap()
        keep["yg"] = nc.dram_tensor("rows_out", (NPT * P, D), fp32).ap()
        keep["wt"] = mem.sb("wt", [P, 2, NT])
        keep["dest"] = mem.sb("dest", [P, 2, NT], mybir.dt.int32)
        keep["which"] = mem.sb("which", [1, NPT], mybir.dt.int32)
        keep["nmax"] = mem.sb("nmax", [P, B * G, TPB * 4])
        stage("n3", finish_rstd, keep, st, False)
        keep["need_max"] = mem.sb("need_max", [1, 1], mybir.dt.int32)
        with ExitStack() as sub:
            nn = Memory(nc, sub, "qk").sb("nn", [P, NT, 3 * H])
            stage("qk", project_qkv, io, keep, nn)
            stage("bd", bound_scores, io, keep, nn)
        stage("mx", row_maxima, io, keep)
        stage("at", attention, io, keep)
        stage("pr", project_out, io, keep, st)
        stage("n4", finish_rstd, keep, st, False)
        stage("rt", route, io, keep)
        stage("ex", experts, io, keep)


_OUTS = [((4, 2048, 256), 'float32')]


def kernel(**inputs):
    import numpy as _np
    import concourse.bacc as _bacc
    from concourse import mybir as _mybir
    from concourse.bass_utils import run_bass_kernel_spmd as _run

    nc = _bacc.Bacc("TRN2", target_bir_lowering=False, num_devices=1)
    c = _np.ascontiguousarray
    i = {k: _np.asarray(v) for k, v in inputs.items()}
    laid = {
        "x": c(i["L0_attn_x"]),
        "qkvT": c(i["L0_attn_qkv_w"].T), "qkv_b": c(i["L0_attn_qkv_b"]),
        "projT": c(i["L0_attn_proj_w"].T), "proj_b": c(i["L0_attn_proj_b"]),
        "pmT": c(i["L0_attn_projection_matrix"].T),
        "gamma": c(i["L0_ffn_ln_gamma"]), "beta": c(i["L0_ffn_ln_beta"]),
        "mu": c(i["L0_ffn_mu"].reshape(256, 256)), "scale": c(i["L0_ffn_scale"]),
        "w1": c(i["L0_ffn_w1"]), "b1": c(i["L0_ffn_b1"]), "w2": c(i["L0_ffn_w2"]), "b2": c(i["L0_ffn_b2"]),
        "WqT": c(i["L1_attn_Wq"].T), "WkT": c(i["L1_attn_Wk"].T), "WvT": c(i["L1_attn_Wv"].T),
        "WoT": c(i["L1_attn_Wo"].T),
        "routerT": c(i["L1_ffn_router_w"].T), "we": c(i["L1_ffn_expert_weights"]),
    }
    laid.update(tables())
    io, arrays = {}, {}
    for name, a in laid.items():
        arrays[f"in_{name}"] = a
        io[name] = nc.dram_tensor(f"in_{name}", a.shape, _mybir.dt.from_np(a.dtype), kind="ExternalInput").ap()
    for n, (shape, dtype) in enumerate(_OUTS):
        io["out"] = nc.dram_tensor(f"out_{n}_dram", shape, _mybir.dt.from_np(_np.dtype(dtype)), kind="ExternalOutput").ap()
    build(nc, io)
    r = _run(nc, [arrays], core_ids=[0])
    return r.results[0]["out_0_dram"]
```

```python
import concourse.bass as bass
from concourse import mybir
from contextlib import ExitStack
import numpy as np

fp32 = mybir.dt.float32
bf16 = mybir.dt.bfloat16
ALU = mybir.AluOpType
ACT = mybir.ActivationFunctionType
AX = mybir.AxisListType.X
ds = bass.ds

B, N, D = 4, 2048, 256
P = 128
TPB = N // P
NT = B * TPB
H, HD = 16, 16
M = 64
DC = D // P
VW = 32
G = H // 4
E0, S0, HID = 16, 16, 64
NS = E0 * S0
E1 = 32
LN_EPS = 1e-5
FEAT_EPS = 1e-6
MASKED = -1e30


class Memory:

    def __init__(self, nc, ctx, stage):
        self.nc, self.ctx, self.stage, self.sems = nc, ctx, stage, []

    def sb(self, name, shape, dt=fp32):
        return self.ctx.enter_context(self.nc.sbuf_tensor(f"{self.stage}_{name}", shape, dt))

    def ps(self, name, shape, dt=fp32):
        return self.ctx.enter_context(self.nc.psum_tensor(f"{self.stage}_{name}", shape, dt))

    def sem(self, name):
        self.sems.append(self.ctx.enter_context(self.nc.semaphore(f"{self.stage}_{name}")))
        return self.sems[-1]

    def clear(self):
        with self.nc.Block() as block:
            @block.gpsimd
            def _(pool):
                for s in self.sems:
                    pool.sem_clear(s)


def in_pairs(eng, front, back):
    front(0, 0)
    front(1, 1)
    back(0, 0)
    with eng.Fori(1, TPB // 4) as q:
        front(q * 2, 0)
        back(q * 2 - 1, 1)
        front(q * 2 + 1, 1)
        back(q * 2, 0)
    back(TPB // 2 - 1, 1)


def finish_rstd(nc, mem, keep, st, extra_norm):
    mean, rstd = keep["mean"], keep["rstd"]
    t1, t2, ve = mem.sb("ln_t1", [P, NT]), mem.sb("ln_t2", [P, NT]), mem.sb("ln_ve", [P, NT])
    var = mem.sb("ln_var", [P, NT])
    ve_ready, root_ready = mem.sem("ve_ready"), mem.sem("root_ready")
    rounds = 2 if extra_norm else 1
    with nc.Block() as block:
        @block.vector
        def _(dve):
            v = nc.vector
            v.tensor_tensor(mean[:, :], st[:, :, 1], st[:, :, 4], ALU.add)
            v.tensor_tensor(t1[:, :], st[:, :, 1], st[:, :, 4], ALU.subtract)
            v.tensor_tensor(var[:, :], st[:, :, 2], st[:, :, 5], ALU.add)
            dve.drain()
            v.tensor_scalar(mean[:, :], mean[:, :], 0.5, None, ALU.mult)
            v.tensor_tensor(t1[:, :], t1[:, :], t1[:, :], ALU.mult)
            v.tensor_scalar(var[:, :], var[:, :], 1.0 / D, None, ALU.mult)
            dve.drain()
            v.tensor_scalar(t1[:, :], t1[:, :], 0.25, None, ALU.mult)
            dve.drain()
            v.tensor_tensor(var[:, :], var[:, :], t1[:, :], ALU.add)
            dve.drain()
            for r in range(rounds):
                v.tensor_scalar(ve[:, :], var[:, :], LN_EPS, None, ALU.add).then_inc(ve_ready, 1)
                dve.wait_ge(root_ready, r + 1)
                v.reciprocal(t1[:, :], t2[:, :])
                dve.drain()
                v.tensor_tensor(t2[:, :], t1[:, :], t1[:, :], ALU.mult)
                dve.drain()
                v.tensor_tensor(t2[:, :], t2[:, :], ve[:, :], ALU.mult)
                dve.drain()
                v.tensor_scalar(t2[:, :], t2[:, :], -0.5, 1.5, ALU.mult, ALU.add)
                dve.drain()
                if r == 0:
                    v.tensor_tensor(rstd[:, :], t1[:, :], t2[:, :], ALU.mult)
                    dve.drain()
                    if extra_norm:
                        v.tensor_tensor(t1[:, :], rstd[:, :], rstd[:, :], ALU.mult)
                        dve.drain()
                        v.tensor_tensor(var[:, :], var[:, :], t1[:, :], ALU.mult)
                        dve.drain()
                else:
                    v.tensor_tensor(t1[:, :], t1[:, :], t2[:, :], ALU.mult)
                    dve.drain()
                    v.tensor_tensor(rstd[:, :], rstd[:, :], t1[:, :], ALU.mult)

        @block.scalar
        def _(act):
            for r in range(rounds):
                act.wait_ge(ve_ready, r + 1)
                nc.scalar.activation(t2[:, :], ve[:, :], ACT.Sqrt).then_inc(root_ready, 1)


def load_and_constants(nc, mem, io, keep, st):
    X = keep["X"]
    ident, identb = keep["ident"], keep["identb"]
    x_loaded = [mem.sem(f"x_loaded{b}") for b in range(B)]
    made = mem.sem("made")
    xv = io["x"].rearrange("b (t p) d -> b p t d", p=P)
    with nc.Block() as block:
        @block.sync
        def _(sp):
            for b in range(B):
                sp.dma_start(X[:, b * TPB:(b + 1) * TPB, :], xv[b]).then_inc(x_loaded[b], 16)

        @block.gpsimd
        def _(pool):
            nc.gpsimd.memset(ident[:, :], 0.0).then_inc(made, 1)
            pool.wait_ge(made, 1)
            nc.gpsimd.affine_select(out=ident[:, :], in_=ident[:, :], compare_op=ALU.not_equal, fill=1.0,
                                    base=0, pattern=[[-1, P]], channel_multiplier=1).then_inc(made, 1)
            pool.wait_ge(made, 2)
            nc.gpsimd.tensor_copy(identb[:, :], ident[:, :])

        @block.vector
        def _(dve):
            for b in range(B):
                dve.wait_ge(x_loaded[b], 16)
                with dve.Fori(0, TPB) as i:
                    nc.vector.bn_stats(st[:, ds(b * TPB + i, 1), :], X[:, ds(b * TPB + i, 1), :])


def tables():
    freq = 1.0 / 10000.0 ** (np.arange(0, HD, 2, dtype=np.float32) / HD)
    angle = np.arange(N, dtype=np.float32)[:, None] * freq.astype(np.float32)[None, :]
    return {"cos": np.cos(angle).astype(np.float32), "sin": np.sin(angle).astype(np.float32)}


def linear_attention(nc, mem, io, keep, st):
    X, mean, rstd, ident = keep["X"], keep["mean"], keep["rstd"], keep["ident"]
    W = mem.sb("qkv_w", [P, DC, 3 * D])
    PW = mem.sb("proj_w", [P, DC, D])
    FM = mem.sb("feature_w", [P, 8 * M])
    qb, kb = mem.sb("qb", [P, DC]), mem.sb("kb", [P, DC])
    vb, pb = mem.sb("vb", [P, D]), mem.sb("pb", [P, D])
    zeros = mem.sb("zeros", [P, D])
    z, zT = mem.sb("z", [P, 4, D]), mem.sb("zT", [P, DC, 512])
    kT = [mem.sb(f"kT{u}", [P, DC, 512]) for u in range(2)]
    qT = mem.sb("qT", [P, TPB // 4, DC, 512])
    vx = [mem.sb(f"vx{u}", [P, 4, H, VW]) for u in range(2)]
    ft = [mem.sb(f"ft{u}", [P, H * M]) for u in range(4)]
    mx = [mem.sb(f"mx{u}", [P, H]) for u in range(2)]
    kvs = mem.sb("kvs", [P, G * M])
    NU, DE = mem.sb("NU", [P, 8, 2 * HD]), mem.sb("DE", [P, 8, 2 * HD])
    FT = [mem.sb(f"FT{u}", [P, 8, 512]) for u in range(2)]
    dn, rd = ([mem.sb(f"{n}{h}", [P, 512]) for h in range(2)] for n in ("dn", "rd"))
    oT = [mem.sb(f"oT{u}", [P, DC, 512]) for u in range(2)]
    w_sem = mem.sem("weights")
    fm_sem = mem.sem("fm_loaded")
    fm_zero = mem.sem("fm_zero")

    with nc.Block() as block:
        @block.vector
        def _(dve):
            nc.vector.memset(FM[:, :], 0.0).then_inc(fm_zero, 1)
            nc.vector.memset(zeros[:, :], 0.0)
            nc.vector.memset(NU[:, :, :], 0.0)
            nc.vector.memset(DE[:, :, :], 0.0)
            for u in range(2):
                nc.vector.memset(vx[u][:, :, :, :], 0.0)
            dve.drain()
            for u in range(2):
                nc.vector.memset(vx[u][:, :, :, HD:HD + 1], 1.0)

        @block.sync
        def _(sp):
            n = 0
            for dst, src in ((W[:, :, :], io["qkvT"].rearrange("(c p) n -> p c n", p=P)),
                             (PW[:, :, :], io["projT"].rearrange("(c p) n -> p c n", p=P)),
                             (qb[:, :], io["qkv_b"][0:D].rearrange("(c p) -> p c", p=P)),
                             (kb[:, :], io["qkv_b"][D:2 * D].rearrange("(c p) -> p c", p=P)),
                             (vb[:, :], io["qkv_b"][2 * D:3 * D].partition_broadcast(P)),
                             (pb[:, :], io["proj_b"].partition_broadcast(P))):
                with nc.allow_non_contiguous_dma(reason="a bias as columns, once"):
                    sp.dma_start(dst, src).then_inc(w_sem, 16)
                n += 16
                sp.wait_ge(w_sem, n)
            sp.wait_ge(fm_zero, 1)
            for hl in range(8):
                sp.dma_start(FM[hl * HD:(hl + 1) * HD, hl * M:(hl + 1) * M], io["pmT"]).then_inc(fm_sem, 16)
            sp.wait_ge(fm_sem, 8 * 16)

    q_slot = {}
    for e in range(TPB):
        q_slot.setdefault(TPB + e + 2, []).extend([("Ea", e, 0), ("Eb", e, 0)])
    for qd in range(TPB // 4):
        for h in range(2):
            q_slot.setdefault(TPB + 4 * qd + 6 + h, []).extend([("D", qd, h), ("N", qd, h)])
        q_slot.setdefault(TPB + 4 * qd + 8, []).extend([("P", qd, 0), ("P", qd, 1)])
    LAST_SLOT = max(q_slot)
    q_units = [u for s in sorted(q_slot) for u in q_slot[s]]
    BY_ACT = ("Ea", "D")
    QU, KU = len(q_units), 8 * (TPB // 4)
    QA = sum(u[0] in BY_ACT for u in q_units)
    QD = QU - QA
    KA, KD = 6 * (TPB // 4), 2 * (TPB // 4)

    def q_emptied(unit):
        n = q_units.index(unit)
        by_act = unit[0] in BY_ACT
        return by_act, sum((u[0] in BY_ACT) == by_act for u in q_units[:n + 1])

    with ExitStack() as sub:
        m = Memory(nc, sub, "la")
        (z_ready, k_unit, k_by_act, k_by_dve, w_done, sub_done, exp_done, kf_ready, ft_used, kv_saved, kv_turned, kv_built,
         q_unit, q_by_act, q_by_dve, xb_done, seen) = (m.sem(n) for n in (
             "z_ready", "k_unit", "k_by_act", "k_by_dve", "w_done", "sub_done", "exp_done", "kf_ready", "ft_used", "kv_saved",
             "kv_turned", "kv_built", "q_unit", "q_by_act", "q_by_dve", "xb_done", "seen"))
        pW = [m.ps(f"pW{i}", [P, H * M]) for i in range(2)]
        R = [m.ps(f"R{i}", [P, 512]) for i in range(4)]
        pKV = R[3][:, 0:G * M]
        block = sub.enter_context(nc.Block())

        @block.vector
        def _(dve):
            v = nc.vector
            dve.sem_inc(sub_done, 2)
            dve.sem_inc(q_by_dve, 1)
            with dve.Fori(0, B) as b:
                def normalise(qd, fs):
                    if qd:
                        dve.wait_ge(k_unit, b * KU + 8 * (qd - 1) + 2)
                    for f in fs:
                        t = b * TPB + qd * 4 + f
                        v.tensor_scalar(z[:, f:f + 1, :], X[:, ds(t, 1), :], mean[:, ds(t, 1)], rstd[:, ds(t, 1)],
                                        ALU.subtract, ALU.mult).then_inc(z_ready, 1)

                def values(qd):
                    for w in range(2):
                        n = 8 * qd + 6 + w
                        dve.wait_ge(k_unit, b * KU + n + 1)
                        v.tensor_tensor(vx[qd % 2][:, 2 * w:2 * w + 2, :, 0:HD], R[n % 3][:, :].rearrange("p (a h e) -> p a h e", a=2, h=H),
                                        vb[:, :].rearrange("p (h e) -> p h e", h=H).unsqueeze(1).broadcast_to([P, 2, H, HD]),
                                        ALU.add).then_inc(k_by_dve, 1)

                def centre(s):
                    dve.wait_ge(w_done, b * (2 * TPB) + s + 1)
                    src = pW[s % 2][:, :].rearrange("p (h m) -> p h m", h=H)
                    v.tensor_reduce(mx[s % 2][:, :], src, AX, ALU.max)
                    dve.drain()
                    old = s - 4
                    if 0 <= old < TPB:
                        dve.wait_ge(ft_used, b * TPB + old + 1)
                    elif old >= TPB:
                        dve.wait_ge(q_unit, b * QU + q_units.index(("Eb", old - TPB, 0)) + 1)
                    v.tensor_tensor(ft[s % 4][:, :].rearrange("p (h m) -> p h m", h=H), src,
                                    mx[s % 2][:, :].unsqueeze(2).broadcast_to([P, H, M]), ALU.subtract).then_inc(sub_done, 1)

                def build_kv():
                    dve.wait_ge(kv_turned, b + 1)
                    for g in range(2):
                        rows = slice(g * M, (g + 1) * M)
                        src = R[3][rows, 0:2 * P].rearrange("p (c e) -> p c e", e=VW)
                        v.tensor_copy(NU[rows, :, g * HD:(g + 1) * HD], src[:, :, 0:HD])
                        last = v.tensor_copy(DE[rows, :, g * HD:(g + 1) * HD], src[:, :, HD:HD + 1].broadcast_to([M, 8, HD]))
                    last.then_inc(kv_built, 1)

                def empty(unit):
                    kind, x, h = unit
                    n = q_units.index(unit)
                    if kind == "D":
                        by_act, count = q_emptied(unit)
                        dve.wait_ge(q_by_act, b * QA + count + 1)
                        v.reciprocal(rd[h][:, :], dn[h][:, :])
                        dve.drain()
                        return
                    dve.wait_ge(q_unit, b * QU + n + 1)
                    src = R[n % 4]
                    if kind == "Eb":
                        v.tensor_scalar(FT[x // 4 % 2][:, 4:8, x % 4 * P:(x % 4 + 1) * P], src[:, :].rearrange("p (c t) -> p c t", c=4),
                                        0.125, FEAT_EPS, ALU.mult, ALU.add).then_inc(q_by_dve, 1)
                    elif kind == "N":
                        v.tensor_tensor(oT[x % 2][:, h, :], src[:, :], rd[h][:, :], ALU.mult).then_inc(q_by_dve, 1)
                    else:
                        t = b * TPB + 4 * x + 2 * h
                        v.tensor_tensor(X[:, ds(t, 2), :], X[:, ds(t, 2), :], src[:, :].rearrange("p (a d) -> p a d", a=2), ALU.add)\
                         .then_inc(q_by_dve, 1)
                        dve.drain()
                        for a in range(2):
                            v.bn_stats(st[:, ds(t + a, 1), :], X[:, ds(t + a, 1), :])

                normalise(0, range(4))
                normalise(1, range(4))
                values(0)
                for s in range(LAST_SLOT + 1):
                    if s < 2 * TPB:
                        centre(s)
                    qd, f = s // 4, s % 4
                    if f and qd + 2 < TPB // 4:
                        normalise(qd + 2, ((), (0, 1), (2,), (3,))[f])
                    if f == 3 and qd + 1 < TPB // 4:
                        values(qd + 1)
                    if s == TPB + 2:
                        build_kv()
                    if s == TPB + 8:
                        dve.wait_ge(xb_done, b * TPB + TPB)
                    for unit in q_slot.get(s, []):
                        if unit[0] != "Ea":
                            empty(unit)

        @block.scalar
        def _(act):
            sc = nc.scalar
            act.sem_inc(q_by_act, 1)
            with act.Fori(0, B) as b:
                def empty_k(n):
                    qd, kind, c = n // 8, n % 8 // 2, n % 2
                    act.wait_ge(k_unit, b * KU + n + 1)
                    if kind == 0:
                        last = sc.activation(zT[:, c, :], R[n % 3][:, :], ACT.Copy)
                    elif kind == 1:
                        last = sc.activation(kT[qd % 2][:, c, :], R[n % 3][:, :], ACT.Identity, bias=kb[:, c:c + 1])
                    else:
                        last = sc.activation(qT[:, qd, c, :], R[n % 3][:, :], ACT.Identity, bias=qb[:, c:c + 1])
                    last.then_inc(k_by_act, 1)

                def empty_q(unit):
                    kind, x, h = unit
                    n = q_units.index(unit)
                    act.wait_ge(q_unit, b * QU + n + 1)
                    if kind == "Ea":
                        sc.activation(FT[x // 4 % 2][:, 0:4, x % 4 * P:(x % 4 + 1) * P], R[n % 4][:, :].rearrange("p (c t) -> p c t", c=4),
                                      ACT.Copy, scale=0.125, bias=FEAT_EPS).then_inc(q_by_act, 1)
                    else:
                        if x:
                            act.wait_ge(q_by_dve, b * QD + q_emptied(("N", x - 1, h))[1] + 1)
                        sc.activation(dn[h][:, :], R[n % 4][:, :], ACT.Copy, bias=FEAT_EPS).then_inc(q_by_act, 1)

                for n in range(6):
                    empty_k(n)
                for s in range(LAST_SLOT + 1):
                    nxt = (s // 4 + 1) * 8 + s % 4 * 2
                    k_units = s % 4 < 3 and nxt < KU
                    if k_units:
                        empty_k(nxt)
                    for unit in q_slot.get(s, []):
                        if unit[0] == "Ea":
                            empty_q(unit)
                    if s < 2 * TPB:
                        act.wait_ge(sub_done, b * (2 * TPB) + s + 3)
                        sc.activation(ft[s % 4][:, :], ft[s % 4][:, :], ACT.Exp, scale=0.25).then_inc(exp_done, 1)
                    if k_units:
                        empty_k(nxt + 1)
                    if s == TPB + 1:
                        act.wait_ge(ft_used, b * TPB + TPB)
                        sc.activation(kvs[:, :], pKV, ACT.Copy).then_inc(kv_saved, 1)
                    for unit in q_slot.get(s, []):
                        if unit[0] == "D":
                            empty_q(unit)

        @block.gpsimd
        def _(pool):
            with pool.Fori(0, B) as b:
                for s in range(TPB):
                    pool.wait_ge(exp_done, b * (2 * TPB) + s + 1)
                    pool.sem_inc(seen, 1)
                    nc.gpsimd.tensor_scalar(ft[s % 4][:, :], ft[s % 4][:, :], 0.125, FEAT_EPS, ALU.mult, ALU.add).then_inc(kf_ready, 1)
                    pool.wait_ge(z_ready, b * TPB + s + 1)
                    pool.sem_inc(seen, 1)
                    nc.gpsimd.tensor_tensor(X[:, ds(b * TPB + s, 1), :], X[:, ds(b * TPB + s, 1), :], pb[:, :].unsqueeze(1), ALU.add).then_inc(xb_done, 1)

        @block.tensor
        def _(pe):
            mm = nc.tensor.matmul
            with pe.Fori(0, B) as b:
                def make_k(n):
                    qd, kind, c = n // 8, n % 8 // 2, n % 2
                    out = R[n % 3]
                    if n >= 3:
                        old = n - 3
                        if old % 8 < 6:
                            pe.wait_ge(k_by_act, b * KA + old // 8 * 6 + old % 8 + 1)
                        else:
                            pe.wait_ge(k_by_dve, b * KD + old // 8 * 2 + old % 8 - 5)
                    if kind == 0:
                        pe.wait_ge(z_ready, b * TPB + 4 * qd + 4)
                        for f in range(4):
                            last = nc.tensor.transpose(out[:, f * P:(f + 1) * P], z[:, f, c * P:(c + 1) * P], ident[:, :])
                    elif kind < 3:
                        col = (0, D, 0)[kind] + c * P
                        pe.wait_ge(k_by_act, b * KA + 6 * qd + 2)
                        for a in range(DC):
                            last = mm(out[:, :], W[:, a, col:col + P], zT[:, a, :], start=(a == 0), stop=(a == DC - 1))
                    else:
                        for w in range(2):
                            f = 2 * c + w
                            for a in range(DC):
                                last = mm(out[:, w * D:(w + 1) * D], zT[:, a, f * P:(f + 1) * P], W[:, a, 2 * D:3 * D],
                                          start=(a == 0), stop=(a == DC - 1))
                    last.then_inc(k_unit, 1)

                def exponents(s):
                    qd, f = s % TPB // 4, s % 4
                    pe.wait_ge(k_by_act, b * KA + 6 * qd + (4 if s < TPB else 6))
                    pe.wait_ge(sub_done, b * (2 * TPB) + s + 1)
                    src = kT[qd % 2] if s < TPB else qT[:, qd]
                    for c in range(DC):
                        last = mm(pW[s % 2][:, c * 512:(c + 1) * 512], src[:, c, f * P:(f + 1) * P], FM[:, :], start=True, stop=True)
                    last.then_inc(w_done, 1)

                def add_kv(s):
                    qd, f = s // 4, s % 4
                    pe.wait_ge(kf_ready, b * TPB + s + 1)
                    pe.wait_ge(k_by_dve, b * KD + 2 * qd + 2)
                    for blk in range(2):
                        for g in range(2):
                            for j in range(4):
                                h = 8 * blk + 2 * j + g
                                last = mm(pKV[32 * j:32 * j + 32, (2 * blk + g) * M:(2 * blk + g + 1) * M],
                                          vx[qd % 2][:, f, h, :], ft[s % 4][:, h * M:(h + 1) * M],
                                          start=False, stop=True, skip_group_check=True)
                    last.then_inc(ft_used, 1)

                def make_q(unit):
                    kind, x, h = unit
                    n = q_units.index(unit)
                    out = R[n % 4]
                    if n >= 4:
                        by_act, count = q_emptied(q_units[n - 4])
                        pe.wait_ge(*((q_by_act, b * QA + count + 1) if by_act else (q_by_dve, b * QD + count + 1)))
                    elif n == 3:
                        pe.wait_ge(kv_built, b + 1)
                    if kind in ("Ea", "Eb"):
                        if kind == "Ea":
                            pe.wait_ge(exp_done, b * (2 * TPB) + TPB + x + 1)
                        for c in range(4):
                            k = c + (4 if kind == "Eb" else 0)
                            last = nc.tensor.transpose(out[:, c * P:(c + 1) * P], ft[x % 4][:, k * P:(k + 1) * P], ident[:, :])
                        last.then_inc(q_unit, 1)
                    elif kind in ("D", "N"):
                        pe.wait_ge(q_by_act, b * QA + q_emptied(("Ea", 4 * x + 3, 0))[1] + 1)
                        pe.wait_ge(q_by_dve, b * QD + q_emptied(("Eb", 4 * x + 3, 0))[1] + 1)
                        for j in range(4):
                            c = 4 * h + j
                            last = mm(out[32 * j:32 * j + 32, :], (NU if kind == "N" else DE)[:, c, :], FT[x % 2][:, c, :], start=True, stop=True)
                        last.then_inc(q_unit, 1)
                    else:
                        pe.wait_ge(q_by_dve, b * QD + q_emptied(("N", x, 1))[1] + 1)
                        for w in range(2):
                            f = 2 * h + w
                            for c in range(DC):
                                last = mm(out[:, w * D:(w + 1) * D], oT[x % 2][:, c, f * P:(f + 1) * P], PW[:, c, :],
                                          start=(c == 0), stop=(c == DC - 1))
                        last.then_inc(q_unit, 1)

                pe.wait_ge(q_by_act, b * QA + 1)
                pe.wait_ge(q_by_dve, b * QD + 1)
                mm(pKV, zeros[:, 0:P], zeros[:, :], start=True, stop=True)
                for n in range(8):
                    make_k(n)
                for s in range(LAST_SLOT + 1):
                    if s < 2 * TPB:
                        exponents(s)
                    nxt = (s // 4 + 1) * 8 + s % 4 * 2
                    if nxt < KU:
                        make_k(nxt)
                        make_k(nxt + 1)
                    if 2 <= s < TPB + 2:
                        add_kv(s - 2)
                    if s == TPB + 2:
                        pe.wait_ge(kv_saved, b + 1)
                        pe.wait_ge(k_by_act, b * KA + KA)
                        pe.wait_ge(k_by_dve, b * KD + KD)
                        for h in range(2):
                            last = nc.tensor.transpose(R[3][:, h * P:(h + 1) * P], kvs[:, h * P:(h + 1) * P], ident[:, :])
                        last.then_inc(kv_turned, 1)
                    for unit in q_slot.get(s, []):
                        make_q(unit)
    m.clear()


def soft_mixture(nc, mem, io, keep, st):
    X, mean, rstd, ident = keep["X"], keep["mean"], keep["rstd"], keep["ident"]
    QT = TPB // 4
    NP = E0 // 2
    gam, bet = mem.sb("gamma", [P, D]), mem.sb("beta", [P, D])
    scol = mem.sb("scale", [P, 1])
    mu = mem.sb("mu", [P, DC, NS])
    ones = mem.sb("ones", [P, P])
    w1 = mem.sb("w1", [P, DC, E0, HID])
    w2 = mem.sb("w2", [P, NP, D])
    b1 = mem.sb("b1", [P, NP])
    b2 = mem.sb("b2", [E0, D])
    pick = mem.sb("pick", [E0, NS])
    XN = mem.sb("XN", [P, NT, D + 2])
    ss, rn = mem.sb("ss", [P, NT]), mem.sb("rn", [P, NT])
    L = mem.sb("L", [P, TPB, NS])
    cm, mrow = mem.sb("cm", [P, NS]), mem.sb("mrow", [P, NS])
    ccol, dg = mem.sb("ccol", [P, 2]), mem.sb("dg", [P, 2, P])
    nrm = mem.sb("nrm", [P, TPB])
    rs, rr = mem.sb("rs", [P, NT]), mem.sb("rr", [P, NT])
    xnT = [mem.sb(f"xnT{f}", [P, DC, P]) for f in range(4)]
    Ed = [mem.sb(f"Ed{u}", [P, 4, NS]) for u in range(2)]
    si, siT = mem.sb("si", [P, 2, D]), mem.sb("siT", [P, DC, NS])
    rsi = mem.sb("rsi", [P, 2])
    sq, ty, tz = siT, cm, mrow
    Hp = mem.sb("Hp", [P, NP, P])
    SO = mem.sb("SO", [P, 2, D])
    C = [mem.sb(f"C{f}", [P, NS]) for f in range(4)]
    loads = mem.sem("loads")

    made, ss_ready, root_ready, sumd = (mem.sem(n) for n in ("made", "ss_ready", "root_ready", "sumd"))
    with ExitStack() as sub:
        m = Memory(nc, sub, "sm0")
        pSS = m.ps("pSS", [P, NS])
        block = sub.enter_context(nc.Block())

        @block.sync
        def _(sp):
            n = 0
            for dst, src in ((mu[:, :, :], io["mu"].rearrange("(c p) n -> p c n", p=P)),
                             (gam[:, :], io["gamma"].partition_broadcast(P)),
                             (bet[:, :], io["beta"].partition_broadcast(P)),
                             (scol[:, :], io["scale"].partition_broadcast(P)),
                             (w1[:, 0, :, :], io["w1"][:, 0:P, :].rearrange("e p h -> p e h")),
                             (w1[:, 1, :, :], io["w1"][:, P:D, :].rearrange("e p h -> p e h")),
                             (w2[0:HID, :, :], io["w2"].rearrange("(k a) h d -> a h k d", a=2)[0]),
                             (w2[HID:P, :, :], io["w2"].rearrange("(k a) h d -> a h k d", a=2)[1]),
                             (b1[0:HID, :], io["b1"].rearrange("(k a) h -> a h k", a=2)[0]),
                             (b1[HID:P, :], io["b1"].rearrange("(k a) h -> a h k", a=2)[1]),
                             (b2[:, :], io["b2"])):
                with nc.allow_non_contiguous_dma(reason="a bias as columns, once"):
                    sp.dma_start(dst, src).then_inc(loads, 16)
                n += 16
                sp.wait_ge(loads, n)

        @block.gpsimd
        def _(pool):
            nc.gpsimd.memset(pick[:, :], 1.0).then_inc(made, 1)
            pool.wait_ge(made, 1)
            nc.gpsimd.affine_select(out=pick[:, :], in_=pick[:, :], compare_op=ALU.is_ge, fill=0.0,
                                    base=0, pattern=[[1, NS]], channel_multiplier=-S0).then_inc(made, 1)
            pool.wait_ge(made, 2)
            nc.gpsimd.affine_select(out=pick[:, :], in_=pick[:, :], compare_op=ALU.is_ge, fill=0.0,
                                    base=S0 - 1, pattern=[[-1, NS]], channel_multiplier=S0)

        @block.vector
        def _(dve):
            v = nc.vector
            v.memset(ones[:, :], 1.0)
            v.memset(Hp[:, :, :], 0.0)
            v.memset(XN[:, :, D:D + 2], 1.0)
            dve.wait_ge(loads, 16)
            v.tensor_tensor(sq[:, :, :], mu[:, :, :], mu[:, :, :], ALU.mult).then_inc(ss_ready, 1)
            dve.wait_ge(sumd, 1)
            v.tensor_scalar(ty[:, :], pSS[:, :], 1e-24, None, ALU.max).then_inc(ss_ready, 1)
            dve.wait_ge(root_ready, 1)
            v.reciprocal(tz[:, :], sq[:, 0, :])
            dve.drain()
            v.tensor_tensor(sq[:, 0, :], tz[:, :], tz[:, :], ALU.mult)
            dve.drain()
            v.tensor_tensor(sq[:, 0, :], sq[:, 0, :], ty[:, :], ALU.mult)
            dve.drain()
            v.tensor_scalar(sq[:, 0, :], sq[:, 0, :], -0.5, 1.5, ALU.mult, ALU.add)
            dve.drain()
            v.tensor_tensor(tz[:, :], tz[:, :], sq[:, 0, :], ALU.mult)
            dve.drain()
            v.tensor_tensor(mu[:, :, :], mu[:, :, :], tz[:, :].unsqueeze(1).broadcast_to([P, DC, NS]), ALU.mult)

        @block.scalar
        def _(act):
            act.wait_ge(ss_ready, 2)
            nc.scalar.activation(sq[:, 0, :], ty[:, :], ACT.Sqrt).then_inc(root_ready, 1)

        @block.tensor
        def _(pe):
            pe.wait_ge(ss_ready, 1)
            for c in range(DC):
                last = nc.tensor.matmul(pSS[:, :], ones[:, :], sq[:, c, :], start=(c == 0), stop=(c == DC - 1))
            last.then_inc(sumd, 1)

    xn_ready, sqd, nroot, ssr = (mem.sem(n) for n in ("xn_ready", "sqd", "nroot", "ssr"))
    with ExitStack() as sub:
        block = sub.enter_context(nc.Block())

        @block.vector
        def _(dve):
            v = nc.vector
            with dve.Fori(0, NT // 4) as q:
                for j in range(4):
                    v.tensor_scalar(XN[:, ds(q * 4 + j, 1), 0:D], X[:, ds(q * 4 + j, 1), :], mean[:, ds(q * 4 + j, 1)],
                                    rstd[:, ds(q * 4 + j, 1)], ALU.subtract, ALU.mult)
                dve.drain()
                v.tensor_tensor(XN[:, ds(q * 4, 4), 0:D], XN[:, ds(q * 4, 4), 0:D],
                                gam[:, :].unsqueeze(1).broadcast_to([P, 4, D]), ALU.mult)
                dve.drain()
                v.tensor_tensor(XN[:, ds(q * 4, 4), 0:D], XN[:, ds(q * 4, 4), 0:D],
                                bet[:, :].unsqueeze(1).broadcast_to([P, 4, D]), ALU.add).then_inc(xn_ready, 1)
            dve.wait_ge(sqd, NT)
            v.tensor_scalar(ss[:, :], ss[:, :], 1e-24, None, ALU.max).then_inc(ssr, 1)
            dve.wait_ge(nroot, 1)
            v.reciprocal(rn[:, :], rs[:, :])
            dve.drain()
            v.tensor_tensor(rs[:, :], rn[:, :], rn[:, :], ALU.mult)
            dve.drain()
            v.tensor_tensor(rs[:, :], rs[:, :], ss[:, :], ALU.mult)
            dve.drain()
            v.tensor_scalar(rs[:, :], rs[:, :], -0.5, 1.5, ALU.mult, ALU.add)
            dve.drain()
            v.tensor_tensor(rn[:, :], rn[:, :], rs[:, :], ALU.mult)
            dve.drain()
            v.tensor_scalar(rn[:, :], rn[:, :], scol[:, 0:1], None, ALU.mult)

        @block.scalar
        def _(act):
            with act.Fori(0, NT // 4) as q:
                act.drain()
                act.wait_ge(xn_ready, q + 1)
                for j in range(4):
                    nc.scalar.activation(C[j][:, :], XN[:, ds(q * 4 + j, 1), 0:D], ACT.Square,
                                         accum_out=ss[:, ds(q * 4 + j, 1)]).then_inc(sqd, 1)
            act.wait_ge(ssr, 1)
            nc.scalar.activation(rs[:, :], ss[:, :], ACT.Sqrt).then_inc(nroot, 1)

    with ExitStack() as sub:
        m = Memory(nc, sub, "sm2")
        xs_ready, seen = m.sem("xs_ready"), m.sem("seen")
        XS = [m.sb(f"XS{f}", [P, D]) for f in range(4)]
        trB, xnT_ready, lgB, L_ready = (m.sem(n) for n in ("trB", "xnT_ready", "lgB", "L_ready"))
        cm_ready, cmT, dg_ready, mr_ready = (m.sem(n) for n in ("cm_ready", "cmT", "dg_ready", "mr_ready"))
        sub_done, ed_ready, ed_used = (m.sem(n) for n in ("sub_done", "ed_ready", "ed_used"))
        si_ready, siT_done, siT_ready, h_done, hp_ready, so_done, so_ready = (m.sem(n) for n in (
            "si_ready", "siT_done", "siT_ready", "h_done", "hp_ready", "so_done", "so_ready"))
        C_ready, trD, CT_ready, mmD, x_ready = (m.sem(n) for n in ("C_ready", "trD", "CT_ready", "mmD", "x_ready"))
        pT = [m.ps(f"pT{u}", [P, DC, P]) for u in range(2)]
        pL = [m.ps(f"pL{u}", [P, 2, NS]) for u in range(2)]
        pA = [m.ps(f"pA{h}", [P, 512]) for h in range(2)]
        pM = m.ps("pM", [P, 2, NS])
        pH = m.ps("pH", [P, NP, S0])
        block = sub.enter_context(nc.Block())

        @block.vector
        def _(dve):
            v = nc.vector
            dve.sem_inc(L_ready, 2)
            dve.sem_inc(x_ready, 2)
            with dve.Fori(0, B) as b:
                v.memset(cm[:, :], -3.0e38)

                def logits(i, k):
                    for u in range(2):
                        t = b * TPB + i * 2 + u
                        dve.wait_ge(lgB, t + 5)
                        v.tensor_scalar(L[:, ds(i * 2 + u, 1), :], pL[u][:, 0, :], rn[:, ds(t, 1)], None,
                                        ALU.mult).then_inc(L_ready, 1)
                        dve.drain()
                        v.tensor_tensor(cm[:, :], cm[:, :], L[:, ds(i * 2 + u, 1), :].rearrange("p a n -> p (a n)"), ALU.max)
                dve.drain()
                in_pairs(dve, lambda i, k: None, logits)
                dve.drain().then_inc(cm_ready, 1)
                v.tensor_reduce(nrm[:, :], L[:, :, :], AX, ALU.max, negate=True)
                dve.wait_ge(cmT, b + 1)
                v.tensor_reduce(ccol[:, :], pM[:, 0, :].rearrange("p (h q) -> p h q", h=2), AX, ALU.max)
                dve.drain()
                for h in range(2):
                    last = v.tensor_scalar(dg[:, h, :], ident[:, :], ccol[:, h:h + 1], None, ALU.mult)
                last.then_inc(dg_ready, 1)
                dve.wait_ge(mr_ready, b + 1)
                v.tensor_copy(mrow[:, :], pM[:, 1, :])
                dve.drain()
                for q in range(QT):
                    dve.wait_ge(ed_used, b * QT + q + 1)
                    v.tensor_tensor(Ed[q % 2][:, :, :], L[:, q * 4:q * 4 + 4, :],
                                    mrow[:, :].unsqueeze(1).broadcast_to([P, 4, NS]), ALU.subtract).then_inc(sub_done, 1)
                dve.wait_ge(ed_used, b * QT + QT + 2)
                for h in range(2):
                    v.reciprocal(rsi[:, h:h + 1], pA[h][:, D:D + 1])
                dve.drain()
                for h in range(2):
                    last = v.tensor_scalar(si[:, h, :], pA[h][:, 0:D], rsi[:, h:h + 1], None, ALU.mult)
                last.then_inc(si_ready, 1)
                dve.wait_ge(so_done, b + 1)
                for h in range(2):
                    last = v.tensor_copy(SO[:, h, :], pA[h][:, 0:D])
                last.then_inc(so_ready, 1)

                def add(i, k):
                    for u in range(2):
                        t = b * TPB + i * 2 + u
                        dve.wait_ge(mmD, t + 5)
                        v.reciprocal(rr[:, ds(t, 1)], rs[:, ds(t, 1)])
                        dve.drain()
                        v.scalar_tensor_tensor(X[:, ds(t, 1), :], pL[u][:, 0, :].unsqueeze(1), rr[:, ds(t, 1)],
                                               X[:, ds(t, 1), :], ALU.mult, ALU.add).then_inc(x_ready, 1)
                        dve.drain()
                        v.bn_stats(st[:, ds(t, 1), :], X[:, ds(t, 1), :])
                in_pairs(dve, lambda i, k: None, add)

        @block.scalar
        def _(act):
            s = nc.scalar
            act.sem_inc(xnT_ready, 2)
            act.sem_inc(CT_ready, 2)
            with act.Fori(0, B) as b:
                def turn_in(i, k):
                    for u in range(2):
                        t = b * TPB + i * 2 + u
                        act.wait_ge(trB, t + 5)
                        act.wait_ge(lgB, t + 1)
                        s.activation(xnT[2 * k + u][:, :, :], pT[u][:, :, :], ACT.Copy).then_inc(xnT_ready, 1)
                in_pairs(act, turn_in, lambda i, k: None)
                for q in range(QT):
                    act.wait_ge(sub_done, b * QT + q + 1)
                    s.activation(Ed[q % 2][:, :, :], Ed[q % 2][:, :, :], ACT.Exp).then_inc(ed_ready, 1)
                act.wait_ge(siT_done, b + 1)
                s.activation(siT[:, :, :], pL[0][:, :, :], ACT.Copy).then_inc(siT_ready, 1)
                act.wait_ge(h_done, b + 1)
                for e in range(E0):
                    k, a = e // 2, e % 2
                    col = (e % 8) * S0
                    last = s.activation(Hp[a * HID:(a + 1) * HID, k, col:col + S0], pH[a * HID:(a + 1) * HID, k, :],
                                        ACT.Gelu, bias=b1[a * HID:(a + 1) * HID, k:k + 1])
                last.then_inc(hp_ready, 1)

                def mix(i, k):
                    for u in range(2):
                        t = b * TPB + i * 2 + u
                        act.wait_ge(trD, t + 1)
                        s.activation(C[2 * k + u][:, :].unsqueeze(1), L[:, ds(i * 2 + u, 1), :], ACT.Exp,
                                     bias=nrm[:, ds(i * 2 + u, 1)], accum_out=rs[:, ds(t, 1)]).then_inc(C_ready, 1)

                def turn_out(i, k):
                    for u in range(2):
                        t = b * TPB + i * 2 + u
                        act.wait_ge(trD, t + 5)
                        act.wait_ge(mmD, t + 1)
                        s.activation(xnT[2 * k + u][:, :, :], pT[u][:, :, :], ACT.Copy).then_inc(CT_ready, 1)
                in_pairs(act, mix, turn_out)

        @block.gpsimd
        def _(pool):
            with pool.Fori(0, NT // 4) as q:
                for f in range(4):
                    pool.wait_ge(trB, q * 4 + f + 1)
                    pool.sem_inc(seen, 1)
                    nc.gpsimd.tensor_copy(XS[f][:, :].unsqueeze(1), XN[:, ds(q * 4 + f, 1), 0:D]).then_inc(xs_ready, 1)

        @block.tensor
        def _(pe):
            mm = nc.tensor.matmul
            for sem_, n in ((trB, 4), (lgB, 4), (ed_used, 2), (trD, 4), (mmD, 4)):
                pe.sem_inc(sem_, n)
            with pe.Fori(0, B) as b:
                pe.wait_ge(x_ready, b * TPB + 2)

                def turn(i, k):
                    for u in range(2):
                        t = b * TPB + i * 2 + u
                        pe.wait_ge(xs_ready, t + 1)
                        pe.wait_ge(xnT_ready, t + 1)
                        for c in range(DC):
                            last = nc.tensor.transpose(pT[u][:, c, :], XS[2 * k + u][:, c * P:(c + 1) * P], ident[:, :])
                        last.then_inc(trB, 1)

                def logits(i, k):
                    for u in range(2):
                        t = b * TPB + i * 2 + u
                        pe.wait_ge(xnT_ready, t + 3)
                        pe.wait_ge(L_ready, t + 1)
                        for c in range(DC):
                            last = mm(pL[u][:, 0, :], xnT[2 * k + u][:, c, :], mu[:, c, :], start=(c == 0), stop=(c == DC - 1))
                        last.then_inc(lgB, 1)
                in_pairs(pe, turn, logits)

                pe.wait_ge(cm_ready, b + 1)
                for h in range(2):
                    last = nc.tensor.transpose(pM[:, 0, h * P:(h + 1) * P], cm[:, h * P:(h + 1) * P], ident[:, :])
                last.then_inc(cmT, 1)
                pe.wait_ge(dg_ready, b + 1)
                for h in range(2):
                    last = mm(pM[:, 1, h * P:(h + 1) * P], ones[:, :], dg[:, h, :], start=True, stop=True)
                last.then_inc(mr_ready, 1)
                for q in range(QT):
                    pe.wait_ge(ed_ready, b * QT + q + 1)
                    for j in range(4):
                        for h in range(2):
                            first, end = q + j == 0, q * 4 + j == TPB - 1
                            last = mm(pA[h][:, 0:D + 1].unsqueeze(1), Ed[q % 2][:, j, h * P:(h + 1) * P],
                                      XN[:, ds(b * TPB + q * 4 + j, 1), 0:D + 1], start=first, stop=end)
                    last.then_inc(ed_used, 1)
                pe.wait_ge(si_ready, b + 1)
                for h in range(2):
                    for c in range(DC):
                        last = nc.tensor.transpose(pL[0][:, c, h * P:(h + 1) * P], si[:, h, c * P:(c + 1) * P], ident[:, :])
                last.then_inc(siT_done, 1)
                pe.wait_ge(siT_ready, b + 1)
                for e in range(E0):
                    k, a = e // 2, e % 2
                    for c in range(DC):
                        last = mm(pH[a * HID:(a + 1) * HID, k, :], w1[:, c, e, :], siT[:, c, e * S0:(e + 1) * S0],
                                  start=(c == 0), stop=(c == DC - 1))
                last.then_inc(h_done, 1)
                pe.wait_ge(hp_ready, b + 1)
                for h in range(2):
                    for k in range(4):
                        mm(pA[h][:, 0:D], Hp[:, h * 4 + k, :], w2[:, h * 4 + k, :], start=(k == 0), stop=False)
                    last = mm(pA[h][:, 0:D], pick[:, h * P:(h + 1) * P], b2[:, :], start=False, stop=True)
                last.then_inc(so_done, 1)

                def turn_mix(i, k):
                    for u in range(2):
                        t = b * TPB + i * 2 + u
                        pe.wait_ge(C_ready, t + 1)
                        pe.wait_ge(CT_ready, t + 1)
                        for c in range(2):
                            last = nc.tensor.transpose(pT[u][:, c, :], C[2 * k + u][:, c * P:(c + 1) * P], ident[:, :])
                        last.then_inc(trD, 1)

                def mix(i, k):
                    for u in range(2):
                        t = b * TPB + i * 2 + u
                        pe.wait_ge(CT_ready, t + 3)
                        pe.wait_ge(so_ready, b + 1)
                        pe.wait_ge(x_ready, t + 1)
                        for c in range(2):
                            last = mm(pL[u][:, 0, :], xnT[2 * k + u][:, c, :], SO[:, c, :], start=(c == 0), stop=(c == 1))
                        last.then_inc(mmD, 1)
                in_pairs(pe, turn_mix, mix)
    m.clear()


def project_qkv(nc, mem, io, keep, nn):
    X, mean, rstd, ident = keep["X"], keep["mean"], keep["rstd"], keep["ident"]
    W = mem.sb("W", [P, DC, 3 * D])
    cos, sin = mem.sb("cos", [P, NT, HD // 2]), mem.sb("sin", [P, NT, HD // 2])
    z = [mem.sb(f"z{f}", [P, D]) for f in range(4)]
    zT = [mem.sb(f"zT{f}", [P, DC, P]) for f in range(4)]
    xc = [mem.sb(f"xc{u}", [P, 2 * D]) for u in range(2)]
    xs = [mem.sb(f"xs{u}", [P, 2 * D]) for u in range(2)]
    rqk = [mem.sb(f"rqk{f}", [P, G, 2, 4 * HD]) for f in range(4)]
    rv = [mem.sb(f"rv{f}", [P, G, 4, VW]) for f in range(4)]
    sq = [mem.sb(f"sq{f}", [P, 3, D]) for f in range(4)]
    z_ready, turned, zT_ready, qk_done, v_done, rot_ready, v_ready, rec_ready, sq_ready, own_ready, summed = (mem.sem(n) for n in (
        "z_ready", "turned", "zT_ready", "qk_done", "v_done", "rot_ready", "v_ready", "rec_ready", "sq_ready", "own_ready", "summed"))
    seen = mem.sem("seen")
    w_loaded = mem.sem("w_loaded")
    qk_stored = [mem.sem(f"qk_stored{f}") for f in range(4)]
    v_stored = [mem.sem(f"v_stored{f}") for f in range(4)]
    pT = [mem.ps(f"pT{u}", [P, DC, P]) for u in range(2)]
    pQK = [mem.ps(f"pQK{u}", [P, 2 * D]) for u in range(2)]
    pV = [mem.ps(f"pV{u}", [P, D]) for u in range(2)]
    qk_d = keep["qk"].rearrange("(b g) t p e -> b g t p e", g=G)
    v_d = keep["v"].rearrange("(b g) t p e -> b g t p e", g=G)
    with nc.Block() as block:
        @block.sync
        def _(sp):
            n = 0
            for c in range(3):
                sp.dma_start(W[:, :, c * D:(c + 1) * D],
                             io[("WqT", "WkT", "WvT")[c]].rearrange("(c p) n -> p c n", p=P)).then_inc(w_loaded, 16)
                n += 16
                sp.wait_ge(w_loaded, n)
            for b in range(B):
                for dst, src in ((cos, io["cos"]), (sin, io["sin"])):
                    sp.dma_start(dst[:, b * TPB:(b + 1) * TPB, :], src.rearrange("(t p) j -> p t j", p=P)).then_inc(w_loaded, 16)
                    n += 16
                    sp.wait_ge(w_loaded, n)
            for f in range(4):
                sp.sem_inc(qk_stored[f], 16)
                sp.sem_inc(v_stored[f], 16)
            with sp.Fori(0, B) as b:
                with sp.Fori(0, TPB // 4) as q:
                    for f in range(4):
                        t = b * TPB + q * 4 + f
                        for ready, buf, dram, done in ((rec_ready, rqk[f], qk_d, qk_stored[f]), (v_ready, rv[f], v_d, v_stored[f])):
                            sp.wait_ge(ready, t + 3)
                            sp.dma_start(dram[ds(b, 1), :, ds(q * 4 + f, 1), :, :].rearrange("b g t p e -> p (b g t) e"),
                                         buf[:, :, :, :].rearrange("p g a e -> p g (a e)")).then_inc(done, 16)
            for f in range(4):
                sp.wait_ge(qk_stored[f], 16 + 16 * (NT // 4))
                sp.wait_ge(v_stored[f], 16 + 16 * (NT // 4))

        @block.vector
        def _(dve):
            v = nc.vector
            for f in range(4):
                v.memset(rv[f][:, :, :, :], 0.0)
            dve.drain()
            for f in range(4):
                v.memset(rv[f][:, :, :, HD:HD + 1], 1.0)
            dve.drain().then_inc(z_ready, 1)
            dve.sem_inc(rot_ready, 2)
            dve.wait_ge(w_loaded, 16 * 11)

            def normalise(t, f):
                dve.wait_ge(turned, t + 1)
                v.tensor_scalar(z[f][:, :].unsqueeze(1), X[:, ds(t, 1), :], mean[:, ds(t, 1)], rstd[:, ds(t, 1)],
                                ALU.subtract, ALU.mult).then_inc(z_ready, 1)

            def rotate(t, f):
                u = f % 2
                src = pQK[u][:, :].rearrange("p (h i a) -> p h i a", h=2 * H, a=2)
                dve.wait_ge(qk_done, t + 1)
                for table, dst in ((cos, xc), (sin, xs)):
                    tab = table[:, ds(t, 1), :].unsqueeze(3).broadcast_to([P, 2 * H, HD // 2, 2])
                    last = v.tensor_tensor(dst[u][:, :].rearrange("p (h i a) -> p h i a", h=2 * H, a=2), src, tab, ALU.mult)
                last.then_inc(rot_ready, 1)
            dve.sem_inc(summed, 4)

            def sums(t, f):
                dve.wait_ge(sq_ready, t + 1)
                dve.wait_ge(own_ready, t + 1)
                v.tensor_reduce(nn[:, ds(t, 1), :], sq[f][:, :, :].rearrange("p a (h e) -> p (a h) e", h=H), AX, ALU.add)\
                 .then_inc(summed, 1)

            def quad(q, sums_too):
                for f in range(4):
                    normalise(q * 4 + f, f)
                    if sums_too:
                        sums(q * 4 + f - 4, f)
                for f in range(4):
                    dve.wait_ge(rec_ready, q * 4 + f + 1)
                    rotate(q * 4 + f, f)
            quad(0, False)
            with dve.Fori(1, NT // 4) as q:
                quad(q, True)
            for f in range(4):
                sums(NT - 4 + f, f)

        @block.gpsimd
        def _(pool):
            pool.sem_inc(rec_ready, 2)
            with pool.Fori(0, NT // 4) as q:
                for f in range(4):
                    u = f % 2
                    pool.wait_ge(rot_ready, q * 4 + f + 3)
                    pool.wait_ge(qk_stored[f], q * 16 + 16)
                    pool.sem_inc(seen, 1)
                    c4 = xc[u][:, :].rearrange("p (q g r a) -> p q g r a", q=2, g=G, a=2)
                    s4 = xs[u][:, :].rearrange("p (q g r a) -> p q g r a", q=2, g=G, a=2)
                    out = rqk[f][:, :, :, :].rearrange("p g q (r a) -> p q g r a", a=2)
                    nc.gpsimd.tensor_tensor(out[:, :, :, :, 0], c4[:, :, :, :, 0], s4[:, :, :, :, 1], ALU.subtract)
                    nc.gpsimd.tensor_tensor(out[:, :, :, :, 1], s4[:, :, :, :, 0], c4[:, :, :, :, 1], ALU.add).then_inc(rec_ready, 1)
                    pool.wait_ge(summed, q * 4 + f + 1)
                    pool.wait_ge(rec_ready, q * 4 + f + 3)
                    pool.sem_inc(seen, 1)
                    nc.gpsimd.tensor_tensor(sq[f][:, 2, :].rearrange("p (g e) -> p g e", g=G), rqk[f][:, :, 0, :],
                                            rqk[f][:, :, 1, :], ALU.mult).then_inc(own_ready, 1)

        @block.scalar
        def _(act):
            act.sem_inc(zT_ready, 2)
            act.sem_inc(v_ready, 2)
            with act.Fori(0, NT // 4) as q:
                def turn(f):
                    act.wait_ge(turned, q * 4 + f + 5)
                    nc.scalar.activation(zT[f][:, :, :], pT[f % 2][:, :, :], ACT.Copy).then_inc(zT_ready, 1)

                def value(f):
                    act.wait_ge(v_done, q * 4 + f + 1)
                    act.wait_ge(v_stored[f], q * 16 + 16)
                    nc.scalar.activation(rv[f][:, :, :, 0:HD].rearrange("p g h e -> p (g h) e"),
                                         pV[f % 2][:, :].rearrange("p (h e) -> p h e", h=H), ACT.Copy).then_inc(v_ready, 1)
                def square(f):
                    act.wait_ge(rec_ready, q * 4 + f + 3)
                    act.wait_ge(summed, q * 4 + f + 1)
                    nc.scalar.activation(sq[f][:, 0:2, :].rearrange("p q (g e) -> p g q e", g=G), rqk[f][:, :, :, :], ACT.Square).then_inc(sq_ready, 1)
                for f in (0, 1, 2, 3):
                    turn(f)
                    if f:
                        value(f - 1)
                value(3)
                for f in range(4):
                    square(f)

        @block.tensor
        def _(pe):
            mm = nc.tensor.matmul
            pe.sem_inc(turned, 4)
            pe.wait_ge(w_loaded, 48)
            with pe.Fori(0, NT // 4) as q:
                def turn(f):
                    pe.wait_ge(z_ready, q * 4 + f + 2)
                    pe.wait_ge(zT_ready, q * 4 + f + 1)
                    for c in range(DC):
                        last = nc.tensor.transpose(pT[f % 2][:, c, :], z[f][:, c * P:(c + 1) * P], ident[:, :])
                    last.then_inc(turned, 1)

                def project(f):
                    pe.wait_ge(zT_ready, q * 4 + f + 3)
                    pe.wait_ge(rot_ready, q * 4 + f + 1)
                    for c in range(DC):
                        last = mm(pQK[f % 2][:, :], zT[f][:, c, :], W[:, c, 0:2 * D], start=(c == 0), stop=(c == DC - 1))
                    last.then_inc(qk_done, 1)
                    pe.wait_ge(v_ready, q * 4 + f + 1)
                    for c in range(DC):
                        last = mm(pV[f % 2][:, :], zT[f][:, c, :], W[:, c, 2 * D:3 * D], start=(c == 0), stop=(c == DC - 1))
                    last.then_inc(v_done, 1)
                for f in range(4):
                    turn(f)
                    if f:
                        project(f - 1)
                project(3)


ROOM = 55.0 / HD ** -0.5
LOOSE = 124.0 / HD ** -0.5


def bound_scores(nc, mem, io, keep, nn):
    ident, nmax, need_max = keep["ident"], keep["nmax"], keep["need_max"]
    BH = B * H
    km, kcol, dg = mem.sb("km", [P, BH]), mem.sb("kcol", [BH, 1]), mem.sb("dg", [BH, BH])
    ones = mem.sb("ones", [BH, P])
    bd = mem.sb("bd", [P, NT, H])
    gap, worst, over = mem.sb("gap", [P, 1]), mem.sb("worst", [1, 1]), mem.sb("over", [1, 1])
    km_ready, km_turned, dg_ready, spread, squared, rooted, gap_ready, gap_turned = (mem.sem(n) for n in (
        "km_ready", "km_turned", "dg_ready", "spread", "squared", "rooted", "gap_ready", "gap_turned"))
    pK, pM, pG = mem.ps("pK", [BH, P]), mem.ps("pM", [P, BH]), mem.ps("pG", [1, P])
    q2, k2, own = (nn[:, :, n * H:(n + 1) * H] for n in range(3))
    with nc.Block() as block:
        @block.vector
        def _(dve):
            v = nc.vector
            v.memset(ones[:, :], 1.0)
            for b in range(B):
                v.tensor_reduce(km[:, b * H:(b + 1) * H], k2[:, b * TPB:(b + 1) * TPB, :].rearrange("p t h -> p h t"), AX, ALU.max)
            dve.drain().then_inc(km_ready, 1)
            dve.wait_ge(km_turned, 1)
            v.tensor_reduce(kcol[:, :], pK[:, :], AX, ALU.max)
            dve.drain()
            v.tensor_scalar(dg[:, :], ident[0:BH, 0:BH], kcol[:, 0:1], None, ALU.mult).then_inc(dg_ready, 1)
            dve.wait_ge(spread, 1)
            for b in range(B):
                last = v.tensor_tensor(bd[:, b * TPB:(b + 1) * TPB, :], q2[:, b * TPB:(b + 1) * TPB, :],
                                       pM[:, b * H:(b + 1) * H].unsqueeze(1).broadcast_to([P, TPB, H]), ALU.mult)
            last.then_inc(squared, 1)
            dve.wait_ge(rooted, 1)
            for b in range(B):
                for g in range(G):
                    v.tensor_scalar(nmax[:, b * G + g, :].rearrange("p (t h) -> p t h", h=4),
                                    bd[:, b * TPB:(b + 1) * TPB, g * 4:g * 4 + 4], -1.0, ROOM, ALU.mult, ALU.add)
            dve.drain()
            v.tensor_tensor(bd[:, :, :], bd[:, :, :], own, ALU.subtract)
            dve.drain()
            v.tensor_reduce(gap[:, :], bd[:, :, :].rearrange("p t h -> p (t h)"), AX, ALU.max).then_inc(gap_ready, 1)
            dve.wait_ge(gap_turned, 1)
            v.tensor_reduce(worst[:, :], pG[:, :], AX, ALU.max)
            dve.drain()
            v.tensor_scalar(over[:, :], worst[:, :], LOOSE, None, ALU.is_lt)
            dve.drain()
            v.tensor_scalar(over[:, :], over[:, :], -1.0, 1.0, ALU.mult, ALU.add)
            dve.drain()
            v.tensor_copy(need_max[:, :], over[:, :])

        @block.scalar
        def _(act):
            act.wait_ge(squared, 1)
            nc.scalar.activation(bd[:, :, :], bd[:, :, :], ACT.Sqrt).then_inc(rooted, 1)

        @block.tensor
        def _(pe):
            pe.wait_ge(km_ready, 1)
            nc.tensor.transpose(pK[:, :], km[:, :], ident[:, :]).then_inc(km_turned, 1)
            pe.wait_ge(dg_ready, 1)
            nc.tensor.matmul(pM[:, :], ones[:, :], dg[:, :], start=True, stop=True).then_inc(spread, 1)
            pe.wait_ge(gap_ready, 1)
            nc.tensor.transpose(pG[:, :], gap[:, :], ident[:, :]).then_inc(gap_turned, 1)


TERMS_Q = (0, 0, 0, 1, 1, 2)
TERMS_K = (0, 1, 2, 0, 1, 0)
KR = 6 * HD
KS = KR + 3


class Turner:

    def __init__(self, nc, m, keep, rqk, QT, KT, shifted, pG):
        self.nc, self.keep, self.rqk, self.dst, self.shifted = nc, keep, rqk, (QT, KT), shifted
        self.rep = [[m.sb(f"{x}r{w}", [P, 16, 100], bf16) for w in range(2)] for x in "qk"]
        self.hi, self.mid = m.sb("hi", [P, 4, P], bf16), m.sb("mid", [P, 4, P], bf16)
        self.r1 = m.sb("r1", [P, 4, P])
        self.sh, self.shr = m.sb("sh", [P, 3, 16], bf16), m.sb("shr", [P, 16])
        self.pG = pG
        self.split_done, self.turned, self.evicted = m.sem("split_done"), m.sem("group_turned"), m.sem("group_evicted")

    def begin_dve(self, dve):
        for w in range(2):
            self.nc.vector.memset(self.rep[0][w][:, :, KR:100], 0.0)
            self.nc.vector.memset(self.rep[1][w][:, :, KR:100], 1.0)
        dve.sem_inc(self.evicted, 1)

    def split(self, dve, n, qd):
        v, hi, mid, r1 = self.nc.vector, self.hi, self.mid, self.r1
        src = self.rqk[:, qd * 4:qd * 4 + 4, :]
        v.tensor_copy(hi[:, :, :], src)
        if self.shifted:
            cur = self.keep["nmax"][:, ds(n, 1), qd * 16:qd * 16 + 16]
            sh, shr = self.sh, self.shr
            v.tensor_copy(sh[:, 0:1, :], cur)
        dve.drain()
        v.tensor_tensor(r1[:, :, :], src, hi[:, :, :], ALU.subtract)
        if self.shifted:
            v.tensor_tensor(shr[:, :].unsqueeze(1), cur, sh[:, 0:1, :], ALU.subtract)
        dve.drain()
        v.tensor_copy(mid[:, :, :], r1[:, :, :])
        if self.shifted:
            v.tensor_copy(sh[:, 1, :], shr[:, :])
        dve.drain()
        v.tensor_tensor(r1[:, :, :], r1[:, :, :], mid[:, :, :], ALU.subtract)
        if self.shifted:
            v.tensor_tensor(sh[:, 2, :], shr[:, :], sh[:, 1, :], ALU.subtract)
        for x, terms in enumerate((TERMS_Q, TERMS_K)):
            rep = self.rep[x][qd % 2]
            for part, from_ in ((0, hi), (1, mid), (2, r1)):
                s = from_[:, :, x * 64:(x + 1) * 64].rearrange("p t (h e) -> p t h e", h=4)
                if part == 2:
                    dve.drain()
                for slot in [n for n, w in enumerate(terms) if w == part]:
                    d = rep[:, :, slot * HD:(slot + 1) * HD].rearrange("p (t h) e -> p t h e", t=4)
                    last = v.tensor_copy(d, s)
        if self.shifted:
            for n in range(3):
                last = v.tensor_copy(self.rep[0][qd % 2][:, :, KR + n:KR + n + 1], self.sh[:, n, :].unsqueeze(2))
        dve.drain().then_inc(self.split_done, 1)

    def turn(self, pe, n, qd, gi):
        x, half = gi % 2, gi // 2
        rows = 100 if self.shifted else KR
        pe.wait_ge(self.split_done, n * 4 + qd + 1)
        pe.wait_ge(self.evicted, n * 16 + qd * 4 + gi + 1)
        for h in range(4):
            for t in range(2):
                last = self.nc.tensor.transpose(self.pG[0:rows, h * 2 + t, :],
                                                self.rep[x][qd % 2][:, (half * 2 + t) * 4 + h, 0:rows],
                                                self.keep["identb"][:, :])
        last.then_inc(self.turned, 1)

    def evict(self, dve, n, qd, gi, par):
        x, half = gi % 2, gi // 2
        rows = 100 if self.shifted else KR
        col = (qd * 4 + half * 2) * P
        dve.wait_ge(self.turned, n * 16 + qd * 4 + gi + 1)
        self.nc.vector.tensor_copy(self.dst[x][par][0:rows, :, col:col + 2 * P],
                                   self.pG[0:rows, :, :].rearrange("p (h t) q -> p h (t q)", t=2)).then_inc(self.evicted, 1)


def row_maxima(nc, mem, io, keep):
    nmax, identb, need_max = keep["nmax"], keep["identb"], keep["need_max"]
    rqk = mem.sb("rqk", [P, TPB, P])
    QT, KT = [mem.sb("QT", [P, 4, N], bf16)], [mem.sb("KT", [P, 4, N], bf16)]
    mask = mem.sb("mask", [P, P], bf16)
    pm = mem.sb("pm", [P, TPB, 4, 2])
    T = Turner(nc, mem, keep, rqk, QT, KT, False, mem.ps("pG", [P, 8, P], bf16))
    made, loaded, scored, reduced, mx_done = (mem.sem(n) for n in ("made", "loaded", "scored", "reduced", "mx_done"))
    pS = [mem.ps(f"pS{s}", [P, 1024]) for s in range(3)]
    units = [(t, h, k) for t in range(TPB) for h in range(4) for k in range(1 + t // 8)]
    U = len(units)
    assert U % 3 == 0
    with nc.Block() as block:
        @block.gpsimd
        def _(pool):
            nc.gpsimd.memset(mask[:, :], 0.0).then_inc(made, 1)
            pool.wait_ge(made, 1)
            nc.gpsimd.affine_select(out=mask[:, :], in_=mask[:, :], compare_op=ALU.is_ge, fill=MASKED,
                                    base=0, pattern=[[-1, P]], channel_multiplier=1).then_inc(made, 1)

        @block.sync
        def _(sp):
            need = sp.value_load(need_max[0:1, 0:1], min_val=0, max_val=1)
            with sp.If(need > 0):
                with sp.Fori(0, B) as b:
                    for g in range(G):
                        n = b * G + g
                        sp.wait_ge(mx_done, n + 1)
                        for half in (slice(0, TPB // 2), slice(TPB // 2, TPB)):
                            sp.dma_start(rqk[:, half, :], keep["qk"][ds(n, 1), half, :, :].rearrange("i t p e -> p (i t) e")).then_inc(loaded, 16)

        @block.vector
        def _(dve):
            need = dve.value_load(need_max[0:1, 0:1], min_val=0, max_val=1)
            with dve.If(need > 0):
                v = nc.vector
                T.begin_dve(dve)
                dve.sem_inc(reduced, 3)
                dve.sem_inc(mx_done, 1)
                with dve.Fori(0, B) as b:
                    for g in range(G):
                        n = b * G + g
                        dve.wait_ge(loaded, n * 32 + 32)
                        for qd in range(4):
                            T.split(dve, n, qd)
                            for gi in range(4):
                                T.evict(dve, n, qd, gi, 0)
                        for i, (t, h, k) in enumerate(units):
                            width = min(1024, (t + 1) * P - k * 1024)
                            dve.wait_ge(scored, n * U + i + 1)
                            v.tensor_reduce(pm[:, t, h, k:k + 1], pS[i % 3][:, 0:width], AX, ALU.max).then_inc(reduced, 1)
                        dve.drain()
                        v.tensor_tensor(pm[:, 8:16, :, 0], pm[:, 8:16, :, 0], pm[:, 8:16, :, 1], ALU.max)
                        dve.drain()
                        v.tensor_scalar(nmax[:, ds(n, 1), :].rearrange("p i (t h) -> p (i t) h", h=4), pm[:, :, :, 0], -1.0, None, ALU.mult).then_inc(mx_done, 1)

        @block.tensor
        def _(pe):
            need = pe.value_load(need_max[0:1, 0:1], min_val=0, max_val=1)
            with pe.If(need > 0):
                pe.wait_ge(made, 2)
                with pe.Fori(0, B) as b:
                    for g in range(G):
                        n = b * G + g
                        for qd in range(4):
                            for gi in range(4):
                                T.turn(pe, n, qd, gi)
                        pe.wait_ge(T.evicted, n * 16 + 17)
                        for i, (t, h, k) in enumerate(units):
                            width = min(1024, (t + 1) * P - k * 1024)
                            pe.wait_ge(reduced, n * U + i + 1)
                            for c in range(0, width, 512):
                                w = min(512, width - c)
                                key = k * 1024 + c
                                diag = key + w == (t + 1) * P
                                last = nc.tensor.matmul(pS[i % 3][:, c:c + w], QT[0][0:KR, h, t * P:(t + 1) * P],
                                                        KT[0][0:KR, h, key:key + w], start=True, stop=not diag)
                                if diag:
                                    last = nc.tensor.matmul(pS[i % 3][:, c + w - P:c + w], identb[:, :], mask[:, :], start=False, stop=True)
                            last.then_inc(scored, 1)


def attention(nc, mem, io, keep):
    ident, identb = keep["ident"], keep["identb"]
    QC = N // 512
    STEPS = [(c, kb) for c in range(QC) for kb in range(4 * c + 4)]
    NST = len(STEPS)
    LAST = [STEPS.index((c, 4 * c + 3)) for c in range(QC)]
    UNITS, PLACE = [], {}
    for n, (c, kb) in enumerate(STEPS):
        width = 512 - max(0, kb - 4 * c) * P
        per = min(4, 1024 // width) if width <= 256 else 2
        for first in range(0, 4, per):
            for h in range(first, first + per):
                PLACE[n, h] = (len(UNITS), (h - first) * width // 512 if per == 4 else h - first, (h - first) * width % 512 if per == 4 else 0)
            UNITS.append((n, range(first, first + per), per * width // 512 if per == 4 else 2, 512 if per == 4 else width))
    NU = len(UNITS)
    assert NU % 12 == 0
    rqk = mem.sb("rqk", [P, TPB, P])
    V = [mem.sb(f"V{k}", [P, TPB, P]) for k in range(2)]
    QT = [mem.sb(f"QT{k}", [P, 4, N], bf16) for k in range(2)]
    KT = [mem.sb(f"KT{k}", [P, 4, N], bf16) for k in range(2)]
    PT = [mem.sb(f"PT{s}", [P, 2, 512]) for s in range(4)]
    mask = mem.sb("mask", [P, P], bf16)
    zero = mem.sb("zero", [P, D])
    zeroed = mem.sem("zeroed")
    OT = [mem.sb(f"OT{s}", [P, 512]) for s in range(2)]
    rc = mem.sb("rc", [P, 4, 4])
    ob = [mem.sb(f"ob{s}", [P, 4, 4, HD]) for s in range(2)]
    made, qk_loaded, scored, exp_done, pv_done, out_copied, out_turned, divided = (mem.sem(n) for n in (
        "made", "qk_loaded", "scored", "exp_done", "pv_done", "out_copied", "out_turned", "divided"))
    v_loaded = [mem.sem(f"v_loaded{k}") for k in range(2)]
    stored = [mem.sem(f"stored{s}") for s in range(2)]
    pS = [mem.ps(f"pS{s}", [P, 2, 512]) for s in range(3)]
    pO = mem.ps("pO", [P, 512])
    bank = mem.ps("bank", [P, 512])
    pY = bank[:, :].rearrange("p (q e) -> p q e", q=4)
    T = Turner(nc, mem, keep, rqk, QT, KT, True, bank[:, :].bitcast(bf16).rearrange("p (a e) -> p a e", a=8))
    NIT = B * G

    def iterations(eng, first, body):
        first()
        with eng.Fori(0, NIT // 2 - 1) as j:
            body(j * 2, 0, j, True)
            body(j * 2 + 1, 1, j, True)
        body(NIT - 2, 0, NIT // 2 - 1, True)
        body(NIT - 1, 1, NIT // 2 - 1, False)

    with nc.Block() as block:
        @block.gpsimd
        def _(pool):
            nc.gpsimd.memset(mask[:, :], 0.0).then_inc(made, 1)
            pool.wait_ge(made, 1)
            nc.gpsimd.affine_select(out=mask[:, :], in_=mask[:, :], compare_op=ALU.is_ge, fill=MASKED,
                                    base=0, pattern=[[1, P]], channel_multiplier=-1).then_inc(made, 1)
            nc.gpsimd.memset(zero[:, :], 0.0).then_inc(made, 1)
            pool.wait_ge(made, 3)
            rows = keep["xg"].rearrange("(q n p) d -> q p n d", n=20, p=P)
            for n in range(8):
                pool.dma_start(rows[n], zero[:, :].unsqueeze(1).broadcast_to([P, 20, D])).then_inc(zeroed, 16)
                pool.wait_ge(zeroed, n * 16 + 16)

        @block.sync
        def _(sp):
            for s in range(2):
                sp.sem_inc(stored[s], 16)

            def load(it, par):
                for dst, src, done in ((rqk, keep["qk"], qk_loaded), (V[par], keep["v"], v_loaded[par])):
                    for half in (slice(0, TPB // 2), slice(TPB // 2, TPB)):
                        sp.dma_start(dst[:, half, :], src[ds(it, 1), half, :, :].rearrange("i t p e -> p (i t) e")).then_inc(done, 16)

            def body(it, par, j, more):
                if more:
                    sp.wait_ge(T.split_done, it * 4 + 4)
                    sp.wait_ge(pv_done, it * NST + 2)
                    load(it + 1, 1 - par)
                for c in range(QC):
                    sp.wait_ge(divided, it * QC + c + 2)
                    sp.dma_start(keep["ao"][ds(it * QC + c, 1), :, :, :].rearrange("n q p e -> p (n q) e"),
                                 ob[c % 2][:, :, :, :].rearrange("p q h e -> p q (h e)")).then_inc(stored[c % 2], 16)
            iterations(sp, lambda: load(0, 0), body)
            for s in range(2):
                sp.wait_ge(stored[s], 16 + 16 * NIT * QC // 2)

        @block.vector
        def _(dve):
            v = nc.vector
            T.begin_dve(dve)
            dve.sem_inc(out_copied, 2)
            dve.sem_inc(divided, 1)

            def finish(it, c):
                s = c % 2
                dve.wait_ge(pv_done, it * NST + LAST[c] + 3)
                v.tensor_copy(OT[s][:, :], pO[:, :]).then_inc(out_copied, 1)
                dve.wait_ge(out_turned, it * QC + c + 1)
                y = pY[:, :, :].rearrange("p q (h e) -> p q h e", h=4)
                v.reciprocal(rc[:, :, :], y[:, :, :, HD])
                dve.drain()
                dve.wait_ge(stored[s], (it * 2 + c // 2) * 16 + 16)
                v.tensor_tensor(ob[s][:, :, :, :], y[:, :, :, 0:HD], rc[:, :, :].unsqueeze(3).broadcast_to([P, 4, 4, HD]),
                                ALU.mult).then_inc(divided, 1)

            def evict(n, qd, par):
                for gi in range(4):
                    T.evict(dve, n, qd, gi, par)

            def first():
                dve.wait_ge(qk_loaded, 32)
                for qd in range(4):
                    T.split(dve, 0, qd)
                    evict(0, qd, 0)

            def body(it, par, j, more):
                n = it + 1
                finish(it, 0)
                if more:
                    dve.wait_ge(qk_loaded, it * 32 + 64)
                    T.split(dve, n, 0)
                    T.split(dve, n, 1)
                finish(it, 1)
                if more:
                    dve.wait_ge(pv_done, it * NST + 2)
                    evict(n, 0, 1 - par)
                    T.split(dve, n, 2)
                    evict(n, 1, 1 - par)
                finish(it, 2)
                if more:
                    T.split(dve, n, 3)
                    evict(n, 2, 1 - par)
                    evict(n, 3, 1 - par)
                finish(it, 3)
            iterations(dve, first, body)

        @block.scalar
        def _(act):
            act.sem_inc(exp_done, 3)

            def body(it, par, j, more):
                for u, (n, heads, banks, width) in enumerate(UNITS):
                    act.wait_ge(scored, it * NU + u + 1)
                    user = UNITS[u - 4][0] if u >= 4 else UNITS[u - 4][0] - NST
                    act.wait_ge(pv_done, it * NST + user + 3)
                    nc.scalar.activation(PT[u % 4][:, 0:banks, 0:width], pS[u % 3][:, 0:banks, 0:width], ACT.Exp,
                                         scale=HD ** -0.5).then_inc(exp_done, 1)
            iterations(act, lambda: None, body)

        @block.tensor
        def _(pe):
            mm = nc.tensor.matmul
            pe.sem_inc(pv_done, 2)
            pe.wait_ge(made, 2)

            def scores(it, par, n):
                c, kb = STEPS[n]
                off = max(0, kb - 4 * c) * P
                for u, (of, heads, banks, width) in enumerate(UNITS):
                    if of != n:
                        continue
                    pe.wait_ge(exp_done, it * NU + u + 1)
                    for h in heads:
                        _, b, col = PLACE[n, h]
                        last = mm(pS[u % 3][:, b, col:col + 512 - off], KT[par][0:KS, h, kb * P:(kb + 1) * P],
                                  QT[par][0:KS, h, c * 512 + off:(c + 1) * 512], start=True, stop=kb < 4 * c)
                        if kb >= 4 * c:
                            last = mm(pS[u % 3][:, b, col:col + P], identb[:, :], mask[:, :], start=False, stop=True)
                    last.then_inc(scored, 1)

            def values(it, par, n):
                c, kb = STEPS[n]
                off = max(0, kb - 4 * c) * P
                if kb == 0:
                    pe.wait_ge(out_copied, it * QC + c + 2)
                pe.wait_ge(exp_done, it * NU + PLACE[n, 3][0] + 4)
                for h in range(4):
                    u, b, col = PLACE[n, h]
                    last = mm(pO[32 * h:32 * h + 32, off:512], V[par][:, kb, 32 * h:32 * h + 32],
                              PT[u % 4][:, b, col:col + 512 - off], start=(kb == 0), stop=(kb == 4 * c + 3))
                last.then_inc(pv_done, 1)

            def turn_out(it, c, groups):
                pe.wait_ge(out_copied, it * QC + c + 3)
                pe.wait_ge(divided, it * QC + c + 1)
                pe.wait_ge(T.evicted, it * 16 + 16 + groups + 1)
                for q in range(4):
                    last = nc.tensor.transpose(pY[:, q, :], OT[c % 2][:, q * P:(q + 1) * P], ident[:, :])
                last.then_inc(out_turned, 1)

            def first():
                for qd in range(4):
                    for gi in range(4):
                        T.turn(pe, 0, qd, gi)

            extra = {}
            for c in range(1, QC):
                extra.setdefault((c, 1), []).append(("out", c - 1))
            for qd, (c, kb) in enumerate(((2, 2), (2, 8), (3, 4), (3, 9))):
                for gi in range(4):
                    extra.setdefault((c, kb + gi), []).append((qd, gi))

            def body(it, par, j, more):
                pe.wait_ge(T.evicted, it * 16 + 17)
                pe.wait_ge(v_loaded[par], j * 32 + 32)
                groups = 0
                for n, (c, kb) in enumerate(STEPS):
                    scores(it, par, n)
                    if n:
                        values(it, par, n - 1)
                    for what, x in extra.get((c, kb), []):
                        if what == "out":
                            turn_out(it, x, groups)
                        elif more:
                            pe.wait_ge(divided, it * QC + c + 1)
                            T.turn(pe, it + 1, what, x)
                            groups += 1
                values(it, par, NST - 1)
                turn_out(it, QC - 1, groups)
            iterations(pe, first, body)


def project_out(nc, mem, io, keep, st):
    X, ident = keep["X"], keep["ident"]
    W = mem.sb("W", [P, DC, D])
    a = [mem.sb(f"a{k}", [P, 4, G, 4 * HD]) for k in range(2)]
    aT = [mem.sb(f"aT{f}", [P, DC, P]) for f in range(4)]
    w_loaded, a_ready, turned, aT_ready, projected, x_ready = (mem.sem(n) for n in (
        "w_loaded", "a_ready", "turned", "aT_ready", "projected", "x_ready"))
    a_loaded = [mem.sem(f"a_loaded{k}") for k in range(2)]
    pT = [mem.ps(f"pT{u}", [P, DC, P]) for u in range(2)]
    pP = [mem.ps(f"pP{u}", [P, D]) for u in range(2)]
    with nc.Block() as block:
        @block.sync
        def _(sp):
            sp.dma_start(W[:, :, :], io["WoT"].rearrange("(c p) n -> p c n", p=P)).then_inc(w_loaded, 16)
            with sp.Fori(0, B) as b:
                for c in range(4):
                    k = c % 2
                    sp.wait_ge(turned, (b * 4 + c) * 4 + 4)
                    for g in range(G):
                        sp.dma_start(a[k][:, :, g, :], keep["ao"][ds(b * 16 + g * 4 + c, 1), :, :, :].rearrange("n q p e -> p (n q) e"))\
                          .then_inc(a_loaded[k], 16)

        @block.vector
        def _(dve):
            dve.sem_inc(x_ready, 2)
            with dve.Fori(0, NT // 4) as q:
                for f in range(4):
                    t = q * 4 + f
                    dve.wait_ge(projected, t + 1)
                    nc.vector.tensor_tensor(X[:, ds(t, 1), :], X[:, ds(t, 1), :], pP[f % 2][:, :].unsqueeze(1), ALU.add).then_inc(x_ready, 1)
                    dve.drain()
                    nc.vector.bn_stats(st[:, ds(t, 1), :], X[:, ds(t, 1), :])

        @block.scalar
        def _(act):
            act.sem_inc(aT_ready, 2)
            with act.Fori(0, NT // 4) as q:
                for f in range(4):
                    act.wait_ge(turned, q * 4 + f + 9)
                    nc.scalar.activation(aT[f][:, :, :], pT[f % 2][:, :, :], ACT.Copy).then_inc(aT_ready, 1)

        @block.tensor
        def _(pe):
            pe.sem_inc(turned, 8)
            pe.wait_ge(w_loaded, 16)
            with pe.Fori(0, NT // 8) as q:
                for k in range(2):
                    def turn(f):
                        pe.wait_ge(aT_ready, q * 8 + k * 4 + f + 1)
                        av = a[k][:, f, :, :].rearrange("p g e -> p (g e)")
                        for c in range(DC):
                            last = nc.tensor.transpose(pT[f % 2][:, c, :], av[:, c * P:(c + 1) * P], ident[:, :])
                        last.then_inc(turned, 1)

                    def project(f):
                        pe.wait_ge(aT_ready, q * 8 + k * 4 + f + 3)
                        pe.wait_ge(x_ready, q * 8 + k * 4 + f + 1)
                        for c in range(DC):
                            last = nc.tensor.matmul(pP[f % 2][:, :], aT[f][:, c, :], W[:, c, :], start=(c == 0), stop=(c == DC - 1))
                        last.then_inc(projected, 1)
                    pe.wait_ge(a_loaded[k], q * (16 * G) + 16 * G)
                    for f in range(4):
                        turn(f)
                        if f:
                            project(f - 1)
                    project(3)


NPT = 2 * NT + E1


def route(nc, mem, io, keep):
    X, mean, rstd, ident = keep["X"], keep["mean"], keep["rstd"], keep["ident"]
    wt, dest, which = keep["wt"], keep["dest"], keep["which"]
    R = mem.sb("R", [P, DC, E1])
    z = [mem.sb(f"z{f}", [P, D]) for f in range(4)]
    zT = [mem.sb(f"zT{f}", [P, DC, P]) for f in range(4)]
    rw = mem.sb("rw", [P, NT, E1])
    M1, M2 = mem.sb("M1", [P, NT, E1]), mem.sb("M2", [P, NT, E1])
    t1, t2 = mem.sb("t1", [P, NT, E1]), mem.sb("t2", [P, NT, E1])
    Mb = mem.sb("Mb", [P, NT, E1], bf16)
    before, onesb = mem.sb("before", [P, P], bf16), mem.sb("onesb", [P, P], bf16)
    code = mem.sb("code", [P, E1])
    row = mem.sb("row", [P, NPT])
    s1, s2 = mem.sb("s1", [P, NT]), mem.sb("s2", [P, NT])
    n1, n2, nt, ni = mem.sb("n1", [P, E1]), mem.sb("n2", [P, E1]), mem.sb("nt", [P, E1]), mem.sb("ni", [P, E1], mybir.dt.int32)
    wf = mem.sb("wf", [1, NPT])
    codei, rowi = mem.sb("codei", [P, E1], mybir.dt.int32), mem.sb("rowi", [P, NPT], mybir.dt.int32)
    z_ready, turned, zT_ready, l_done, l_ready, made, w_loaded = (mem.sem(n) for n in (
        "z_ready", "turned", "zT_ready", "l_done", "l_ready", "made", "w_loaded"))
    less_max, exps, chosen, ranked = (mem.sem(n) for n in ("less_max", "exps", "chosen", "ranked"))

    with ExitStack() as sub:
        m = Memory(nc, sub, "rt1")
        pT = [m.ps(f"pT{u}", [P, DC, P]) for u in range(2)]
        pR = [m.ps(f"pR{u}", [P, E1]) for u in range(2)]
        block = sub.enter_context(nc.Block())

        @block.sync
        def _(sp):
            sp.dma_start(R[:, :, :], io["routerT"].rearrange("(c p) n -> p c n", p=P)).then_inc(w_loaded, 16)

        @block.gpsimd
        def _(pool):
            g = nc.gpsimd
            g.memset(before[:, :], 1.0).then_inc(made, 1)
            g.memset(onesb[:, :], 1.0)
            pool.wait_ge(made, 1)
            g.affine_select(out=before[:, :], in_=before[:, :], compare_op=ALU.is_gt, fill=0.0,
                            base=0, pattern=[[1, P]], channel_multiplier=-1)
            g.iota(codei[:, :], pattern=[[-1, E1]], base=E1, channel_multiplier=0)
            g.iota(rowi[:, :], pattern=[[1, NPT]], base=0, channel_multiplier=0)

        @block.vector
        def _(dve):
            dve.sem_inc(l_ready, 2)
            with dve.Fori(0, NT // 4) as q:
                for f in range(4):
                    dve.wait_ge(turned, q * 4 + f + 1)
                    nc.vector.tensor_scalar(z[f][:, :].unsqueeze(1), X[:, ds(q * 4 + f, 1), :], mean[:, ds(q * 4 + f, 1)],
                                            rstd[:, ds(q * 4 + f, 1)], ALU.subtract, ALU.mult).then_inc(z_ready, 1)
                for f in range(4):
                    dve.wait_ge(l_done, q * 4 + f + 1)
                    nc.vector.tensor_copy(rw[:, ds(q * 4 + f, 1), :], pR[f % 2][:, :].unsqueeze(1)).then_inc(l_ready, 1)

        @block.scalar
        def _(act):
            act.sem_inc(zT_ready, 2)
            with act.Fori(0, NT // 4) as q:
                for f in range(4):
                    act.wait_ge(turned, q * 4 + f + 5)
                    nc.scalar.activation(zT[f][:, :, :], pT[f % 2][:, :, :], ACT.Copy).then_inc(zT_ready, 1)

        @block.tensor
        def _(pe):
            pe.sem_inc(turned, 4)
            pe.wait_ge(w_loaded, 16)
            with pe.Fori(0, NT // 4) as q:
                def turn(f):
                    pe.wait_ge(z_ready, q * 4 + f + 1)
                    pe.wait_ge(zT_ready, q * 4 + f + 1)
                    for c in range(DC):
                        last = nc.tensor.transpose(pT[f % 2][:, c, :], z[f][:, c * P:(c + 1) * P], ident[:, :])
                    last.then_inc(turned, 1)

                def logits(f):
                    pe.wait_ge(zT_ready, q * 4 + f + 3)
                    pe.wait_ge(l_ready, q * 4 + f + 1)
                    for c in range(DC):
                        last = nc.tensor.matmul(pR[f % 2][:, :], zT[f][:, c, :], R[:, c, :], start=(c == 0), stop=(c == DC - 1))
                    last.then_inc(l_done, 1)
                for f in range(4):
                    turn(f)
                    if f:
                        logits(f - 1)
                logits(3)

    with ExitStack() as sub:
        m = Memory(nc, sub, "rt2")
        pB = m.ps("pB", [P, NT * E1])
        pC = m.ps("pC", [P, NT * E1])
        block = sub.enter_context(nc.Block())
        wide = lambda a: a.unsqueeze(2).broadcast_to([P, NT, E1])
        per = lambda a: a.unsqueeze(1).broadcast_to([P, NT, E1])

        @block.vector
        def _(dve):
            v = nc.vector

            def step(*ops):
                for op in ops:
                    op()
                dve.drain()
            A = lambda t: t[:, :, :]
            tt = lambda o, a, b, op: (lambda: v.tensor_tensor(o, a, b, op))
            ts = lambda o, a, s, op, s2=None, op2=ALU.bypass: (lambda: v.tensor_scalar(o, a, s, s2, op, op2))
            red = lambda o, a, op: (lambda: v.tensor_reduce(o, a, AX, op))
            step(red(s1[:, :], A(rw), ALU.max), lambda: v.tensor_copy(code[:, :], codei[:, :]), lambda: v.tensor_copy(row[:, :], rowi[:, :]))
            step(tt(A(rw), A(rw), wide(s1[:, :]), ALU.subtract))
            dve.drain().then_inc(less_max, 1)
            dve.wait_ge(exps, 1)
            step(red(s1[:, :], A(rw), ALU.add))
            step(lambda: v.reciprocal(s1[:, :], s1[:, :]))
            step(tt(A(rw), A(rw), wide(s1[:, :]), ALU.mult))
            for k, Mk in enumerate((M1, M2)):
                src = rw if k == 0 else t2
                best = wt[:, k, :]
                step(red(best, A(src), ALU.max))
                step(tt(A(t1), A(src), wide(best), ALU.is_equal))
                step(tt(A(t1), A(t1), per(code[:, :]), ALU.mult))
                step(red(s1[:, :], A(t1), ALU.max))
                step(tt(A(Mk), per(code[:, :]), wide(s1[:, :]), ALU.is_equal))
                if k == 0:
                    step(ts(A(t1), A(M1), 2.0, ALU.mult))
                    step(tt(A(t2), A(rw), A(t1), ALU.subtract))
            step(tt(A(Mb), A(M1), A(M2), ALU.add))
            dve.drain().then_inc(chosen, 1)
            dve.wait_ge(ranked, 1)
            pc = pC[:, :].rearrange("p (t e) -> p t e", e=E1)
            pb = pB[:, :].rearrange("p (t e) -> p t e", e=E1)
            step(lambda: v.tensor_copy(A(t1), pc))
            a, c = t1, t2
            n = 1
            while n < NT:
                step(tt(c[:, n:, :], a[:, n:, :], a[:, :NT - n, :], ALU.add), lambda n=n, a=a, c=c: v.tensor_copy(c[:, :n, :], a[:, :n, :]))
                a, c = c, a
                n *= 2
            step(ts(nt[:, :], a[:, NT - 1, :], float(P - 1), ALU.add))
            step(lambda: v.tensor_copy(ni[:, :], nt[:, :]))
            step(ts(ni[:, :], ni[:, :], 7, ALU.arith_shift_right))
            step(lambda: v.tensor_copy(nt[:, :], ni[:, :]), lambda: v.tensor_copy(n1[:, :], ni[:, :]))
            x, y = n1, n2
            n = 1
            while n < E1:
                step(tt(y[:, n:], x[:, n:], x[:, :E1 - n], ALU.add), lambda n=n, x=x, y=y: v.tensor_copy(y[:, :n], x[:, :n]))
                x, y = y, x
                n *= 2
            step(tt(nt[:, :], x[:, :], nt[:, :], ALU.subtract))
            step(ts(nt[:, :], nt[:, :], float(P), ALU.mult))
            step(tt(A(a), A(a), pc, ALU.subtract))
            step(tt(A(a), A(a), pb, ALU.add))
            step(tt(A(a), A(a), per(nt[:, :]), ALU.add))
            for k, Mk in enumerate((M1, M2)):
                step(tt(A(c), A(a), A(Mk), ALU.mult))
                step(red(s2[:, :], A(c), ALU.add))
                step(lambda: v.tensor_copy(dest[:, k, :], s2[:, :]))
            cnt = t1[0:1, :, :].rearrange("p t e -> p (t e)")
            for lo in range(0, NPT, 64):
                w = min(64, NPT - lo)
                sl = cnt[:, 0:w * E1].rearrange("p (t e) -> p t e", e=E1)
                step(tt(sl, row[0:1, lo:lo + w].unsqueeze(2).broadcast_to([1, w, E1]),
                        x[0:1, :].unsqueeze(1).broadcast_to([1, w, E1]), ALU.is_ge))
                step(red(wf[:, lo:lo + w], sl, ALU.add))
            step(ts(wf[:, :], wf[:, :], float(E1 - 1), ALU.min))
            v.tensor_copy(which[:, :], wf[:, :])

        @block.scalar
        def _(act):
            act.wait_ge(less_max, 1)
            nc.scalar.activation(rw[:, :, :], rw[:, :, :], ACT.Exp).then_inc(exps, 1)

        @block.tensor
        def _(pe):
            pe.wait_ge(chosen, 1)
            flat = Mb[:, :, :].rearrange("p t e -> p (t e)")
            for src, dst in ((before, pB), (onesb, pC)):
                for c in range(0, NT * E1, 512):
                    last = nc.tensor.matmul(dst[:, c:c + 512], src[:, :], flat[:, c:c + 512], start=True, stop=True)
            last.then_inc(ranked, 1)


def experts(nc, mem, io, keep):
    X, mean, rstd, ident = keep["X"], keep["mean"], keep["rstd"], keep["ident"]
    wt, dest, which = keep["wt"], keep["dest"], keep["which"]
    xg, yg = keep["xg"], keep["yg"]
    i32 = mybir.dt.int32
    W = mem.sb("W", [P, DC, E1, D])
    w_loaded = [mem.sem(f"w_loaded{c}") for c in range(2)]

    with ExitStack() as sub:
        m = Memory(nc, sub, "ex1")
        z = [m.sb(f"z{f}", [P, D]) for f in range(4)]
        zw = [[m.sb(f"zw{k}{f}", [P, D]) for f in range(4)] for k in range(2)]
        ix = [[m.sb(f"ix{k}{f}", [P, 1], i32) for f in range(4)] for k in range(2)]
        sent = [[m.sem(f"sent{k}{f}") for f in range(4)] for k in range(2)]
        ready, seen = m.sem("ready"), m.sem("seen")
        block = sub.enter_context(nc.Block())

        @block.sync
        def _(sp):
            for c in range(DC):
                sp.dma_start(W[:, c, :, :], io["we"][:, c * P:(c + 1) * P, :].rearrange("e p d -> p e d")).then_inc(w_loaded[c], 16)

        @block.vector
        def _(dve):
            v = nc.vector

            def copies(q):
                for f in range(4):
                    t = q * 4 + f
                    v.tensor_scalar(z[f][:, :].unsqueeze(1), X[:, ds(t, 1), :], mean[:, ds(t, 1)], rstd[:, ds(t, 1)], ALU.subtract, ALU.mult)
                    dve.drain()
                    for k in range(2):
                        if not (isinstance(q, int) and q == 0):
                            dve.wait_ge(sent[k][f], q * 16)
                        v.tensor_copy(ix[k][f][:, :], dest[:, k, ds(t, 1)])
                        v.tensor_scalar(zw[k][f][:, :], z[f][:, :], wt[:, k, ds(t, 1)], None, ALU.mult)
                    dve.drain().then_inc(ready, 1)
            copies(0)
            with dve.Fori(1, NT // 4) as q:
                copies(q)

        @block.gpsimd
        def _(pool):
            with pool.Fori(0, NT // 4) as q:
                for f in range(4):
                    pool.wait_ge(ready, q * 4 + f + 1)
                    pool.sem_inc(seen, 1)
                    for k in range(2):
                        nc.gpsimd.indirect_dma_start(out=xg, out_offset=bass.IndirectOffsetOnAxis(ap=ix[k][f][:, 0:1], axis=0),
                                                     in_=zw[k][f][:, :], in_offset=None).then_inc(sent[k][f], 16)
            for k in range(2):
                for f in range(4):
                    pool.wait_ge(sent[k][f], 16 * (NT // 4))

    with ExitStack() as sub:
        m = Memory(nc, sub, "ex2")
        NB = 4
        xin = [m.sb(f"xin{k}", [P, NB, D]) for k in range(2)]
        xT = [m.sb(f"xT{f}", [P, DC, P]) for f in range(4)]
        yout = [m.sb(f"yout{k}", [P, NB, D]) for k in range(2)]
        x_in = [m.sem(f"x_in{k}") for k in range(2)]
        y_out = [m.sem(f"y_out{k}") for k in range(2)]
        turned, xT_ready, multiplied, y_ready = (m.sem(n) for n in ("turned", "xT_ready", "multiplied", "y_ready"))
        pT = [m.ps(f"pT{u}", [P, DC, P]) for u in range(2)]
        pY = [m.ps(f"pY{u}", [P, D]) for u in range(2)]
        xgv = xg.rearrange("(q n p) d -> q n p d", n=NB, p=P)
        ygv = yg.rearrange("(q n p) d -> q n p d", n=NB, p=P)
        block = sub.enter_context(nc.Block())

        @block.sync
        def _(sp):
            for k in range(2):
                sp.sem_inc(y_out[k], 16)

            def load(r, k):
                sp.wait_ge(turned, (r * 2 + k) * NB + NB)
                sp.dma_start(xin[k][:, :, :], xgv[ds(r * 2 + k, 1), :, :, :].rearrange("q n p d -> p (q n) d")).then_inc(x_in[k], 16)

            def keep_y(r, k):
                sp.wait_ge(y_ready, (r * 2 + k) * NB + NB + 2)
                sp.dma_start(ygv[ds(r * 2 + k, 1), :, :, :].rearrange("q n p d -> p (q n) d"), yout[k][:, :, :]).then_inc(y_out[k], 16)
            load(0, 0)
            load(0, 1)
            with sp.Fori(1, NPT // NB // 2) as r:
                for k in range(2):
                    load(r, k)
                    keep_y(r - 1, k)
            for k in range(2):
                keep_y(NPT // NB // 2 - 1, k)
            for k in range(2):
                sp.wait_ge(y_out[k], 16 + 16 * (NPT // NB // 2))

        @block.vector
        def _(dve):
            dve.sem_inc(y_ready, 2)
            with dve.Fori(0, NPT // NB // 2) as r:
                for k in range(2):
                    dve.wait_ge(y_out[k], r * 16 + 16)
                    for f in range(NB):
                        dve.wait_ge(multiplied, r * 8 + k * 4 + f + 1)
                        nc.vector.tensor_copy(yout[k][:, f, :], pY[f % 2][:, :]).then_inc(y_ready, 1)

        @block.scalar
        def _(act):
            act.sem_inc(xT_ready, 2)
            with act.Fori(0, NPT // NB) as q:
                for f in range(NB):
                    act.wait_ge(turned, q * 4 + f + 9)
                    nc.scalar.activation(xT[f][:, :, :], pT[f % 2][:, :, :], ACT.Copy).then_inc(xT_ready, 1)

        @block.tensor
        def _(pe):
            pe.sem_inc(turned, 2 * NB)
            for c in range(DC):
                pe.wait_ge(w_loaded[c], 16)
            with pe.Fori(0, NPT // NB // 2) as r:
                for k in range(2):
                    def turn(f):
                        pe.wait_ge(xT_ready, r * 8 + k * 4 + f + 1)
                        for c in range(DC):
                            last = nc.tensor.transpose(pT[f % 2][:, c, :], xin[k][:, f, c * P:(c + 1) * P], ident[:, :])
                        last.then_inc(turned, 1)

                    def multiply(f):
                        e = pe.value_load(which[0:1, ds(r * 8 + k * 4 + f, 1)], min_val=0, max_val=E1 - 1)
                        pe.wait_ge(xT_ready, r * 8 + k * 4 + f + 3)
                        pe.wait_ge(y_ready, r * 8 + k * 4 + f + 1)
                        for c in range(DC):
                            last = nc.tensor.matmul(pY[f % 2][:, :].unsqueeze(1), xT[f][:, c, :], W[:, c, ds(e, 1), :],
                                                    start=(c == 0), stop=(c == DC - 1))
                        last.then_inc(multiplied, 1)
                    pe.wait_ge(x_in[k], r * 16 + 16)
                    for f in range(NB):
                        turn(f)
                        if f:
                            multiply(f - 1)
                    multiply(NB - 1)

    with ExitStack() as sub:
        m = Memory(nc, sub, "ex3")
        y = [[m.sb(f"y{k}{f}", [P, D]) for f in range(4)] for k in range(2)]
        ix = [[m.sb(f"ix{k}{f}", [P, 1], i32) for f in range(4)] for k in range(2)]
        res = [m.sb(f"res{f}", [P, D]) for f in range(4)]
        got = [[m.sem(f"got{k}{f}") for f in range(4)] for k in range(2)]
        stored = [m.sem(f"stored{f}") for f in range(4)]
        named, added, seen = m.sem("named"), m.sem("added"), m.sem("seen")
        ov = io["out"].rearrange("b (t p) d -> (b t) p d", p=P)
        block = sub.enter_context(nc.Block())

        @block.vector
        def _(dve):
            v = nc.vector
            dve.sem_inc(added, 4)
            for f in range(4):
                dve.sem_inc(stored[f], 16)

            def name(q, f):
                for k in range(2):
                    v.tensor_copy(ix[k][f][:, :], dest[:, k, ds(q * 4 + f, 1)])
                dve.drain().then_inc(named, 1)

            def add(q, f):
                t = q * 4 + f
                for k in range(2):
                    dve.wait_ge(got[k][f], q * 16 + 16)
                dve.wait_ge(stored[f], q * 16 + 16)
                v.tensor_tensor(res[f][:, :].unsqueeze(1), X[:, ds(t, 1), :], y[0][f][:, :].unsqueeze(1), ALU.add)
                dve.drain()
                v.tensor_tensor(res[f][:, :], res[f][:, :], y[1][f][:, :], ALU.add).then_inc(added, 1)
            for f in range(4):
                name(0, f)
            with dve.Fori(1, NT // 4) as q:
                for f in range(4):
                    add(q - 1, f)
                    name(q, f)
            for f in range(4):
                add(NT // 4 - 1, f)

        @block.gpsimd
        def _(pool):
            with pool.Fori(0, NT // 4) as q:
                for f in range(4):
                    pool.wait_ge(named, q * 4 + f + 1)
                    pool.sem_inc(seen, 1)
                    for k in range(2):
                        nc.gpsimd.indirect_dma_start(out=y[k][f][:, :], out_offset=None, in_=yg,
                                                     in_offset=bass.IndirectOffsetOnAxis(ap=ix[k][f][:, 0:1], axis=0)).then_inc(got[k][f], 16)

        @block.sync
        def _(sp):
            with sp.Fori(0, NT // 4) as q:
                for f in range(4):
                    sp.wait_ge(added, q * 4 + f + 5)
                    sp.dma_start(ov[ds(q * 4 + f, 1), :, :].rearrange("n p d -> p n d"), res[f][:, :].unsqueeze(1)).then_inc(stored[f], 16)
            for f in range(4):
                sp.wait_ge(stored[f], 16 + 16 * (NT // 4))


def store(nc, mem, io, keep):
    X = keep["X"]
    stored = [mem.sem(f"stored{b}") for b in range(B)]
    ov = io["out"].rearrange("b (t p) d -> b p t d", p=P)
    with nc.Block() as block:
        @block.sync
        def _(sp):
            for b in range(B):
                sp.dma_start(ov[b], X[:, b * TPB:(b + 1) * TPB, :]).then_inc(stored[b], 16)
            for b in range(B):
                sp.wait_ge(stored[b], 16)


def build(nc, io):
    with ExitStack() as ctx:
        mem = Memory(nc, ctx, "all")
        keep = {"X": mem.sb("X", [P, NT, D]), "ident": mem.sb("ident", [P, P]), "identb": mem.sb("identb", [P, P], bf16),
                "mean": mem.sb("mean", [P, NT]), "rstd": mem.sb("rstd", [P, NT])}
        st = mem.sb("stats", [P, NT, 6])
        def stage(name, f, *args):
            with ExitStack() as sub:
                own = Memory(nc, sub, name)
                f(nc, own, *args)
                if name in ("in", "n1", "n2", "bd"):
                    own.clear()
        stage("in", load_and_constants, io, keep, st)
        stage("n1", finish_rstd, keep, st, False)
        stage("la", linear_attention, io, keep, st)
        stage("n2", finish_rstd, keep, st, True)
        stage("sm", soft_mixture, io, keep, st)
        keep["qk"] = nc.dram_tensor("rotated_qk", (B * G, TPB, P, P), fp32).ap()
        keep["v"] = nc.dram_tensor("values", (B * G, TPB, P, 4 * VW), fp32).ap()
        keep["ao"] = nc.dram_tensor("head_outputs", (B * G * (N // 512), 4, P, 4 * HD), fp32).ap()
        keep["xg"] = nc.dram_tensor("rows_in", (NPT * P, D), fp32).ap()
        keep["yg"] = nc.dram_tensor("rows_out", (NPT * P, D), fp32).ap()
        keep["wt"] = mem.sb("wt", [P, 2, NT])
        keep["dest"] = mem.sb("dest", [P, 2, NT], mybir.dt.int32)
        keep["which"] = mem.sb("which", [1, NPT], mybir.dt.int32)
        keep["nmax"] = mem.sb("nmax", [P, B * G, TPB * 4])
        stage("n3", finish_rstd, keep, st, False)
        keep["need_max"] = mem.sb("need_max", [1, 1], mybir.dt.int32)
        with ExitStack() as sub:
            nn = Memory(nc, sub, "qk").sb("nn", [P, NT, 3 * H])
            stage("qk", project_qkv, io, keep, nn)
            stage("bd", bound_scores, io, keep, nn)
        stage("mx", row_maxima, io, keep)
        stage("at", attention, io, keep)
        stage("pr", project_out, io, keep, st)
        stage("n4", finish_rstd, keep, st, False)
        stage("rt", route, io, keep)
        stage("ex", experts, io, keep)


_OUTS = [((4, 2048, 256), 'float32')]


def kernel(**inputs):
    import numpy as _np
    import concourse.bacc as _bacc
    from concourse import mybir as _mybir
    from concourse.bass_utils import run_bass_kernel_spmd as _run

    nc = _bacc.Bacc("TRN2", target_bir_lowering=False, num_devices=1)
    c = _np.ascontiguousarray
    i = {k: _np.asarray(v) for k, v in inputs.items()}
    laid = {
        "x": c(i["L0_attn_x"]),
        "qkvT": c(i["L0_attn_qkv_w"].T), "qkv_b": c(i["L0_attn_qkv_b"]),
        "projT": c(i["L0_attn_proj_w"].T), "proj_b": c(i["L0_attn_proj_b"]),
        "pmT": c(i["L0_attn_projection_matrix"].T),
        "gamma": c(i["L0_ffn_ln_gamma"]), "beta": c(i["L0_ffn_ln_beta"]),
        "mu": c(i["L0_ffn_mu"].reshape(256, 256)), "scale": c(i["L0_ffn_scale"]),
        "w1": c(i["L0_ffn_w1"]), "b1": c(i["L0_ffn_b1"]), "w2": c(i["L0_ffn_w2"]), "b2": c(i["L0_ffn_b2"]),
        "WqT": c(i["L1_attn_Wq"].T), "WkT": c(i["L1_attn_Wk"].T), "WvT": c(i["L1_attn_Wv"].T),
        "WoT": c(i["L1_attn_Wo"].T),
        "routerT": c(i["L1_ffn_router_w"].T), "we": c(i["L1_ffn_expert_weights"]),
    }
    laid.update(tables())
    io, arrays = {}, {}
    for name, a in laid.items():
        arrays[f"in_{name}"] = a
        io[name] = nc.dram_tensor(f"in_{name}", a.shape, _mybir.dt.from_np(a.dtype), kind="ExternalInput").ap()
    for n, (shape, dtype) in enumerate(_OUTS):
        io["out"] = nc.dram_tensor(f"out_{n}_dram", shape, _mybir.dt.from_np(_np.dtype(dtype)), kind="ExternalOutput").ap()
    build(nc, io)
    r = _run(nc, [arrays], core_ids=[0])
    return r.results[0]["out_0_dram"]
```

```python
import concourse.bass as bass
from concourse import mybir
from contextlib import ExitStack
import numpy as np

fp32 = mybir.dt.float32
bf16 = mybir.dt.bfloat16
ALU = mybir.AluOpType
ACT = mybir.ActivationFunctionType
AX = mybir.AxisListType.X
ds = bass.ds

B, N, D = 4, 2048, 256
P = 128
TPB = N // P
NT = B * TPB
H, HD = 16, 16
M = 64
DC = D // P
VW = 32
G = H // 4
E0, S0, HID = 16, 16, 64
NS = E0 * S0
E1 = 32
LN_EPS = 1e-5
FEAT_EPS = 1e-6
MASKED = -1e30


class Memory:

    def __init__(self, nc, ctx, stage):
        self.nc, self.ctx, self.stage, self.sems = nc, ctx, stage, []

    def sb(self, name, shape, dt=fp32):
        return self.ctx.enter_context(self.nc.sbuf_tensor(f"{self.stage}_{name}", shape, dt))

    def ps(self, name, shape, dt=fp32):
        return self.ctx.enter_context(self.nc.psum_tensor(f"{self.stage}_{name}", shape, dt))

    def sem(self, name):
        self.sems.append(self.ctx.enter_context(self.nc.semaphore(f"{self.stage}_{name}")))
        return self.sems[-1]

    def clear(self):
        with self.nc.Block() as block:
            @block.gpsimd
            def _(pool):
                for s in self.sems:
                    pool.sem_clear(s)


def in_pairs(eng, front, back):
    front(0, 0)
    front(1, 1)
    back(0, 0)
    with eng.Fori(1, TPB // 4) as q:
        front(q * 2, 0)
        back(q * 2 - 1, 1)
        front(q * 2 + 1, 1)
        back(q * 2, 0)
    back(TPB // 2 - 1, 1)


def newton_rstd(nc, dve, mean, rstd, st, scratch, ve_ready, root_ready, before, rounds=1):
    v = nc.vector
    t1, t2, ve, var = (scratch[n][:, :] for n in ("t1", "t2", "ve", "var"))
    v.tensor_tensor(mean, st[:, :, 1], st[:, :, 4], ALU.add)
    v.tensor_tensor(t1, st[:, :, 1], st[:, :, 4], ALU.subtract)
    v.tensor_tensor(var, st[:, :, 2], st[:, :, 5], ALU.add)
    dve.drain()
    v.tensor_scalar(mean, mean, 0.5, None, ALU.mult)
    v.tensor_tensor(t1, t1, t1, ALU.mult)
    v.tensor_scalar(var, var, 1.0 / D, None, ALU.mult)
    dve.drain()
    v.tensor_scalar(t1, t1, 0.25, None, ALU.mult)
    dve.drain()
    v.tensor_tensor(var, var, t1, ALU.add)
    dve.drain()
    for r in range(rounds):
        v.tensor_scalar(ve, var, LN_EPS, None, ALU.add).then_inc(ve_ready, 1)
        dve.wait_ge(root_ready, before + r + 1)
        v.reciprocal(t1, t2)
        dve.drain()
        v.tensor_tensor(t2, t1, t1, ALU.mult)
        dve.drain()
        v.tensor_tensor(t2, t2, ve, ALU.mult)
        dve.drain()
        v.tensor_scalar(t2, t2, -0.5, 1.5, ALU.mult, ALU.add)
        dve.drain()
        if r == 0:
            v.tensor_tensor(rstd, t1, t2, ALU.mult)
            dve.drain()
            if rounds == 2:
                v.tensor_tensor(t1, rstd, rstd, ALU.mult)
                dve.drain()
                v.tensor_tensor(var, var, t1, ALU.mult)
                dve.drain()
        else:
            v.tensor_tensor(t1, t1, t2, ALU.mult)
            dve.drain()
            v.tensor_tensor(rstd, rstd, t1, ALU.mult)


def finish_rstd(nc, mem, keep, st, tiles, rounds):
    scratch = {n: mem.sb(f"ln_{n}", [P, tiles]) for n in ("t1", "t2", "ve", "var")}
    ve_ready, root_ready = mem.sem("ve_ready"), mem.sem("root_ready")
    with nc.Block() as block:
        @block.vector
        def _(dve):
            newton_rstd(nc, dve, keep["mean"][:, 0:tiles], keep["rstd"][:, 0:tiles], st[:, 0:tiles, :], scratch,
                        ve_ready, root_ready, 0, rounds)

        @block.scalar
        def _(act):
            for r in range(rounds):
                act.wait_ge(ve_ready, r + 1)
                nc.scalar.activation(scratch["t2"][:, :], scratch["ve"][:, :], ACT.Sqrt).then_inc(root_ready, 1)


def load_and_constants(nc, mem, io, keep, st):
    X = keep["X"]
    ident, identb = keep["ident"], keep["identb"]
    x_loaded = mem.sem("x_loaded")
    made = mem.sem("made")
    xv = io["x"].rearrange("b (t p) d -> b p t d", p=P)
    with nc.Block() as block:
        @block.sync
        def _(sp):
            sp.dma_start(X[:, 0:TPB, :], xv[0]).then_inc(x_loaded, 16)

        @block.gpsimd
        def _(pool):
            nc.gpsimd.memset(ident[:, :], 0.0).then_inc(made, 1)
            pool.wait_ge(made, 1)
            nc.gpsimd.affine_select(out=ident[:, :], in_=ident[:, :], compare_op=ALU.not_equal, fill=1.0,
                                    base=0, pattern=[[-1, P]], channel_multiplier=1).then_inc(made, 1)
            pool.wait_ge(made, 2)
            nc.gpsimd.tensor_copy(identb[:, :], ident[:, :])

        @block.vector
        def _(dve):
            dve.wait_ge(x_loaded, 16)
            with dve.Fori(0, TPB) as i:
                nc.vector.bn_stats(st[:, ds(i, 1), :], X[:, ds(i, 1), :])


def tables():
    freq = 1.0 / 10000.0 ** (np.arange(0, HD, 2, dtype=np.float32) / HD)
    angle = np.arange(N, dtype=np.float32)[:, None] * freq.astype(np.float32)[None, :]
    return {"cos": np.cos(angle).astype(np.float32), "sin": np.sin(angle).astype(np.float32)}


def linear_attention(nc, mem, io, keep, st):
    X, mean, rstd, ident = keep["X"], keep["mean"], keep["rstd"], keep["ident"]
    W = mem.sb("qkv_w", [P, DC, 3 * D])
    PW = mem.sb("proj_w", [P, DC, D])
    FM = mem.sb("feature_w", [P, 8 * M])
    qb, kb = mem.sb("qb", [P, DC]), mem.sb("kb", [P, DC])
    vb, pb = mem.sb("vb", [P, D]), mem.sb("pb", [P, D])
    zeros = mem.sb("zeros", [P, D])
    z, zT = mem.sb("z", [P, 4, D]), mem.sb("zT", [P, DC, 512])
    kT = [mem.sb(f"kT{u}", [P, DC, 512]) for u in range(2)]
    qT = mem.sb("qT", [P, TPB // 4, DC, 512])
    vx = [mem.sb(f"vx{u}", [P, 4, H, VW]) for u in range(2)]
    ft = [mem.sb(f"ft{u}", [P, H * M]) for u in range(4)]
    mx = [mem.sb(f"mx{u}", [P, H]) for u in range(2)]
    kvs = mem.sb("kvs", [P, G * M])
    NU, DE = mem.sb("NU", [P, 8, 2 * HD]), mem.sb("DE", [P, 8, 2 * HD])
    FT = [mem.sb(f"FT{u}", [P, 8, 512]) for u in range(2)]
    dn, rd = ([mem.sb(f"{n}{h}", [P, 512]) for h in range(2)] for n in ("dn", "rd"))
    oT = [mem.sb(f"oT{u}", [P, DC, 512]) for u in range(2)]
    ln = {n: mem.sb(f"ln_{n}", [P, TPB]) for n in ("t1", "t2", "ve", "var")}
    w_sem = mem.sem("weights")
    fm_sem = mem.sem("fm_loaded")
    fm_zero = mem.sem("fm_zero")

    with nc.Block() as block:
        @block.vector
        def _(dve):
            nc.vector.memset(FM[:, :], 0.0).then_inc(fm_zero, 1)
            nc.vector.memset(zeros[:, :], 0.0)
            nc.vector.memset(NU[:, :, :], 0.0)
            nc.vector.memset(DE[:, :, :], 0.0)
            for u in range(2):
                nc.vector.memset(vx[u][:, :, :, :], 0.0)
            dve.drain()
            for u in range(2):
                nc.vector.memset(vx[u][:, :, :, HD:HD + 1], 1.0)

        @block.sync
        def _(sp):
            n = 0
            for dst, src in ((W[:, :, :], io["qkvT"].rearrange("(c p) n -> p c n", p=P)),
                             (PW[:, :, :], io["projT"].rearrange("(c p) n -> p c n", p=P)),
                             (qb[:, :], io["qkv_b"][0:D].rearrange("(c p) -> p c", p=P)),
                             (kb[:, :], io["qkv_b"][D:2 * D].rearrange("(c p) -> p c", p=P)),
                             (vb[:, :], io["qkv_b"][2 * D:3 * D].partition_broadcast(P)),
                             (pb[:, :], io["proj_b"].partition_broadcast(P))):
                with nc.allow_non_contiguous_dma(reason="a bias as columns, once"):
                    sp.dma_start(dst, src).then_inc(w_sem, 16)
                n += 16
            sp.wait_ge(fm_zero, 1)
            for hl in range(8):
                sp.dma_start(FM[hl * HD:(hl + 1) * HD, hl * M:(hl + 1) * M], io["pmT"]).then_inc(fm_sem, 16)
            sp.wait_ge(fm_sem, 8 * 16)
            sp.wait_ge(w_sem, n)

    q_slot = {}
    for e in range(TPB):
        q_slot.setdefault(TPB + e + 2, []).extend([("Ea", e, 0), ("Eb", e, 0)])
    for qd in range(TPB // 4):
        for h in range(2):
            q_slot.setdefault(TPB + 4 * qd + 6 + h, []).extend([("D", qd, h), ("N", qd, h)])
        q_slot.setdefault(TPB + 4 * qd + 8, []).extend([("P", qd, 0), ("P", qd, 1)])
    LAST_SLOT = max(q_slot)
    for n in range(8):
        q_slot[2 * TPB + (0, 0, 1, 1, 2, 2, 3, 3)[n]].append(("A", n, 0))
    ring = [u for s in sorted(q_slot) for u in q_slot[s]]
    q_units = [u for u in ring if u[0] != "A"]
    BY_ACT = ("Ea", "Eb", "D")
    QU, KU = len(q_units), 8 * (TPB // 4)
    QA = sum(u[0] in BY_ACT for u in q_units)
    QD = QU - QA
    KA, KD = 6 * (TPB // 4), 2 * (TPB // 4)

    def q_emptied(unit):
        n = q_units.index(unit)
        by_act = unit[0] in BY_ACT
        return by_act, sum((u[0] in BY_ACT) == by_act for u in q_units[:n + 1])

    def k_bank(n):
        return ring.index(("A", n, 0)) % 4 if n < 8 else n % 3

    def bank_user(unit, more):
        n = ring.index(unit) - 4
        while n >= 0 and ring[n][0] == "A" and not more:
            n -= 4
        return ring[n] if n >= 0 else None

    with ExitStack() as sub:
        m = Memory(nc, sub, "la")
        (z_ready, k_unit, k_by_act, k_by_dve, w_done, sub_done, exp_done, kf_ready, ft_used, kv_saved, kv_turned, kv_built,
         q_unit, q_by_act, q_by_dve, xb_done, seen) = (m.sem(n) for n in (
             "z_ready", "k_unit", "k_by_act", "k_by_dve", "w_done", "sub_done", "exp_done", "kf_ready", "ft_used", "kv_saved",
             "kv_turned", "kv_built", "q_unit", "q_by_act", "q_by_dve", "xb_done", "seen"))
        x_in, ve_ready, root_ready, zeroed = (m.sem(n) for n in ("x_in", "ve_ready", "root_ready", "zeroed"))
        pW = [m.ps(f"pW{i}", [P, H * M]) for i in range(2)]
        R = [m.ps(f"R{i}", [P, 512]) for i in range(4)]
        pKV = R[3][:, 0:G * M]
        block = sub.enter_context(nc.Block())

        def batches(eng, first, body):
            first(0)
            with eng.Fori(0, B - 1) as b:
                body(b, True)
            body(B - 1, False)

        @block.sync
        def _(sp):
            xv = io["x"].rearrange("b (t p) d -> b p t d", p=P)
            for b in range(1, B):
                sp.dma_start(X[:, b * TPB:(b + 1) * TPB, :], xv[b]).then_inc(x_in, 16)
                sp.wait_ge(x_in, b * 16)
            for hf in range(2):
                rows = keep["xg"][hf].rearrange("(q n p) d -> q p n d", n=HPT // 4, p=P)
                for n in range(4):
                    sp.dma_start(rows[n], zeros[:, :].unsqueeze(1).broadcast_to([P, HPT // 4, D])).then_inc(zeroed, 16)
                    sp.wait_ge(zeroed, (hf * 4 + n) * 16 + 16)

        @block.vector
        def _(dve):
            v = nc.vector
            dve.sem_inc(sub_done, 2)
            dve.sem_inc(q_by_dve, 1)

            def functions(b):
                def normalise(qd, fs):
                    if qd:
                        dve.wait_ge(k_unit, b * KU + 8 * (qd - 1) + 2)
                    for f in fs:
                        t = b * TPB + qd * 4 + f
                        v.tensor_scalar(z[:, f:f + 1, :], X[:, ds(t, 1), :], mean[:, ds(t, 1)], rstd[:, ds(t, 1)],
                                        ALU.subtract, ALU.mult).then_inc(z_ready, 1)

                def values(qd):
                    for w in range(2):
                        n = 8 * qd + 6 + w
                        dve.wait_ge(k_unit, b * KU + n + 1)
                        v.tensor_tensor(vx[qd % 2][:, 2 * w:2 * w + 2, :, 0:HD], R[k_bank(n)][:, :].rearrange("p (a h e) -> p a h e", a=2, h=H),
                                        vb[:, :].rearrange("p (h e) -> p h e", h=H).unsqueeze(1).broadcast_to([P, 2, H, HD]),
                                        ALU.add).then_inc(k_by_dve, 1)

                def centre(s):
                    dve.wait_ge(w_done, b * (2 * TPB) + s + 1)
                    src = pW[s % 2][:, :].rearrange("p (h m) -> p h m", h=H)
                    v.tensor_reduce(mx[s % 2][:, :], src, AX, ALU.max)
                    dve.drain()
                    old = s - 4
                    if 0 <= old < TPB:
                        dve.wait_ge(ft_used, b * TPB + old + 1)
                    elif old >= TPB:
                        dve.wait_ge(q_unit, b * QU + q_units.index(("Eb", old - TPB, 0)) + 1)
                    v.tensor_tensor(ft[s % 4][:, :].rearrange("p (h m) -> p h m", h=H), src,
                                    mx[s % 2][:, :].unsqueeze(2).broadcast_to([P, H, M]), ALU.subtract).then_inc(sub_done, 1)

                def build_kv():
                    dve.wait_ge(kv_turned, b + 1)
                    for g in range(2):
                        rows = slice(g * M, (g + 1) * M)
                        src = R[3][rows, 0:2 * P].rearrange("p (c e) -> p c e", e=VW)
                        v.tensor_copy(NU[rows, :, g * HD:(g + 1) * HD], src[:, :, 0:HD])
                        last = v.tensor_copy(DE[rows, :, g * HD:(g + 1) * HD], src[:, :, HD:HD + 1].broadcast_to([M, 8, HD]))
                    last.then_inc(kv_built, 1)

                def empty(unit):
                    kind, x, h = unit
                    n = q_units.index(unit)
                    if kind == "D":
                        by_act, count = q_emptied(unit)
                        dve.wait_ge(q_by_act, b * QA + count + 1)
                        v.reciprocal(rd[h][:, :], dn[h][:, :])
                        dve.drain()
                        return
                    dve.wait_ge(q_unit, b * QU + n + 1)
                    src = R[ring.index(unit) % 4]
                    if kind == "N":
                        v.tensor_tensor(oT[x % 2][:, h, :], src[:, :], rd[h][:, :], ALU.mult).then_inc(q_by_dve, 1)
                    else:
                        t = b * TPB + 4 * x + 2 * h
                        v.tensor_tensor(X[:, ds(t, 2), :], X[:, ds(t, 2), :], src[:, :].rearrange("p (a d) -> p a d", a=2), ALU.add)\
                         .then_inc(q_by_dve, 1)
                        dve.drain()
                        for a in range(2):
                            v.bn_stats(st[:, ds(t + a, 1), :], X[:, ds(t + a, 1), :])

                return normalise, values, centre, build_kv, empty

            def first(b):
                normalise, values = functions(b)[:2]
                normalise(0, range(4))
                normalise(1, range(4))
                values(0)

            def body(b, more):
                normalise, values, centre, build_kv, empty = functions(b)
                next_normalise, next_values = functions(b + 1)[:2]
                for s in range(LAST_SLOT + 1):
                    if s < 2 * TPB:
                        centre(s)
                    qd, f = s // 4, s % 4
                    if f and qd + 2 < TPB // 4:
                        normalise(qd + 2, ((), (0, 1), (2,), (3,))[f])
                    if f == 3 and qd + 1 < TPB // 4:
                        values(qd + 1)
                    if s == TPB + 2:
                        build_kv()
                    if s == TPB + 8:
                        dve.wait_ge(xb_done, b * TPB + TPB)
                    for unit in q_slot.get(s, []):
                        if unit[0] not in ("Ea", "Eb", "A"):
                            empty(unit)
                    if more and TPB <= s < 2 * TPB:
                        if s == TPB:
                            dve.wait_ge(x_in, b * 16 + 16)
                        t = (b + 1) * TPB + s - TPB
                        v.bn_stats(st[:, ds(t, 1), :], X[:, ds(t, 1), :])
                    if more and s == 2 * TPB - 1:
                        dve.drain()
                        sl = ds((b + 1) * TPB, TPB)
                        newton_rstd(nc, dve, mean[:, sl], rstd[:, sl], st[:, sl, :], ln, ve_ready, root_ready, b)
                        next_normalise(0, range(4))
                    if more and s == 2 * TPB + 2:
                        next_normalise(1, range(4))
                if more:
                    next_values(0)
            batches(dve, first, body)

        @block.scalar
        def _(act):
            sc = nc.scalar
            act.sem_inc(q_by_act, 1)

            def functions(b):
                def empty_k(n):
                    qd, kind, c = n // 8, n % 8 // 2, n % 2
                    act.wait_ge(k_unit, b * KU + n + 1)
                    if kind == 0:
                        last = sc.activation(zT[:, c, :], R[k_bank(n)][:, :], ACT.Copy)
                    elif kind == 1:
                        last = sc.activation(kT[qd % 2][:, c, :], R[k_bank(n)][:, :], ACT.Identity, bias=kb[:, c:c + 1])
                    else:
                        last = sc.activation(qT[:, qd, c, :], R[k_bank(n)][:, :], ACT.Identity, bias=qb[:, c:c + 1])
                    last.then_inc(k_by_act, 1)

                def empty_q(unit):
                    kind, x, h = unit
                    n = q_units.index(unit)
                    act.wait_ge(q_unit, b * QU + n + 1)
                    if kind in ("Ea", "Eb"):
                        c = 0 if kind == "Ea" else 4
                        sc.activation(FT[x // 4 % 2][:, c:c + 4, x % 4 * P:(x % 4 + 1) * P], R[ring.index(unit) % 4][:, :].rearrange("p (c t) -> p c t", c=4),
                                      ACT.Copy, scale=0.125, bias=FEAT_EPS).then_inc(q_by_act, 1)
                    else:
                        if x:
                            act.wait_ge(q_by_dve, b * QD + q_emptied(("N", x - 1, h))[1] + 1)
                        sc.activation(dn[h][:, :], R[ring.index(unit) % 4][:, :], ACT.Copy, bias=FEAT_EPS).then_inc(q_by_act, 1)

                return empty_k, empty_q

            def first(b):
                empty_k = functions(b)[0]
                for n in range(6):
                    empty_k(n)

            def body(b, more):
                empty_k, empty_q = functions(b)
                next_empty_k = functions(b + 1)[0]
                for s in range(LAST_SLOT + 1):
                    nxt = (s // 4 + 1) * 8 + s % 4 * 2
                    k_units = s % 4 < 3 and nxt < KU
                    if k_units:
                        empty_k(nxt)
                    for unit in q_slot.get(s, []):
                        if unit[0] in ("Ea", "Eb"):
                            empty_q(unit)
                    if s < 2 * TPB:
                        act.wait_ge(sub_done, b * (2 * TPB) + s + 3)
                        sc.activation(ft[s % 4][:, :], ft[s % 4][:, :], ACT.Exp, scale=0.25).then_inc(exp_done, 1)
                    if k_units:
                        empty_k(nxt + 1)
                    if s == TPB + 1:
                        act.wait_ge(ft_used, b * TPB + TPB)
                        sc.activation(kvs[:, :], pKV, ACT.Copy).then_inc(kv_saved, 1)
                    for unit in q_slot.get(s, []):
                        if unit[0] == "D":
                            empty_q(unit)
                        if unit[0] == "A" and more and unit[1] < 6:
                            next_empty_k(unit[1])
                    if more and s == 2 * TPB - 1:
                        act.wait_ge(ve_ready, b + 1)
                        sc.activation(ln["t2"][:, :], ln["ve"][:, :], ACT.Sqrt).then_inc(root_ready, 1)
            batches(act, first, body)

        @block.gpsimd
        def _(pool):
            with pool.Fori(0, B) as b:
                for s in range(TPB):
                    pool.wait_ge(exp_done, b * (2 * TPB) + s + 1)
                    pool.sem_inc(seen, 1)
                    nc.gpsimd.tensor_scalar(ft[s % 4][:, :], ft[s % 4][:, :], 0.125, FEAT_EPS, ALU.mult, ALU.add).then_inc(kf_ready, 1)
                    pool.wait_ge(z_ready, b * TPB + s + 1)
                    pool.sem_inc(seen, 1)
                    nc.gpsimd.tensor_tensor(X[:, ds(b * TPB + s, 1), :], X[:, ds(b * TPB + s, 1), :], pb[:, :].unsqueeze(1), ALU.add).then_inc(xb_done, 1)

        @block.tensor
        def _(pe):
            mm = nc.tensor.matmul

            def functions(b):
                def k_emptied(n):
                    if n % 8 < 6:
                        pe.wait_ge(k_by_act, b * KA + n // 8 * 6 + n % 8 + 1)
                    else:
                        pe.wait_ge(k_by_dve, b * KD + n // 8 * 2 + n % 8 - 5)

                def q_emptied_wait(unit):
                    by_act, count = q_emptied(unit)
                    pe.wait_ge(*((q_by_act, b * QA + count + 1) if by_act else (q_by_dve, b * QD + count + 1)))

                def make_k(n):
                    qd, kind, c = n // 8, n % 8 // 2, n % 2
                    out = R[k_bank(n)]
                    if n >= 11:
                        k_emptied(n - 3)
                    if kind == 0:
                        pe.wait_ge(z_ready, b * TPB + 4 * qd + 4)
                        for f in range(4):
                            last = nc.tensor.transpose(out[:, f * P:(f + 1) * P], z[:, f, c * P:(c + 1) * P], ident[:, :])
                    elif kind < 3:
                        col = (0, D, 0)[kind] + c * P
                        pe.wait_ge(k_by_act, b * KA + 6 * qd + 2)
                        for a in range(DC):
                            last = mm(out[:, :], W[:, a, col:col + P], zT[:, a, :], start=(a == 0), stop=(a == DC - 1))
                    else:
                        for w in range(2):
                            f = 2 * c + w
                            for a in range(DC):
                                last = mm(out[:, w * D:(w + 1) * D], zT[:, a, f * P:(f + 1) * P], W[:, a, 2 * D:3 * D],
                                          start=(a == 0), stop=(a == DC - 1))
                    last.then_inc(k_unit, 1)

                def exponents(s):
                    qd, f = s % TPB // 4, s % 4
                    pe.wait_ge(k_by_act, b * KA + 6 * qd + (4 if s < TPB else 6))
                    pe.wait_ge(sub_done, b * (2 * TPB) + s + 1)
                    src = kT[qd % 2] if s < TPB else qT[:, qd]
                    for c in range(DC):
                        last = mm(pW[s % 2][:, c * 512:(c + 1) * 512], src[:, c, f * P:(f + 1) * P], FM[:, :], start=True, stop=True)
                    last.then_inc(w_done, 1)

                def add_kv(s):
                    qd, f = s // 4, s % 4
                    pe.wait_ge(kf_ready, b * TPB + s + 1)
                    pe.wait_ge(k_by_dve, b * KD + 2 * qd + 2)
                    for blk in range(2):
                        for g in range(2):
                            for j in range(4):
                                h = 8 * blk + 2 * j + g
                                last = mm(pKV[32 * j:32 * j + 32, (2 * blk + g) * M:(2 * blk + g + 1) * M],
                                          vx[qd % 2][:, f, h, :], ft[s % 4][:, h * M:(h + 1) * M],
                                          start=False, stop=True, skip_group_check=True)
                    last.then_inc(ft_used, 1)

                def make_q(unit, more):
                    kind, x, h = unit
                    n = ring.index(unit)
                    out = R[n % 4]
                    user = bank_user(unit, more)
                    if user is not None and user[0] == "A":
                        functions(b + 1)[1](user[1])
                    elif user is not None:
                        q_emptied_wait(user)
                    elif n == 3:
                        pe.wait_ge(kv_built, b + 1)
                    if kind in ("Ea", "Eb"):
                        if kind == "Ea":
                            pe.wait_ge(exp_done, b * (2 * TPB) + TPB + x + 1)
                        for c in range(4):
                            k = c + (4 if kind == "Eb" else 0)
                            last = nc.tensor.transpose(out[:, c * P:(c + 1) * P], ft[x % 4][:, k * P:(k + 1) * P], ident[:, :])
                        last.then_inc(q_unit, 1)
                    elif kind in ("D", "N"):
                        q_emptied_wait(("Eb", 4 * x + 3, 0))
                        for j in range(4):
                            c = 4 * h + j
                            last = mm(out[32 * j:32 * j + 32, :], (NU if kind == "N" else DE)[:, c, :], FT[x % 2][:, c, :], start=True, stop=True)
                        last.then_inc(q_unit, 1)
                    else:
                        pe.wait_ge(q_by_dve, b * QD + q_emptied(("N", x, 1))[1] + 1)
                        for w in range(2):
                            f = 2 * h + w
                            for c in range(DC):
                                last = mm(out[:, w * D:(w + 1) * D], oT[x % 2][:, c, f * P:(f + 1) * P], PW[:, c, :],
                                          start=(c == 0), stop=(c == DC - 1))
                        last.then_inc(q_unit, 1)

                return make_k, k_emptied, exponents, add_kv, q_emptied_wait, make_q

            def first(b):
                make_k, k_emptied = functions(b)[:2]
                for n in range(8):
                    users = [o for o in range(n) if k_bank(o) == k_bank(n)]
                    if users:
                        k_emptied(users[-1])
                    make_k(n)

            def body(b, more):
                make_k, k_emptied, exponents, add_kv, q_emptied_wait, make_q = functions(b)
                next_make_k, next_k_emptied = functions(b + 1)[:2]
                pe.wait_ge(q_by_act, b * QA + 1)
                pe.wait_ge(q_by_dve, b * QD + 1)
                k_emptied(5)
                k_emptied(7)
                mm(pKV, zeros[:, 0:P], zeros[:, :], start=True, stop=True)
                for s in range(LAST_SLOT + 1):
                    if s < 2 * TPB:
                        exponents(s)
                    nxt = (s // 4 + 1) * 8 + s % 4 * 2
                    if nxt < KU:
                        make_k(nxt)
                        make_k(nxt + 1)
                    if 2 <= s < TPB + 2:
                        add_kv(s - 2)
                    if s == TPB + 2:
                        pe.wait_ge(kv_saved, b + 1)
                        pe.wait_ge(k_by_act, b * KA + KA)
                        pe.wait_ge(k_by_dve, b * KD + KD)
                        for h in range(2):
                            last = nc.tensor.transpose(R[3][:, h * P:(h + 1) * P], kvs[:, h * P:(h + 1) * P], ident[:, :])
                        last.then_inc(kv_turned, 1)
                    for unit in q_slot.get(s, []):
                        if unit[0] != "A":
                            make_q(unit, more)
                        elif more:
                            user = bank_user(unit, True)
                            (next_k_emptied(user[1]) if user[0] == "A" else q_emptied_wait(user))
                            next_make_k(unit[1])
            batches(pe, first, body)
    m.clear()


def soft_mixture(nc, mem, io, keep, st):
    X, mean, rstd, ident = keep["X"], keep["mean"], keep["rstd"], keep["ident"]
    QT = TPB // 4
    NP = E0 // 2
    gam, bet = mem.sb("gamma", [P, D]), mem.sb("beta", [P, D])
    scol = mem.sb("scale", [P, 1])
    mu = mem.sb("mu", [P, DC, NS])
    ones = mem.sb("ones", [P, P])
    w1 = mem.sb("w1", [P, DC, E0, HID])
    w2 = mem.sb("w2", [P, NP, D])
    b1 = mem.sb("b1", [P, NP])
    b2 = mem.sb("b2", [E0, D])
    pick = mem.sb("pick", [E0, NS])
    XN = mem.sb("XN", [P, NT, D + 2])
    ss, rn = mem.sb("ss", [P, NT]), mem.sb("rn", [P, NT])
    L = mem.sb("L", [P, TPB, NS])
    cm, mrow = mem.sb("cm", [P, NS]), mem.sb("mrow", [P, NS])
    ccol, dg = mem.sb("ccol", [P, 2]), mem.sb("dg", [P, 2, P])
    nrm = mem.sb("nrm", [P, TPB])
    rs, rr = mem.sb("rs", [P, NT]), mem.sb("rr", [P, NT])
    xnT = [mem.sb(f"xnT{f}", [P, DC, P]) for f in range(4)]
    Ed = [mem.sb(f"Ed{u}", [P, 4, NS]) for u in range(2)]
    si, siT = mem.sb("si", [P, 2, D]), mem.sb("siT", [P, DC, NS])
    rsi = mem.sb("rsi", [P, 2])
    sq, ty, tz = siT, cm, mrow
    Hp = mem.sb("Hp", [P, NP, P])
    SO = mem.sb("SO", [P, 2, D])
    C = [mem.sb(f"C{f}", [P, NS]) for f in range(4)]
    loads, mu_loaded = mem.sem("loads"), mem.sem("mu_loaded")

    made, ss_ready, root_ready, sumd = (mem.sem(n) for n in ("made", "ss_ready", "root_ready", "sumd"))
    with ExitStack() as sub:
        m = Memory(nc, sub, "sm0")
        pSS = m.ps("pSS", [P, NS])
        block = sub.enter_context(nc.Block())

        @block.sync
        def _(sp):
            n = 0
            for dst, src in ((mu[:, :, :], io["mu"].rearrange("(c p) n -> p c n", p=P)),
                             (gam[:, :], io["gamma"].partition_broadcast(P)),
                             (bet[:, :], io["beta"].partition_broadcast(P)),
                             (scol[:, :], io["scale"].partition_broadcast(P)),
                             (w1[:, 0, :, :], io["w1"][:, 0:P, :].rearrange("e p h -> p e h")),
                             (w1[:, 1, :, :], io["w1"][:, P:D, :].rearrange("e p h -> p e h")),
                             (w2[0:HID, :, :], io["w2"].rearrange("(k a) h d -> a h k d", a=2)[0]),
                             (w2[HID:P, :, :], io["w2"].rearrange("(k a) h d -> a h k d", a=2)[1]),
                             (b1[0:HID, :], io["b1"].rearrange("(k a) h -> a h k", a=2)[0]),
                             (b1[HID:P, :], io["b1"].rearrange("(k a) h -> a h k", a=2)[1]),
                             (b2[:, :], io["b2"])):
                with nc.allow_non_contiguous_dma(reason="a bias as columns, once"):
                    sp.dma_start(dst, src).then_inc(loads if n else mu_loaded, 16)
                n += 16
            sp.wait_ge(loads, n - 16)

        @block.gpsimd
        def _(pool):
            nc.gpsimd.memset(pick[:, :], 1.0).then_inc(made, 1)
            pool.wait_ge(made, 1)
            nc.gpsimd.affine_select(out=pick[:, :], in_=pick[:, :], compare_op=ALU.is_ge, fill=0.0,
                                    base=0, pattern=[[1, NS]], channel_multiplier=-S0).then_inc(made, 1)
            pool.wait_ge(made, 2)
            nc.gpsimd.affine_select(out=pick[:, :], in_=pick[:, :], compare_op=ALU.is_ge, fill=0.0,
                                    base=S0 - 1, pattern=[[-1, NS]], channel_multiplier=S0)

        @block.vector
        def _(dve):
            v = nc.vector
            v.memset(ones[:, :], 1.0)
            v.memset(Hp[:, :, :], 0.0)
            v.memset(XN[:, :, D:D + 2], 1.0)
            dve.wait_ge(mu_loaded, 16)
            v.tensor_tensor(sq[:, :, :], mu[:, :, :], mu[:, :, :], ALU.mult).then_inc(ss_ready, 1)
            dve.wait_ge(sumd, 1)
            v.tensor_scalar(ty[:, :], pSS[:, :], 1e-24, None, ALU.max).then_inc(ss_ready, 1)
            dve.wait_ge(root_ready, 1)
            v.reciprocal(tz[:, :], sq[:, 0, :])
            dve.drain()
            v.tensor_tensor(sq[:, 0, :], tz[:, :], tz[:, :], ALU.mult)
            dve.drain()
            v.tensor_tensor(sq[:, 0, :], sq[:, 0, :], ty[:, :], ALU.mult)
            dve.drain()
            v.tensor_scalar(sq[:, 0, :], sq[:, 0, :], -0.5, 1.5, ALU.mult, ALU.add)
            dve.drain()
            v.tensor_tensor(tz[:, :], tz[:, :], sq[:, 0, :], ALU.mult)
            dve.drain()
            v.tensor_tensor(mu[:, :, :], mu[:, :, :], tz[:, :].unsqueeze(1).broadcast_to([P, DC, NS]), ALU.mult)

        @block.scalar
        def _(act):
            act.wait_ge(ss_ready, 2)
            nc.scalar.activation(sq[:, 0, :], ty[:, :], ACT.Sqrt).then_inc(root_ready, 1)

        @block.tensor
        def _(pe):
            pe.wait_ge(ss_ready, 1)
            for c in range(DC):
                last = nc.tensor.matmul(pSS[:, :], ones[:, :], sq[:, c, :], start=(c == 0), stop=(c == DC - 1))
            last.then_inc(sumd, 1)

    xn_ready, sqd, nroot, ssr = (mem.sem(n) for n in ("xn_ready", "sqd", "nroot", "ssr"))
    with ExitStack() as sub:
        block = sub.enter_context(nc.Block())

        @block.vector
        def _(dve):
            v = nc.vector
            with dve.Fori(0, NT // 4) as q:
                for j in range(4):
                    v.scalar_tensor_tensor(XN[:, ds(q * 4 + j, 1), 0:D], X[:, ds(q * 4 + j, 1), :], mean[:, ds(q * 4 + j, 1)],
                                           gam[:, :].unsqueeze(1), ALU.subtract, ALU.mult)
                dve.drain()
                for j in range(4):
                    v.scalar_tensor_tensor(XN[:, ds(q * 4 + j, 1), 0:D], XN[:, ds(q * 4 + j, 1), 0:D], rstd[:, ds(q * 4 + j, 1)],
                                           bet[:, :].unsqueeze(1), ALU.mult, ALU.add).then_inc(xn_ready, 1)
            dve.wait_ge(sqd, NT)
            v.tensor_scalar(ss[:, :], ss[:, :], 1e-24, None, ALU.max).then_inc(ssr, 1)
            dve.wait_ge(nroot, 1)
            v.reciprocal(rn[:, :], rs[:, :])
            dve.drain()
            v.tensor_tensor(rs[:, :], rn[:, :], rn[:, :], ALU.mult)
            dve.drain()
            v.tensor_tensor(rs[:, :], rs[:, :], ss[:, :], ALU.mult)
            dve.drain()
            v.tensor_scalar(rs[:, :], rs[:, :], -0.5, 1.5, ALU.mult, ALU.add)
            dve.drain()
            v.tensor_tensor(rn[:, :], rn[:, :], rs[:, :], ALU.mult)
            dve.drain()
            v.tensor_scalar(rn[:, :], rn[:, :], scol[:, 0:1], None, ALU.mult)

        @block.scalar
        def _(act):
            with act.Fori(0, NT // 4) as q:
                act.drain()
                for j in range(4):
                    act.wait_ge(xn_ready, q * 4 + j + 1)
                    nc.scalar.activation(C[j][:, :], XN[:, ds(q * 4 + j, 1), 0:D], ACT.Square,
                                         accum_out=ss[:, ds(q * 4 + j, 1)]).then_inc(sqd, 1)
            act.wait_ge(ssr, 1)
            nc.scalar.activation(rs[:, :], ss[:, :], ACT.Sqrt).then_inc(nroot, 1)

    with ExitStack() as sub:
        m = Memory(nc, sub, "sm2")
        xs_ready, seen = m.sem("xs_ready"), m.sem("seen")
        XS = [m.sb(f"XS{f}", [P, D]) for f in range(4)]
        trB, xnT_ready, lgB, L_ready = (m.sem(n) for n in ("trB", "xnT_ready", "lgB", "L_ready"))
        cm_ready, cmT, dg_ready, mr_ready = (m.sem(n) for n in ("cm_ready", "cmT", "dg_ready", "mr_ready"))
        sub_done, ed_ready, ed_used = (m.sem(n) for n in ("sub_done", "ed_ready", "ed_used"))
        si_ready, siT_done, siT_ready, h_done, hp_ready, so_done, so_ready = (m.sem(n) for n in (
            "si_ready", "siT_done", "siT_ready", "h_done", "hp_ready", "so_done", "so_ready"))
        C_ready, trD, CT_ready, mmD, x_ready = (m.sem(n) for n in ("C_ready", "trD", "CT_ready", "mmD", "x_ready"))
        pT = [m.ps(f"pT{u}", [P, DC, P]) for u in range(2)]
        pL = [m.ps(f"pL{u}", [P, 2, NS]) for u in range(2)]
        pA = [m.ps(f"pA{h}", [P, 512]) for h in range(2)]
        pM = m.ps("pM", [P, 2, NS])
        pH = m.ps("pH", [P, NP, S0])
        block = sub.enter_context(nc.Block())

        @block.vector
        def _(dve):
            v = nc.vector
            dve.sem_inc(L_ready, 2)
            dve.sem_inc(x_ready, 2)
            with dve.Fori(0, B) as b:
                v.memset(cm[:, :], -3.0e38)

                def logits(i, k):
                    for u in range(2):
                        t = b * TPB + i * 2 + u
                        dve.wait_ge(lgB, t + 5)
                        v.tensor_scalar(L[:, ds(i * 2 + u, 1), :], pL[u][:, 0, :], rn[:, ds(t, 1)], None,
                                        ALU.mult).then_inc(L_ready, 1)
                        dve.drain()
                        v.tensor_tensor(cm[:, :], cm[:, :], L[:, ds(i * 2 + u, 1), :].rearrange("p a n -> p (a n)"), ALU.max)
                dve.drain()
                in_pairs(dve, lambda i, k: None, logits)
                dve.drain().then_inc(cm_ready, 1)
                v.tensor_reduce(nrm[:, :], L[:, :, :], AX, ALU.max, negate=True)
                dve.wait_ge(cmT, b + 1)
                v.tensor_reduce(ccol[:, :], pM[:, 0, :].rearrange("p (h q) -> p h q", h=2), AX, ALU.max)
                dve.drain()
                for h in range(2):
                    last = v.tensor_scalar(dg[:, h, :], ident[:, :], ccol[:, h:h + 1], None, ALU.mult)
                last.then_inc(dg_ready, 1)
                dve.wait_ge(mr_ready, b + 1)
                v.tensor_copy(mrow[:, :], pM[:, 1, :])
                dve.drain()
                for q in range(QT):
                    dve.wait_ge(ed_used, b * QT + q + 1)
                    v.tensor_tensor(Ed[q % 2][:, :, :], L[:, q * 4:q * 4 + 4, :],
                                    mrow[:, :].unsqueeze(1).broadcast_to([P, 4, NS]), ALU.subtract).then_inc(sub_done, 1)
                dve.wait_ge(ed_used, b * QT + QT + 2)
                for h in range(2):
                    v.reciprocal(rsi[:, h:h + 1], pA[h][:, D:D + 1])
                dve.drain()
                for h in range(2):
                    last = v.tensor_scalar(si[:, h, :], pA[h][:, 0:D], rsi[:, h:h + 1], None, ALU.mult)
                last.then_inc(si_ready, 1)
                dve.wait_ge(so_done, b + 1)
                for h in range(2):
                    last = v.tensor_copy(SO[:, h, :], pA[h][:, 0:D])
                last.then_inc(so_ready, 1)

                def add(i, k):
                    for u in range(2):
                        t = b * TPB + i * 2 + u
                        dve.wait_ge(mmD, t + 5)
                        v.reciprocal(rr[:, ds(t, 1)], rs[:, ds(t, 1)])
                        dve.drain()
                        v.scalar_tensor_tensor(X[:, ds(t, 1), :], pL[u][:, 0, :].unsqueeze(1), rr[:, ds(t, 1)],
                                               X[:, ds(t, 1), :], ALU.mult, ALU.add).then_inc(x_ready, 1)
                        dve.drain()
                        v.bn_stats(st[:, ds(t, 1), :], X[:, ds(t, 1), :])
                in_pairs(dve, lambda i, k: None, add)

        @block.scalar
        def _(act):
            s = nc.scalar
            act.sem_inc(xnT_ready, 2)
            act.sem_inc(CT_ready, 2)
            with act.Fori(0, B) as b:
                def turn_in(i, k):
                    for u in range(2):
                        t = b * TPB + i * 2 + u
                        act.wait_ge(trB, t + 5)
                        act.wait_ge(lgB, t + 1)
                        s.activation(xnT[2 * k + u][:, :, :], pT[u][:, :, :], ACT.Copy).then_inc(xnT_ready, 1)
                in_pairs(act, turn_in, lambda i, k: None)
                for q in range(QT):
                    act.wait_ge(sub_done, b * QT + q + 1)
                    s.activation(Ed[q % 2][:, :, :], Ed[q % 2][:, :, :], ACT.Exp).then_inc(ed_ready, 1)
                act.wait_ge(siT_done, b + 1)
                s.activation(siT[:, :, :], pL[0][:, :, :], ACT.Copy).then_inc(siT_ready, 1)
                act.wait_ge(h_done, b + 1)
                for e in range(E0):
                    k, a = e // 2, e % 2
                    col = (e % 8) * S0
                    last = s.activation(Hp[a * HID:(a + 1) * HID, k, col:col + S0], pH[a * HID:(a + 1) * HID, k, :],
                                        ACT.Gelu, bias=b1[a * HID:(a + 1) * HID, k:k + 1])
                last.then_inc(hp_ready, 1)

                def mix(i, k):
                    for u in range(2):
                        t = b * TPB + i * 2 + u
                        act.wait_ge(trD, t + 1)
                        s.activation(C[2 * k + u][:, :].unsqueeze(1), L[:, ds(i * 2 + u, 1), :], ACT.Exp,
                                     bias=nrm[:, ds(i * 2 + u, 1)], accum_out=rs[:, ds(t, 1)]).then_inc(C_ready, 1)

                def turn_out(i, k):
                    for u in range(2):
                        t = b * TPB + i * 2 + u
                        act.wait_ge(trD, t + 5)
                        act.wait_ge(mmD, t + 1)
                        s.activation(xnT[2 * k + u][:, :, :], pT[u][:, :, :], ACT.Copy).then_inc(CT_ready, 1)
                in_pairs(act, mix, turn_out)

        @block.gpsimd
        def _(pool):
            with pool.Fori(0, NT // 4) as q:
                for f in range(4):
                    pool.wait_ge(trB, q * 4 + f + 1)
                    pool.sem_inc(seen, 1)
                    nc.gpsimd.tensor_copy(XS[f][:, :].unsqueeze(1), XN[:, ds(q * 4 + f, 1), 0:D]).then_inc(xs_ready, 1)

        @block.tensor
        def _(pe):
            mm = nc.tensor.matmul
            for sem_, n in ((trB, 4), (lgB, 4), (ed_used, 2), (trD, 4), (mmD, 4)):
                pe.sem_inc(sem_, n)
            with pe.Fori(0, B) as b:
                pe.wait_ge(x_ready, b * TPB + 2)

                def turn(i, k):
                    for u in range(2):
                        t = b * TPB + i * 2 + u
                        pe.wait_ge(xs_ready, t + 1)
                        pe.wait_ge(xnT_ready, t + 1)
                        for c in range(DC):
                            last = nc.tensor.transpose(pT[u][:, c, :], XS[2 * k + u][:, c * P:(c + 1) * P], ident[:, :])
                        last.then_inc(trB, 1)

                def logits(i, k):
                    for u in range(2):
                        t = b * TPB + i * 2 + u
                        pe.wait_ge(xnT_ready, t + 3)
                        pe.wait_ge(L_ready, t + 1)
                        for c in range(DC):
                            last = mm(pL[u][:, 0, :], xnT[2 * k + u][:, c, :], mu[:, c, :], start=(c == 0), stop=(c == DC - 1))
                        last.then_inc(lgB, 1)
                in_pairs(pe, turn, logits)

                pe.wait_ge(cm_ready, b + 1)
                for h in range(2):
                    last = nc.tensor.transpose(pM[:, 0, h * P:(h + 1) * P], cm[:, h * P:(h + 1) * P], ident[:, :])
                last.then_inc(cmT, 1)
                pe.wait_ge(dg_ready, b + 1)
                for h in range(2):
                    last = mm(pM[:, 1, h * P:(h + 1) * P], ones[:, :], dg[:, h, :], start=True, stop=True)
                last.then_inc(mr_ready, 1)
                for q in range(QT):
                    pe.wait_ge(ed_ready, b * QT + q + 1)
                    for j in range(4):
                        for h in range(2):
                            first, end = q + j == 0, q * 4 + j == TPB - 1
                            last = mm(pA[h][:, 0:D + 1].unsqueeze(1), Ed[q % 2][:, j, h * P:(h + 1) * P],
                                      XN[:, ds(b * TPB + q * 4 + j, 1), 0:D + 1], start=first, stop=end)
                    last.then_inc(ed_used, 1)
                pe.wait_ge(si_ready, b + 1)
                for h in range(2):
                    for c in range(DC):
                        last = nc.tensor.transpose(pL[0][:, c, h * P:(h + 1) * P], si[:, h, c * P:(c + 1) * P], ident[:, :])
                last.then_inc(siT_done, 1)
                pe.wait_ge(siT_ready, b + 1)
                for e in range(E0):
                    k, a = e // 2, e % 2
                    for c in range(DC):
                        last = mm(pH[a * HID:(a + 1) * HID, k, :], w1[:, c, e, :], siT[:, c, e * S0:(e + 1) * S0],
                                  start=(c == 0), stop=(c == DC - 1))
                last.then_inc(h_done, 1)
                pe.wait_ge(hp_ready, b + 1)
                for h in range(2):
                    for k in range(4):
                        mm(pA[h][:, 0:D], Hp[:, h * 4 + k, :], w2[:, h * 4 + k, :], start=(k == 0), stop=False)
                    last = mm(pA[h][:, 0:D], pick[:, h * P:(h + 1) * P], b2[:, :], start=False, stop=True)
                last.then_inc(so_done, 1)

                def turn_mix(i, k):
                    for u in range(2):
                        t = b * TPB + i * 2 + u
                        pe.wait_ge(C_ready, t + 1)
                        pe.wait_ge(CT_ready, t + 1)
                        for c in range(2):
                            last = nc.tensor.transpose(pT[u][:, c, :], C[2 * k + u][:, c * P:(c + 1) * P], ident[:, :])
                        last.then_inc(trD, 1)

                def mix(i, k):
                    for u in range(2):
                        t = b * TPB + i * 2 + u
                        pe.wait_ge(CT_ready, t + 3)
                        pe.wait_ge(so_ready, b + 1)
                        pe.wait_ge(x_ready, t + 1)
                        for c in range(2):
                            last = mm(pL[u][:, 0, :], xnT[2 * k + u][:, c, :], SO[:, c, :], start=(c == 0), stop=(c == 1))
                        last.then_inc(mmD, 1)
                in_pairs(pe, turn_mix, mix)
    m.clear()


def project_qkv(nc, mem, io, keep, nn):
    X, mean, rstd, ident = keep["X"], keep["mean"], keep["rstd"], keep["ident"]
    W = mem.sb("W", [P, DC, 3 * D])
    cos, sin = mem.sb("cos", [P, NT, HD // 2]), mem.sb("sin", [P, NT, HD // 2])
    z = [mem.sb(f"z{f}", [P, D]) for f in range(4)]
    zT = [mem.sb(f"zT{f}", [P, DC, P]) for f in range(4)]
    xc = [mem.sb(f"xc{u}", [P, 2 * D]) for u in range(2)]
    xs = [mem.sb(f"xs{u}", [P, 2 * D]) for u in range(2)]
    rqk = [mem.sb(f"rqk{f}", [P, G, 2, 4 * HD]) for f in range(4)]
    rv = [mem.sb(f"rv{f}", [P, G, 4, VW]) for f in range(4)]
    sq = [mem.sb(f"sq{f}", [P, 3, D]) for f in range(4)]
    z_ready, turned, zT_ready, qk_done, v_done, rot_ready, v_ready, rec_ready, sq_ready, own_ready, summed = (mem.sem(n) for n in (
        "z_ready", "turned", "zT_ready", "qk_done", "v_done", "rot_ready", "v_ready", "rec_ready", "sq_ready", "own_ready", "summed"))
    seen = mem.sem("seen")
    w_loaded, angles_loaded = mem.sem("w_loaded"), mem.sem("angles_loaded")
    qk_stored = [mem.sem(f"qk_stored{f}") for f in range(4)]
    v_stored = [mem.sem(f"v_stored{f}") for f in range(4)]
    pT = [mem.ps(f"pT{u}", [P, DC, P]) for u in range(2)]
    pQK = [mem.ps(f"pQK{u}", [P, 2 * D]) for u in range(2)]
    pV = [mem.ps(f"pV{u}", [P, D]) for u in range(2)]
    qk_d = keep["qk"].rearrange("(b g) t p e -> b g t p e", g=G)
    v_d = keep["v"].rearrange("(b g) t p e -> b g t p e", g=G)
    with nc.Block() as block:
        @block.sync
        def _(sp):
            for c in range(3):
                sp.dma_start(W[:, :, c * D:(c + 1) * D],
                             io[("WqT", "WkT", "WvT")[c]].rearrange("(c p) n -> p c n", p=P)).then_inc(w_loaded, 16)
            for b in range(B):
                for dst, src in ((cos, io["cos"]), (sin, io["sin"])):
                    sp.dma_start(dst[:, b * TPB:(b + 1) * TPB, :], src.rearrange("(t p) j -> p t j", p=P)).then_inc(angles_loaded, 16)
            for f in range(4):
                sp.sem_inc(qk_stored[f], 16)
                sp.sem_inc(v_stored[f], 16)
            with sp.Fori(0, B) as b:
                with sp.Fori(0, TPB // 4) as q:
                    for f in range(4):
                        t = b * TPB + q * 4 + f
                        for ready, buf, dram, done in ((rec_ready, rqk[f], qk_d, qk_stored[f]), (v_ready, rv[f], v_d, v_stored[f])):
                            sp.wait_ge(ready, t + 3)
                            sp.dma_start(dram[ds(b, 1), :, ds(q * 4 + f, 1), :, :].rearrange("b g t p e -> p (b g t) e"),
                                         buf[:, :, :, :].rearrange("p g a e -> p g (a e)")).then_inc(done, 16)
            for f in range(4):
                sp.wait_ge(qk_stored[f], 16 + 16 * (NT // 4))
                sp.wait_ge(v_stored[f], 16 + 16 * (NT // 4))

        @block.vector
        def _(dve):
            v = nc.vector
            for f in range(4):
                v.memset(rv[f][:, :, :, :], 0.0)
            dve.drain()
            for f in range(4):
                v.memset(rv[f][:, :, :, HD:HD + 1], 1.0)
            dve.drain().then_inc(z_ready, 1)
            dve.sem_inc(rot_ready, 2)
            dve.wait_ge(angles_loaded, 16 * 2 * B)

            def normalise(t, f):
                dve.wait_ge(turned, t + 1)
                v.tensor_scalar(z[f][:, :].unsqueeze(1), X[:, ds(t, 1), :], mean[:, ds(t, 1)], rstd[:, ds(t, 1)],
                                ALU.subtract, ALU.mult).then_inc(z_ready, 1)

            def rotate(t, f):
                u = f % 2
                src = pQK[u][:, :].rearrange("p (h i a) -> p h i a", h=2 * H, a=2)
                dve.wait_ge(qk_done, t + 1)
                for table, dst in ((cos, xc), (sin, xs)):
                    tab = table[:, ds(t, 1), :].unsqueeze(3).broadcast_to([P, 2 * H, HD // 2, 2])
                    last = v.tensor_tensor(dst[u][:, :].rearrange("p (h i a) -> p h i a", h=2 * H, a=2), src, tab, ALU.mult)
                last.then_inc(rot_ready, 1)
            dve.sem_inc(summed, 4)

            def sums(t, f):
                dve.wait_ge(sq_ready, t + 1)
                dve.wait_ge(own_ready, t + 1)
                v.tensor_reduce(nn[:, ds(t, 1), :], sq[f][:, :, :].rearrange("p a (h e) -> p (a h) e", h=H), AX, ALU.add)\
                 .then_inc(summed, 1)

            def quad(q, *parts):
                for f in range(4):
                    if normalise in parts:
                        normalise(q * 4 + f, f)
                    if sums in parts:
                        sums(q * 4 + f - 8, f)
                    if rotate in parts:
                        dve.wait_ge(rec_ready, q * 4 + f - 3)
                        rotate(q * 4 + f - 4, f)
            quad(0, normalise)
            quad(1, normalise, rotate)
            with dve.Fori(2, NT // 4) as q:
                quad(q, normalise, sums, rotate)
            quad(NT // 4, sums, rotate)
            quad(NT // 4 + 1, sums)

        @block.gpsimd
        def _(pool):
            pool.sem_inc(rec_ready, 2)
            with pool.Fori(0, NT // 4) as q:
                for f in range(4):
                    u = f % 2
                    pool.wait_ge(rot_ready, q * 4 + f + 3)
                    pool.wait_ge(qk_stored[f], q * 16 + 16)
                    pool.sem_inc(seen, 1)
                    c4 = xc[u][:, :].rearrange("p (q g r a) -> p q g r a", q=2, g=G, a=2)
                    s4 = xs[u][:, :].rearrange("p (q g r a) -> p q g r a", q=2, g=G, a=2)
                    out = rqk[f][:, :, :, :].rearrange("p g q (r a) -> p q g r a", a=2)
                    nc.gpsimd.tensor_tensor(out[:, :, :, :, 0], c4[:, :, :, :, 0], s4[:, :, :, :, 1], ALU.subtract)
                    nc.gpsimd.tensor_tensor(out[:, :, :, :, 1], s4[:, :, :, :, 0], c4[:, :, :, :, 1], ALU.add).then_inc(rec_ready, 1)
                    pool.wait_ge(summed, q * 4 + f + 1)
                    pool.wait_ge(rec_ready, q * 4 + f + 3)
                    pool.sem_inc(seen, 1)
                    nc.gpsimd.tensor_tensor(sq[f][:, 2, :].rearrange("p (g e) -> p g e", g=G), rqk[f][:, :, 0, :],
                                            rqk[f][:, :, 1, :], ALU.mult).then_inc(own_ready, 1)

        @block.scalar
        def _(act):
            act.sem_inc(zT_ready, 2)
            act.sem_inc(v_ready, 2)

            def turn(q, f):
                act.wait_ge(turned, q * 4 + f + 5)
                nc.scalar.activation(zT[f][:, :, :], pT[f % 2][:, :, :], ACT.Copy).then_inc(zT_ready, 1)

            def value(q, f):
                act.wait_ge(v_done, q * 4 + f + 1)
                act.wait_ge(v_stored[f], q * 16 + 16)
                nc.scalar.activation(rv[f][:, :, :, 0:HD].rearrange("p g h e -> p (g h) e"),
                                     pV[f % 2][:, :].rearrange("p (h e) -> p h e", h=H), ACT.Copy).then_inc(v_ready, 1)

            def square(q, f):
                act.wait_ge(rec_ready, q * 4 + f + 3)
                act.wait_ge(summed, q * 4 + f + 1)
                nc.scalar.activation(sq[f][:, 0:2, :].rearrange("p q (g e) -> p g q e", g=G), rqk[f][:, :, :, :], ACT.Square).then_inc(sq_ready, 1)

            def quad(q, squares):
                for f in range(4):
                    turn(q, f)
                    if squares:
                        square(q - 1, f)
                    if f:
                        value(q, f - 1)
                value(q, 3)
            quad(0, False)
            with act.Fori(1, NT // 4) as q:
                quad(q, True)
            for f in range(4):
                square(NT // 4 - 1, f)

        @block.tensor
        def _(pe):
            mm = nc.tensor.matmul
            pe.sem_inc(turned, 4)
            pe.wait_ge(w_loaded, 48)
            with pe.Fori(0, NT // 4) as q:
                def turn(f):
                    pe.wait_ge(z_ready, q * 4 + f + 2)
                    pe.wait_ge(zT_ready, q * 4 + f + 1)
                    for c in range(DC):
                        last = nc.tensor.transpose(pT[f % 2][:, c, :], z[f][:, c * P:(c + 1) * P], ident[:, :])
                    last.then_inc(turned, 1)

                def project(f):
                    pe.wait_ge(zT_ready, q * 4 + f + 3)
                    pe.wait_ge(rot_ready, q * 4 + f + 1)
                    for c in range(DC):
                        last = mm(pQK[f % 2][:, :], zT[f][:, c, :], W[:, c, 0:2 * D], start=(c == 0), stop=(c == DC - 1))
                    last.then_inc(qk_done, 1)
                    pe.wait_ge(v_ready, q * 4 + f + 1)
                    for c in range(DC):
                        last = mm(pV[f % 2][:, :], zT[f][:, c, :], W[:, c, 2 * D:3 * D], start=(c == 0), stop=(c == DC - 1))
                    last.then_inc(v_done, 1)
                for f in range(4):
                    turn(f)
                    if f:
                        project(f - 1)
                project(3)


ROOM = 55.0 / HD ** -0.5
LOOSE = 124.0 / HD ** -0.5


def bound_scores(nc, mem, io, keep, nn):
    ident, nmax, need_max = keep["ident"], keep["nmax"], keep["need_max"]
    BH = B * H
    km, kcol, dg = mem.sb("km", [P, BH]), mem.sb("kcol", [BH, 1]), mem.sb("dg", [BH, BH])
    ones = mem.sb("ones", [BH, P])
    bd = mem.sb("bd", [P, NT, H])
    gap, worst, over = mem.sb("gap", [P, 1]), mem.sb("worst", [1, 1]), mem.sb("over", [1, 1])
    km_ready, km_turned, dg_ready, spread, squared, rooted, gap_ready, gap_turned = (mem.sem(n) for n in (
        "km_ready", "km_turned", "dg_ready", "spread", "squared", "rooted", "gap_ready", "gap_turned"))
    pK, pM, pG = mem.ps("pK", [BH, P]), mem.ps("pM", [P, BH]), mem.ps("pG", [1, P])
    q2, k2, own = (nn[:, :, n * H:(n + 1) * H] for n in range(3))
    with nc.Block() as block:
        @block.vector
        def _(dve):
            v = nc.vector
            v.memset(ones[:, :], 1.0)
            for b in range(B):
                v.tensor_reduce(km[:, b * H:(b + 1) * H], k2[:, b * TPB:(b + 1) * TPB, :].rearrange("p t h -> p h t"), AX, ALU.max)
            dve.drain().then_inc(km_ready, 1)
            dve.wait_ge(km_turned, 1)
            v.tensor_reduce(kcol[:, :], pK[:, :], AX, ALU.max)
            dve.drain()
            v.tensor_scalar(dg[:, :], ident[0:BH, 0:BH], kcol[:, 0:1], None, ALU.mult).then_inc(dg_ready, 1)
            dve.wait_ge(spread, 1)
            for b in range(B):
                last = v.tensor_tensor(bd[:, b * TPB:(b + 1) * TPB, :], q2[:, b * TPB:(b + 1) * TPB, :],
                                       pM[:, b * H:(b + 1) * H].unsqueeze(1).broadcast_to([P, TPB, H]), ALU.mult)
            last.then_inc(squared, 1)
            dve.wait_ge(rooted, 1)
            for b in range(B):
                for g in range(G):
                    v.tensor_scalar(nmax[:, b * G + g, :].rearrange("p (t h) -> p t h", h=4),
                                    bd[:, b * TPB:(b + 1) * TPB, g * 4:g * 4 + 4], -1.0, ROOM, ALU.mult, ALU.add)
            dve.drain()
            v.tensor_tensor(bd[:, :, :], bd[:, :, :], own, ALU.subtract)
            dve.drain()
            v.tensor_reduce(gap[:, :], bd[:, :, :].rearrange("p t h -> p (t h)"), AX, ALU.max).then_inc(gap_ready, 1)
            dve.wait_ge(gap_turned, 1)
            v.tensor_reduce(worst[:, :], pG[:, :], AX, ALU.max)
            dve.drain()
            v.tensor_scalar(over[:, :], worst[:, :], LOOSE, None, ALU.is_lt)
            dve.drain()
            v.tensor_scalar(over[:, :], over[:, :], -1.0, 1.0, ALU.mult, ALU.add)
            dve.drain()
            v.tensor_copy(need_max[:, :], over[:, :])

        @block.scalar
        def _(act):
            act.wait_ge(squared, 1)
            nc.scalar.activation(bd[:, :, :], bd[:, :, :], ACT.Sqrt).then_inc(rooted, 1)

        @block.tensor
        def _(pe):
            pe.wait_ge(km_ready, 1)
            nc.tensor.transpose(pK[:, :], km[:, :], ident[:, :]).then_inc(km_turned, 1)
            pe.wait_ge(dg_ready, 1)
            nc.tensor.matmul(pM[:, :], ones[:, :], dg[:, :], start=True, stop=True).then_inc(spread, 1)
            pe.wait_ge(gap_ready, 1)
            nc.tensor.transpose(pG[:, :], gap[:, :], ident[:, :]).then_inc(gap_turned, 1)


TERMS_Q = (0, 0, 0, 1, 1, 2)
TERMS_K = (0, 1, 2, 0, 1, 0)
KR = 6 * HD
KS = KR + 3


class Turner:

    def __init__(self, nc, m, keep, rqk, QT, KT, shifted, pG):
        self.nc, self.keep, self.rqk, self.dst, self.shifted = nc, keep, rqk, (QT, KT), shifted
        self.rep = [[m.sb(f"{x}r{w}", [P, 16, 100], bf16) for w in range(2)] for x in "qk"]
        self.hi, self.mid = m.sb("hi", [P, 4, P], bf16), m.sb("mid", [P, 4, P], bf16)
        self.r1 = m.sb("r1", [P, 4, P])
        self.sh, self.shr = m.sb("sh", [P, 3, 16], bf16), m.sb("shr", [P, 16])
        self.pG = pG
        self.split_done, self.turned, self.evicted = m.sem("split_done"), m.sem("group_turned"), m.sem("group_evicted")

    def begin_dve(self, dve):
        for w in range(2):
            self.nc.vector.memset(self.rep[0][w][:, :, KR:100], 0.0)
            self.nc.vector.memset(self.rep[1][w][:, :, KR:100], 1.0)
        dve.sem_inc(self.evicted, 1)

    def split(self, dve, n, qd):
        v, hi, mid, r1 = self.nc.vector, self.hi, self.mid, self.r1
        src = self.rqk[:, qd * 4:qd * 4 + 4, :]
        v.tensor_copy(hi[:, :, :], src)
        if self.shifted:
            cur = self.keep["nmax"][:, ds(n, 1), qd * 16:qd * 16 + 16]
            sh, shr = self.sh, self.shr
            v.tensor_copy(sh[:, 0:1, :], cur)
        dve.drain()
        v.tensor_tensor(r1[:, :, :], src, hi[:, :, :], ALU.subtract)
        if self.shifted:
            v.tensor_tensor(shr[:, :].unsqueeze(1), cur, sh[:, 0:1, :], ALU.subtract)
        dve.drain()
        v.tensor_copy(mid[:, :, :], r1[:, :, :])
        if self.shifted:
            v.tensor_copy(sh[:, 1, :], shr[:, :])
        dve.drain()
        v.tensor_tensor(r1[:, :, :], r1[:, :, :], mid[:, :, :], ALU.subtract)
        if self.shifted:
            v.tensor_tensor(sh[:, 2, :], shr[:, :], sh[:, 1, :], ALU.subtract)
        for x, terms in enumerate((TERMS_Q, TERMS_K)):
            rep = self.rep[x][qd % 2]
            for part, from_ in ((0, hi), (1, mid), (2, r1)):
                s = from_[:, :, x * 64:(x + 1) * 64].rearrange("p t (h e) -> p t h e", h=4)
                if part == 2:
                    dve.drain()
                for slot in [n for n, w in enumerate(terms) if w == part]:
                    d = rep[:, :, slot * HD:(slot + 1) * HD].rearrange("p (t h) e -> p t h e", t=4)
                    v.tensor_copy(d, s)
        if self.shifted:
            for n in range(3):
                v.tensor_copy(self.rep[0][qd % 2][:, :, KR + n:KR + n + 1], self.sh[:, n, :].unsqueeze(2))
        dve.drain().then_inc(self.split_done, 1)

    def turn(self, pe, n, qd, gi):
        x, half = gi % 2, gi // 2
        rows = 100 if self.shifted else KR
        pe.wait_ge(self.split_done, n * 4 + qd + 1)
        pe.wait_ge(self.evicted, n * 16 + qd * 4 + gi + 1)
        for h in range(4):
            for t in range(2):
                last = self.nc.tensor.transpose(self.pG[0:rows, h * 2 + t, :],
                                                self.rep[x][qd % 2][:, (half * 2 + t) * 4 + h, 0:rows],
                                                self.keep["identb"][:, :])
        last.then_inc(self.turned, 1)

    def evict(self, dve, n, qd, gi, par):
        x, half = gi % 2, gi // 2
        rows = 100 if self.shifted else KR
        col = (qd * 4 + half * 2) * P
        dve.wait_ge(self.turned, n * 16 + qd * 4 + gi + 1)
        self.nc.vector.tensor_copy(self.dst[x][par][0:rows, :, col:col + 2 * P],
                                   self.pG[0:rows, :, :].rearrange("p (h t) q -> p h (t q)", t=2)).then_inc(self.evicted, 1)


def row_maxima(nc, mem, io, keep):
    nmax, identb, need_max = keep["nmax"], keep["identb"], keep["need_max"]
    rqk = mem.sb("rqk", [P, TPB, P])
    QT, KT = [mem.sb("QT", [P, 4, N], bf16)], [mem.sb("KT", [P, 4, N], bf16)]
    mask = mem.sb("mask", [P, P], bf16)
    pm = mem.sb("pm", [P, TPB, 4, 2])
    T = Turner(nc, mem, keep, rqk, QT, KT, False, mem.ps("pG", [P, 8, P], bf16))
    made, loaded, scored, reduced, mx_done = (mem.sem(n) for n in ("made", "loaded", "scored", "reduced", "mx_done"))
    pS = [mem.ps(f"pS{s}", [P, 1024]) for s in range(3)]
    units = [(t, h, k) for t in range(TPB) for h in range(4) for k in range(1 + t // 8)]
    U = len(units)
    assert U % 3 == 0
    with nc.Block() as block:
        @block.gpsimd
        def _(pool):
            nc.gpsimd.memset(mask[:, :], 0.0).then_inc(made, 1)
            pool.wait_ge(made, 1)
            nc.gpsimd.affine_select(out=mask[:, :], in_=mask[:, :], compare_op=ALU.is_ge, fill=MASKED,
                                    base=0, pattern=[[-1, P]], channel_multiplier=1).then_inc(made, 1)

        @block.sync
        def _(sp):
            need = sp.value_load(need_max[0:1, 0:1], min_val=0, max_val=1)
            with sp.If(need > 0):
                with sp.Fori(0, B) as b:
                    for g in range(G):
                        n = b * G + g
                        sp.wait_ge(mx_done, n + 1)
                        for half in (slice(0, TPB // 2), slice(TPB // 2, TPB)):
                            sp.dma_start(rqk[:, half, :], keep["qk"][ds(n, 1), half, :, :].rearrange("i t p e -> p (i t) e")).then_inc(loaded, 16)

        @block.vector
        def _(dve):
            need = dve.value_load(need_max[0:1, 0:1], min_val=0, max_val=1)
            with dve.If(need > 0):
                v = nc.vector
                T.begin_dve(dve)
                dve.sem_inc(reduced, 3)
                dve.sem_inc(mx_done, 1)
                with dve.Fori(0, B) as b:
                    for g in range(G):
                        n = b * G + g
                        dve.wait_ge(loaded, n * 32 + 32)
                        for qd in range(4):
                            T.split(dve, n, qd)
                            for gi in range(4):
                                T.evict(dve, n, qd, gi, 0)
                        for i, (t, h, k) in enumerate(units):
                            width = min(1024, (t + 1) * P - k * 1024)
                            dve.wait_ge(scored, n * U + i + 1)
                            v.tensor_reduce(pm[:, t, h, k:k + 1], pS[i % 3][:, 0:width], AX, ALU.max).then_inc(reduced, 1)
                        dve.drain()
                        v.tensor_tensor(pm[:, 8:16, :, 0], pm[:, 8:16, :, 0], pm[:, 8:16, :, 1], ALU.max)
                        dve.drain()
                        v.tensor_scalar(nmax[:, ds(n, 1), :].rearrange("p i (t h) -> p (i t) h", h=4), pm[:, :, :, 0], -1.0, None, ALU.mult).then_inc(mx_done, 1)

        @block.tensor
        def _(pe):
            need = pe.value_load(need_max[0:1, 0:1], min_val=0, max_val=1)
            with pe.If(need > 0):
                pe.wait_ge(made, 2)
                with pe.Fori(0, B) as b:
                    for g in range(G):
                        n = b * G + g
                        for qd in range(4):
                            for gi in range(4):
                                T.turn(pe, n, qd, gi)
                        pe.wait_ge(T.evicted, n * 16 + 17)
                        for i, (t, h, k) in enumerate(units):
                            width = min(1024, (t + 1) * P - k * 1024)
                            pe.wait_ge(reduced, n * U + i + 1)
                            for c in range(0, width, 512):
                                w = min(512, width - c)
                                key = k * 1024 + c
                                diag = key + w == (t + 1) * P
                                last = nc.tensor.matmul(pS[i % 3][:, c:c + w], QT[0][0:KR, h, t * P:(t + 1) * P],
                                                        KT[0][0:KR, h, key:key + w], start=True, stop=not diag)
                                if diag:
                                    last = nc.tensor.matmul(pS[i % 3][:, c + w - P:c + w], identb[:, :], mask[:, :], start=False, stop=True)
                            last.then_inc(scored, 1)


def attention(nc, mem, io, keep):
    ident, identb = keep["ident"], keep["identb"]
    QC = N // 512
    STEPS = [(c, kb) for c in range(QC) for kb in range(4 * c + 4)]
    NST = len(STEPS)
    LAST = [STEPS.index((c, 4 * c + 3)) for c in range(QC)]
    UNITS, PLACE = [], {}
    for n, (c, kb) in enumerate(STEPS):
        width = 512 - max(0, kb - 4 * c) * P
        per = min(4, 1024 // width) if width <= 256 else 2
        for first in range(0, 4, per):
            for h in range(first, first + per):
                PLACE[n, h] = (len(UNITS), (h - first) * width // 512 if per == 4 else h - first, (h - first) * width % 512 if per == 4 else 0)
            UNITS.append((n, range(first, first + per), per * width // 512 if per == 4 else 2, 512 if per == 4 else width))
    NU = len(UNITS)
    AHEAD = 6
    assert NU % 6 == 0
    rqk = mem.sb("rqk", [P, TPB, P])
    V = [mem.sb(f"V{k}", [P, TPB, P]) for k in range(2)]
    QT = [mem.sb(f"QT{k}", [P, 4, N], bf16) for k in range(2)]
    KT = [mem.sb(f"KT{k}", [P, 4, N], bf16) for k in range(2)]
    PT = [mem.sb(f"PT{s}", [P, 2, 512]) for s in range(6)]
    mask = mem.sb("mask", [P, P], bf16)
    OT = [mem.sb(f"OT{s}", [P, 512]) for s in range(2)]
    rc = mem.sb("rc", [P, 4, 4])
    ob = [mem.sb(f"ob{s}", [P, 4, 4, HD]) for s in range(2)]
    made, qk_loaded, scored, exp_done, pv_done, out_copied, out_turned, divided = (mem.sem(n) for n in (
        "made", "qk_loaded", "scored", "exp_done", "pv_done", "out_copied", "out_turned", "divided"))
    v_loaded = [mem.sem(f"v_loaded{k}") for k in range(2)]
    stored = [mem.sem(f"stored{s}") for s in range(2)]
    pS = [mem.ps(f"pS{s}", [P, 2, 512]) for s in range(3)]
    pO = mem.ps("pO", [P, 512])
    bank = mem.ps("bank", [P, 512])
    pY = bank[:, :].rearrange("p (q e) -> p q e", q=4)
    T = Turner(nc, mem, keep, rqk, QT, KT, True, bank[:, :].bitcast(bf16).rearrange("p (a e) -> p a e", a=8))
    NIT = B * G

    def iterations(eng, first, body):
        first()
        with eng.Fori(0, NIT // 2 - 1) as j:
            body(j * 2, 0, j, True)
            body(j * 2 + 1, 1, j, True)
        body(NIT - 2, 0, NIT // 2 - 1, True)
        body(NIT - 1, 1, NIT // 2 - 1, False)

    with nc.Block() as block:
        @block.gpsimd
        def _(pool):
            nc.gpsimd.memset(mask[:, :], 0.0).then_inc(made, 1)
            pool.wait_ge(made, 1)
            nc.gpsimd.affine_select(out=mask[:, :], in_=mask[:, :], compare_op=ALU.is_ge, fill=MASKED,
                                    base=0, pattern=[[1, P]], channel_multiplier=-1).then_inc(made, 1)

        @block.sync
        def _(sp):
            for s in range(2):
                sp.sem_inc(stored[s], 16)

            def load(it, par):
                for dst, src, done in ((rqk, keep["qk"], qk_loaded), (V[par], keep["v"], v_loaded[par])):
                    for half in (slice(0, TPB // 2), slice(TPB // 2, TPB)):
                        sp.dma_start(dst[:, half, :], src[ds(it, 1), half, :, :].rearrange("i t p e -> p (i t) e")).then_inc(done, 16)

            def body(it, par, j, more):
                if more:
                    sp.wait_ge(T.split_done, it * 4 + 4)
                    sp.wait_ge(pv_done, it * NST + AHEAD)
                    load(it + 1, 1 - par)
                for c in range(QC):
                    sp.wait_ge(divided, it * QC + c + 2)
                    sp.dma_start(keep["ao"][ds(it * QC + c, 1), :, :, :].rearrange("n q p e -> p (n q) e"),
                                 ob[c % 2][:, :, :, :].rearrange("p q h e -> p q (h e)")).then_inc(stored[c % 2], 16)
            iterations(sp, lambda: load(0, 0), body)
            for s in range(2):
                sp.wait_ge(stored[s], 16 + 16 * NIT * QC // 2)

        @block.vector
        def _(dve):
            v = nc.vector
            T.begin_dve(dve)
            dve.sem_inc(out_copied, 2)
            dve.sem_inc(divided, 1)

            def finish(it, c):
                s = c % 2
                dve.wait_ge(pv_done, it * NST + LAST[c] + 1 + AHEAD)
                v.tensor_copy(OT[s][:, :], pO[:, :]).then_inc(out_copied, 1)
                dve.wait_ge(out_turned, it * QC + c + 1)
                y = pY[:, :, :].rearrange("p q (h e) -> p q h e", h=4)
                v.reciprocal(rc[:, :, :], y[:, :, :, HD])
                dve.drain()
                dve.wait_ge(stored[s], (it * 2 + c // 2) * 16 + 16)
                v.tensor_tensor(ob[s][:, :, :, :], y[:, :, :, 0:HD], rc[:, :, :].unsqueeze(3).broadcast_to([P, 4, 4, HD]),
                                ALU.mult).then_inc(divided, 1)

            def evict(n, qd, par):
                for gi in range(4):
                    T.evict(dve, n, qd, gi, par)

            def first():
                dve.wait_ge(qk_loaded, 32)
                for qd in range(4):
                    T.split(dve, 0, qd)
                    evict(0, qd, 0)

            def body(it, par, j, more):
                n = it + 1
                finish(it, 0)
                if more:
                    dve.wait_ge(qk_loaded, it * 32 + 64)
                    T.split(dve, n, 0)
                    T.split(dve, n, 1)
                finish(it, 1)
                if more:
                    dve.wait_ge(pv_done, it * NST + AHEAD)
                    evict(n, 0, 1 - par)
                    T.split(dve, n, 2)
                    evict(n, 1, 1 - par)
                finish(it, 2)
                if more:
                    T.split(dve, n, 3)
                    evict(n, 2, 1 - par)
                    evict(n, 3, 1 - par)
                finish(it, 3)
            iterations(dve, first, body)

        @block.scalar
        def _(act):
            act.sem_inc(exp_done, 3)

            def body(it, par, j, more):
                for u, (n, _, banks, width) in enumerate(UNITS):
                    act.wait_ge(scored, it * NU + u + 1)
                    user = UNITS[u - 6][0] if u >= 6 else UNITS[u - 6][0] - NST
                    act.wait_ge(pv_done, it * NST + user + 1 + AHEAD)
                    nc.scalar.activation(PT[u % 6][:, 0:banks, 0:width], pS[u % 3][:, 0:banks, 0:width], ACT.Exp,
                                         scale=HD ** -0.5).then_inc(exp_done, 1)
            iterations(act, lambda: None, body)

        @block.tensor
        def _(pe):
            mm = nc.tensor.matmul
            pe.sem_inc(pv_done, AHEAD)
            pe.wait_ge(made, 2)

            def scores(it, par, n):
                c, kb = STEPS[n]
                off = max(0, kb - 4 * c) * P
                for u, (of, heads, _, _) in enumerate(UNITS):
                    if of != n:
                        continue
                    pe.wait_ge(exp_done, it * NU + u + 1)
                    for h in heads:
                        _, b, col = PLACE[n, h]
                        last = mm(pS[u % 3][:, b, col:col + 512 - off], KT[par][0:KS, h, kb * P:(kb + 1) * P],
                                  QT[par][0:KS, h, c * 512 + off:(c + 1) * 512], start=True, stop=kb < 4 * c)
                        if kb >= 4 * c:
                            last = mm(pS[u % 3][:, b, col:col + P], identb[:, :], mask[:, :], start=False, stop=True)
                    last.then_inc(scored, 1)

            def values(it, par, n):
                c, kb = STEPS[n]
                off = max(0, kb - 4 * c) * P
                if kb == 0:
                    pe.wait_ge(out_copied, it * QC + c + 2)
                pe.wait_ge(exp_done, it * NU + PLACE[n, 3][0] + 4)
                for h in range(4):
                    u, b, col = PLACE[n, h]
                    last = mm(pO[32 * h:32 * h + 32, off:512], V[par][:, kb, 32 * h:32 * h + 32],
                              PT[u % 6][:, b, col:col + 512 - off], start=(kb == 0), stop=(kb == 4 * c + 3))
                last.then_inc(pv_done, 1)

            def turn_out(it, c, groups):
                pe.wait_ge(out_copied, it * QC + c + 3)
                pe.wait_ge(divided, it * QC + c + 1)
                pe.wait_ge(T.evicted, it * 16 + 16 + groups + 1)
                for q in range(4):
                    last = nc.tensor.transpose(pY[:, q, :], OT[c % 2][:, q * P:(q + 1) * P], ident[:, :])
                last.then_inc(out_turned, 1)

            def first():
                for qd in range(4):
                    for gi in range(4):
                        T.turn(pe, 0, qd, gi)

            extra = {}
            for c in range(1, QC):
                extra.setdefault((c, 1), []).append(("out", c - 1))
            for qd, (c, kb) in enumerate(((2, 2), (2, 8), (3, 4), (3, 9))):
                for gi in range(4):
                    extra.setdefault((c, kb + gi), []).append((qd, gi))

            def body(it, par, j, more):
                pe.wait_ge(T.evicted, it * 16 + 17)
                pe.wait_ge(v_loaded[par], j * 32 + 32)
                groups = 0
                for n, (c, kb) in enumerate(STEPS):
                    scores(it, par, n)
                    if n:
                        values(it, par, n - 1)
                    for what, x in extra.get((c, kb), []):
                        if what == "out":
                            turn_out(it, x, groups)
                        elif more:
                            pe.wait_ge(divided, it * QC + c + 1)
                            T.turn(pe, it + 1, what, x)
                            groups += 1
                values(it, par, NST - 1)
                turn_out(it, QC - 1, groups)
            iterations(pe, first, body)


def project_out(nc, mem, io, keep, st):
    X, ident = keep["X"], keep["ident"]
    W = mem.sb("W", [P, DC, D])
    a = [mem.sb(f"a{k}", [P, 4, G, 4 * HD]) for k in range(2)]
    aT = [mem.sb(f"aT{f}", [P, DC, P]) for f in range(4)]
    w_loaded, turned, aT_ready, projected, x_ready = (mem.sem(n) for n in (
        "w_loaded", "turned", "aT_ready", "projected", "x_ready"))
    a_loaded = [mem.sem(f"a_loaded{k}") for k in range(2)]
    pT = [mem.ps(f"pT{u}", [P, DC, P]) for u in range(2)]
    pP = [mem.ps(f"pP{u}", [P, D]) for u in range(2)]
    with nc.Block() as block:
        @block.sync
        def _(sp):
            sp.dma_start(W[:, :, :], io["WoT"].rearrange("(c p) n -> p c n", p=P)).then_inc(w_loaded, 16)
            with sp.Fori(0, B) as b:
                for c in range(4):
                    k = c % 2
                    sp.wait_ge(turned, (b * 4 + c) * 4 + 4)
                    for g in range(G):
                        sp.dma_start(a[k][:, :, g, :], keep["ao"][ds(b * 16 + g * 4 + c, 1), :, :, :].rearrange("n q p e -> p (n q) e"))\
                          .then_inc(a_loaded[k], 16)

        @block.vector
        def _(dve):
            dve.sem_inc(x_ready, 2)
            with dve.Fori(0, NT // 4) as q:
                for f in range(4):
                    t = q * 4 + f
                    dve.wait_ge(projected, t + 1)
                    nc.vector.tensor_tensor(X[:, ds(t, 1), :], X[:, ds(t, 1), :], pP[f % 2][:, :].unsqueeze(1), ALU.add).then_inc(x_ready, 1)
                    dve.drain()
                    nc.vector.bn_stats(st[:, ds(t, 1), :], X[:, ds(t, 1), :])

        @block.scalar
        def _(act):
            act.sem_inc(aT_ready, 2)
            with act.Fori(0, NT // 4) as q:
                for f in range(4):
                    act.wait_ge(turned, q * 4 + f + 9)
                    nc.scalar.activation(aT[f][:, :, :], pT[f % 2][:, :, :], ACT.Copy).then_inc(aT_ready, 1)

        @block.tensor
        def _(pe):
            pe.sem_inc(turned, 8)
            pe.wait_ge(w_loaded, 16)
            with pe.Fori(0, NT // 8) as q:
                for k in range(2):
                    def turn(f):
                        pe.wait_ge(aT_ready, q * 8 + k * 4 + f + 1)
                        av = a[k][:, f, :, :].rearrange("p g e -> p (g e)")
                        for c in range(DC):
                            last = nc.tensor.transpose(pT[f % 2][:, c, :], av[:, c * P:(c + 1) * P], ident[:, :])
                        last.then_inc(turned, 1)

                    def project(f):
                        pe.wait_ge(aT_ready, q * 8 + k * 4 + f + 3)
                        pe.wait_ge(x_ready, q * 8 + k * 4 + f + 1)
                        for c in range(DC):
                            last = nc.tensor.matmul(pP[f % 2][:, :], aT[f][:, c, :], W[:, c, :], start=(c == 0), stop=(c == DC - 1))
                        last.then_inc(projected, 1)
                    pe.wait_ge(a_loaded[k], q * (16 * G) + 16 * G)
                    for f in range(4):
                        turn(f)
                        if f:
                            project(f - 1)
                    project(3)


HT = NT // 2
HPT = 2 * HT + E1


def route(nc, mem, io, keep):
    X, mean, rstd, ident = keep["X"], keep["mean"], keep["rstd"], keep["ident"]
    wt, dest, which = keep["wt"], keep["dest"], keep["which"]
    R = mem.sb("R", [P, DC, E1])
    z = [mem.sb(f"z{f}", [P, D]) for f in range(4)]
    zT = [mem.sb(f"zT{f}", [P, DC, P]) for f in range(4)]
    rw = mem.sb("rw", [P, NT, E1])
    M1, M2 = mem.sb("M1", [P, NT, E1]), mem.sb("M2", [P, NT, E1])
    t1, t2 = mem.sb("t1", [P, NT, E1]), mem.sb("t2", [P, NT, E1])
    Mb = mem.sb("Mb", [P, NT, E1], bf16)
    before, onesb = mem.sb("before", [P, P], bf16), mem.sb("onesb", [P, P], bf16)
    code = mem.sb("code", [P, E1])
    row = mem.sb("row", [P, HPT])
    s1, s2 = mem.sb("s1", [P, NT]), mem.sb("s2", [P, NT])
    n1, n2, nt = (mem.sb(n, [P, 2, E1]) for n in ("n1", "n2", "nt"))
    ni = mem.sb("ni", [P, 2, E1], mybir.dt.int32)
    wf = mem.sb("wf", [1, 2, HPT])
    codei, rowi = mem.sb("codei", [P, E1], mybir.dt.int32), mem.sb("rowi", [P, HPT], mybir.dt.int32)
    z_ready, turned, zT_ready, l_done, l_ready, made, w_loaded = (mem.sem(n) for n in (
        "z_ready", "turned", "zT_ready", "l_done", "l_ready", "made", "w_loaded"))
    less_max, exps, chosen, ranked = (mem.sem(n) for n in ("less_max", "exps", "chosen", "ranked"))

    with ExitStack() as sub:
        m = Memory(nc, sub, "rt1")
        pT = [m.ps(f"pT{u}", [P, DC, P]) for u in range(2)]
        pR = [m.ps(f"pR{u}", [P, E1]) for u in range(2)]
        block = sub.enter_context(nc.Block())

        @block.sync
        def _(sp):
            sp.dma_start(R[:, :, :], io["routerT"].rearrange("(c p) n -> p c n", p=P)).then_inc(w_loaded, 16)

        @block.gpsimd
        def _(pool):
            g = nc.gpsimd
            g.memset(before[:, :], 1.0).then_inc(made, 1)
            g.memset(onesb[:, :], 1.0)
            pool.wait_ge(made, 1)
            g.affine_select(out=before[:, :], in_=before[:, :], compare_op=ALU.is_gt, fill=0.0,
                            base=0, pattern=[[1, P]], channel_multiplier=-1)
            g.iota(codei[:, :], pattern=[[-1, E1]], base=E1, channel_multiplier=0)
            g.iota(rowi[:, :], pattern=[[1, HPT]], base=0, channel_multiplier=0)

        @block.vector
        def _(dve):
            dve.sem_inc(l_ready, 2)

            def normalise(q):
                for f in range(4):
                    dve.wait_ge(turned, q * 4 + f + 1)
                    nc.vector.tensor_scalar(z[f][:, :].unsqueeze(1), X[:, ds(q * 4 + f, 1), :], mean[:, ds(q * 4 + f, 1)],
                                            rstd[:, ds(q * 4 + f, 1)], ALU.subtract, ALU.mult).then_inc(z_ready, 1)

            def logits(q):
                for f in range(4):
                    dve.wait_ge(l_done, q * 4 + f + 1)
                    nc.vector.tensor_copy(rw[:, ds(q * 4 + f, 1), :], pR[f % 2][:, :].unsqueeze(1)).then_inc(l_ready, 1)
            normalise(0)
            with dve.Fori(1, NT // 4) as q:
                normalise(q)
                logits(q - 1)
            logits(NT // 4 - 1)

        @block.scalar
        def _(act):
            act.sem_inc(zT_ready, 2)
            with act.Fori(0, NT // 4) as q:
                for f in range(4):
                    act.wait_ge(turned, q * 4 + f + 5)
                    nc.scalar.activation(zT[f][:, :, :], pT[f % 2][:, :, :], ACT.Copy).then_inc(zT_ready, 1)

        @block.tensor
        def _(pe):
            pe.sem_inc(turned, 4)
            pe.wait_ge(w_loaded, 16)
            with pe.Fori(0, NT // 4) as q:
                def turn(f):
                    pe.wait_ge(z_ready, q * 4 + f + 1)
                    pe.wait_ge(zT_ready, q * 4 + f + 1)
                    for c in range(DC):
                        last = nc.tensor.transpose(pT[f % 2][:, c, :], z[f][:, c * P:(c + 1) * P], ident[:, :])
                    last.then_inc(turned, 1)

                def logits(f):
                    pe.wait_ge(zT_ready, q * 4 + f + 3)
                    pe.wait_ge(l_ready, q * 4 + f + 1)
                    for c in range(DC):
                        last = nc.tensor.matmul(pR[f % 2][:, :], zT[f][:, c, :], R[:, c, :], start=(c == 0), stop=(c == DC - 1))
                    last.then_inc(l_done, 1)
                for f in range(4):
                    turn(f)
                    if f:
                        logits(f - 1)
                logits(3)

    with ExitStack() as sub:
        m = Memory(nc, sub, "rt2")
        pB = m.ps("pB", [P, NT * E1])
        pC = m.ps("pC", [P, NT * E1])
        block = sub.enter_context(nc.Block())
        wide = lambda a: a.unsqueeze(2).broadcast_to([P, NT, E1])
        per = lambda a: a.unsqueeze(1).broadcast_to([P, NT, E1])

        @block.vector
        def _(dve):
            v = nc.vector

            def step(*ops):
                for op in ops:
                    op()
                dve.drain()
            A = lambda t: t[:, :, :]
            tt = lambda o, a, b, op: (lambda: v.tensor_tensor(o, a, b, op))
            ts = lambda o, a, s, op, s2=None, op2=ALU.bypass: (lambda: v.tensor_scalar(o, a, s, s2, op, op2))
            red = lambda o, a, op: (lambda: v.tensor_reduce(o, a, AX, op))
            step(red(s1[:, :], A(rw), ALU.max), lambda: v.tensor_copy(code[:, :], codei[:, :]), lambda: v.tensor_copy(row[:, :], rowi[:, :]))
            step(tt(A(rw), A(rw), wide(s1[:, :]), ALU.subtract))
            dve.drain().then_inc(less_max, 1)
            dve.wait_ge(exps, 1)
            step(red(s1[:, :], A(rw), ALU.add))
            step(lambda: v.reciprocal(s1[:, :], s1[:, :]))
            step(tt(A(rw), A(rw), wide(s1[:, :]), ALU.mult))
            for k, Mk in enumerate((M1, M2)):
                src = rw if k == 0 else t2
                best = wt[:, k, :]
                step(red(best, A(src), ALU.max))
                step(tt(A(t1), A(src), wide(best), ALU.is_equal))
                step(tt(A(t1), A(t1), per(code[:, :]), ALU.mult))
                step(red(s1[:, :], A(t1), ALU.max))
                step(tt(A(Mk), per(code[:, :]), wide(s1[:, :]), ALU.is_equal))
                if k == 0:
                    step(ts(A(t1), A(M1), 2.0, ALU.mult))
                    step(tt(A(t2), A(rw), A(t1), ALU.subtract))
            step(tt(A(Mb), A(M1), A(M2), ALU.add))
            dve.drain().then_inc(chosen, 1)
            dve.wait_ge(ranked, 1)
            pc = pC[:, :].rearrange("p (t e) -> p t e", e=E1)
            pb = pB[:, :].rearrange("p (t e) -> p t e", e=E1)
            step(lambda: v.tensor_copy(A(t1), pc))
            a, c = t1, t2
            n = 1
            while n < NT:
                step(tt(c[:, n:, :], a[:, n:, :], a[:, :NT - n, :], ALU.add), lambda n=n, a=a, c=c: v.tensor_copy(c[:, :n, :], a[:, :n, :]))
                a, c = c, a
                n *= 2
            first = a[:, HT - 1:HT, :]
            step(ts(nt[:, :, :], a[:, HT - 1:NT:HT, :], float(P - 1), ALU.add))
            step(tt(nt[:, 1:2, :], nt[:, 1:2, :], first, ALU.subtract))
            step(lambda: v.tensor_copy(A(ni), A(nt)))
            step(ts(A(ni), A(ni), 7, ALU.arith_shift_right))
            step(lambda: v.tensor_copy(A(nt), A(ni)), lambda: v.tensor_copy(A(n1), A(ni)))
            x, y = n1, n2
            n = 1
            while n < E1:
                step(tt(y[:, :, n:], x[:, :, n:], x[:, :, :E1 - n], ALU.add), lambda n=n, x=x, y=y: v.tensor_copy(y[:, :, :n], x[:, :, :n]))
                x, y = y, x
                n *= 2
            step(tt(A(nt), A(x), A(nt), ALU.subtract))
            step(ts(A(nt), A(nt), float(P), ALU.mult))
            step(tt(nt[:, 1:2, :], nt[:, 1:2, :], first, ALU.subtract))
            step(tt(A(c), A(a), pc, ALU.subtract))
            step(tt(A(c), A(c), pb, ALU.add))
            step(*(tt(a[:, hf * HT:(hf + 1) * HT, :], c[:, hf * HT:(hf + 1) * HT, :], nt[:, hf:hf + 1, :].broadcast_to([P, HT, E1]), ALU.add)
                   for hf in range(2)))
            for k, Mk in enumerate((M1, M2)):
                step(tt(A(c), A(a), A(Mk), ALU.mult))
                step(red(s2[:, :], A(c), ALU.add))
                step(lambda: v.tensor_copy(dest[:, k, :], s2[:, :]))
            cnt = t1[0:1, :, :].rearrange("p t e -> p (t e)")
            for hf in range(2):
                for lo in range(0, HPT, HPT // 2):
                    w = HPT // 2
                    sl = cnt[:, 0:w * E1].rearrange("p (t e) -> p t e", e=E1)
                    step(tt(sl, row[0:1, lo:lo + w].unsqueeze(2).broadcast_to([1, w, E1]),
                            x[0:1, hf:hf + 1, :].broadcast_to([1, w, E1]), ALU.is_ge))
                    step(red(wf[:, hf, lo:lo + w], sl, ALU.add))
            step(ts(A(wf), A(wf), float(E1 - 1), ALU.min))
            v.tensor_copy(which[:, :], wf[:, :, :].rearrange("p h t -> p (h t)"))

        @block.scalar
        def _(act):
            act.wait_ge(less_max, 1)
            nc.scalar.activation(rw[:, :, :], rw[:, :, :], ACT.Exp).then_inc(exps, 1)

        @block.tensor
        def _(pe):
            pe.wait_ge(chosen, 1)
            flat = Mb[:, :, :].rearrange("p t e -> p (t e)")
            for src, dst in ((before, pB), (onesb, pC)):
                for c in range(0, NT * E1, 512):
                    last = nc.tensor.matmul(dst[:, c:c + 512], src[:, :], flat[:, c:c + 512], start=True, stop=True)
            last.then_inc(ranked, 1)


def experts(nc, mem, io, keep):
    X, mean, rstd, ident = keep["X"], keep["mean"], keep["rstd"], keep["ident"]
    wt, dest, which = keep["wt"], keep["dest"], keep["which"]
    i32 = mybir.dt.int32
    NB = 4
    TR, RR = NT // 4 // 2, HPT // NB // 2
    W = mem.sb("W", [P, DC, E1, D])
    z = [mem.sb(f"z{f}", [P, D]) for f in range(4)]
    zw = [[mem.sb(f"zw{k}{f}", [P, D]) for f in range(4)] for k in range(2)]
    ix = [[mem.sb(f"ix{k}{f}", [P, 1], i32) for f in range(4)] for k in range(2)]
    iy = [[mem.sb(f"iy{k}{f}", [P, 1], i32) for f in range(4)] for k in range(2)]
    xin = [mem.sb(f"xin{k}", [P, NB, D]) for k in range(2)]
    xT = [mem.sb(f"xT{f}", [P, DC, P]) for f in range(4)]
    yout = [mem.sb(f"yout{k}", [P, NB, D]) for k in range(2)]
    y = [[mem.sb(f"y{k}{f}", [P, D]) for f in range(4)] for k in range(2)]
    w_loaded = [mem.sem(f"w_loaded{c}") for c in range(DC)]
    sent, got = ([[mem.sem(f"{n}{k}{f}") for f in range(4)] for k in range(2)] for n in ("sent", "got"))
    x_in, y_out = ([mem.sem(f"{n}{k}") for k in range(2)] for n in ("x_in", "y_out"))
    ready, seen, turned, xT_ready, multiplied, y_ready, named, added, stored = (mem.sem(n) for n in (
        "ready", "seen", "turned", "xT_ready", "multiplied", "y_ready", "named", "added", "stored"))
    pT = [mem.ps(f"pT{u}", [P, DC, P]) for u in range(2)]
    pY = [mem.ps(f"pY{u}", [P, D]) for u in range(2)]
    xgv, ygv = ([t.rearrange("(q n p) d -> q n p d", n=NB, p=P) for t in keep[n]] for n in ("xg", "yg"))
    ov = io["out"].rearrange("b (q n p) d -> (b q) p n d", n=4, p=P)
    with nc.Block() as block:
        @block.sync
        def _(sp):
            for c in range(DC):
                sp.dma_start(W[:, c, :, :], io["we"][:, c * P:(c + 1) * P, :].rearrange("e p d -> p e d")).then_inc(w_loaded[c], 16)
            for k in range(2):
                sp.sem_inc(y_out[k], 16)

            def load(hf, r, k):
                sp.wait_ge(turned, (r * 2 + k) * NB + NB)
                sp.dma_start(xin[k][:, :, :], xgv[hf][ds((r - hf * RR) * 2 + k, 1), :, :, :].rearrange("q n p d -> p (q n) d")).then_inc(x_in[k], 16)

            def keep_y(hf, r, k):
                sp.wait_ge(y_ready, (r * 2 + k) * NB + NB + 2)
                sp.dma_start(ygv[hf][ds((r - hf * RR) * 2 + k, 1), :, :, :].rearrange("q n p d -> p (q n) d"), yout[k][:, :, :]).then_inc(y_out[k], 16)
            for hf in range(2):
                for k in range(2):
                    for f in range(4):
                        sp.wait_ge(sent[k][f], 16 * TR * (hf + 1))
                for k in range(2):
                    load(hf, hf * RR, k)
                with sp.Fori(hf * RR + 1, hf * RR + RR) as r:
                    for k in range(2):
                        load(hf, r, k)
                        keep_y(hf, r - 1, k)
                for k in range(2):
                    keep_y(hf, hf * RR + RR - 1, k)
            for q in range(NT // 4):
                sp.wait_ge(added, q * 4 + 4 + 4)
                sp.dma_start(ov[q], X[:, q * 4:q * 4 + 4, :]).then_inc(stored, 16)
            sp.wait_ge(stored, 16 * (NT // 4))

        @block.vector
        def _(dve):
            v = nc.vector

            def copies(q):
                for f in range(4):
                    t = q * 4 + f
                    v.tensor_scalar(z[f][:, :].unsqueeze(1), X[:, ds(t, 1), :], mean[:, ds(t, 1)], rstd[:, ds(t, 1)], ALU.subtract, ALU.mult)
                    dve.drain()
                    for k in range(2):
                        if not (isinstance(q, int) and q == 0):
                            dve.wait_ge(sent[k][f], q * 16)
                        v.tensor_copy(ix[k][f][:, :], dest[:, k, ds(t, 1)])
                        v.tensor_scalar(zw[k][f][:, :], z[f][:, :], wt[:, k, ds(t, 1)], None, ALU.mult)
                    dve.drain().then_inc(ready, 1)
            copies(0)
            with dve.Fori(1, NT // 4) as q:
                copies(q)

            dve.sem_inc(added, 4)

            def name(q, f):
                for k in range(2):
                    v.tensor_copy(iy[k][f][:, :], dest[:, k, ds(q * 4 + f, 1)])
                dve.drain().then_inc(named, 1)

            def add(q, f):
                t = q * 4 + f
                for k in range(2):
                    dve.wait_ge(got[k][f], q * 16 + 16)
                v.tensor_tensor(X[:, ds(t, 1), :], X[:, ds(t, 1), :], y[0][f][:, :].unsqueeze(1), ALU.add)
                dve.drain()
                v.tensor_tensor(X[:, ds(t, 1), :], X[:, ds(t, 1), :], y[1][f][:, :].unsqueeze(1), ALU.add).then_inc(added, 1)
            for f in range(4):
                name(0, f)
            with dve.Fori(1, NT // 4) as q:
                for f in range(4):
                    add(q - 1, f)
                    name(q, f)
            for f in range(4):
                add(NT // 4 - 1, f)

        @block.gpsimd
        def _(pool):
            for hf in range(2):
                with pool.Fori(hf * TR, hf * TR + TR) as q:
                    for f in range(4):
                        pool.wait_ge(ready, q * 4 + f + 1)
                        pool.sem_inc(seen, 1)
                        for k in range(2):
                            nc.gpsimd.indirect_dma_start(out=keep["xg"][hf], out_offset=bass.IndirectOffsetOnAxis(ap=ix[k][f][:, 0:1], axis=0),
                                                         in_=zw[k][f][:, :], in_offset=None).then_inc(sent[k][f], 16)
            for hf in range(2):
                for k in range(2):
                    pool.wait_ge(y_out[k], 16 + 16 * RR * (hf + 1))
                with pool.Fori(hf * TR, hf * TR + TR) as q:
                    for f in range(4):
                        pool.wait_ge(named, q * 4 + f + 1)
                        pool.sem_inc(seen, 1)
                        for k in range(2):
                            nc.gpsimd.indirect_dma_start(out=y[k][f][:, :], out_offset=None, in_=keep["yg"][hf],
                                                         in_offset=bass.IndirectOffsetOnAxis(ap=iy[k][f][:, 0:1], axis=0)).then_inc(got[k][f], 16)

        @block.scalar
        def _(act):
            act.sem_inc(xT_ready, 2)
            act.sem_inc(y_ready, 2)
            with act.Fori(0, 2 * RR) as r:
                for k in range(2):
                    def turn(f):
                        act.wait_ge(turned, r * 8 + k * 4 + f + 9)
                        nc.scalar.activation(xT[f][:, :, :], pT[f % 2][:, :, :], ACT.Copy).then_inc(xT_ready, 1)

                    def product(f):
                        act.wait_ge(multiplied, r * 8 + k * 4 + f + 1)
                        nc.scalar.activation(yout[k][:, f, :], pY[f % 2][:, :], ACT.Copy).then_inc(y_ready, 1)
                    act.wait_ge(y_out[k], r * 16 + 16)
                    for f in range(NB):
                        turn(f)
                        if f:
                            product(f - 1)
                    product(NB - 1)

        @block.tensor
        def _(pe):
            pe.sem_inc(turned, 2 * NB)
            for c in range(DC):
                pe.wait_ge(w_loaded[c], 16)
            with pe.Fori(0, 2 * RR) as r:
                for k in range(2):
                    def turn(f):
                        pe.wait_ge(xT_ready, r * 8 + k * 4 + f + 1)
                        for c in range(DC):
                            last = nc.tensor.transpose(pT[f % 2][:, c, :], xin[k][:, f, c * P:(c + 1) * P], ident[:, :])
                        last.then_inc(turned, 1)

                    def multiply(f):
                        e = pe.value_load(which[0:1, ds(r * 8 + k * 4 + f, 1)], min_val=0, max_val=E1 - 1)
                        pe.wait_ge(xT_ready, r * 8 + k * 4 + f + 3)
                        pe.wait_ge(y_ready, r * 8 + k * 4 + f + 1)
                        for c in range(DC):
                            last = nc.tensor.matmul(pY[f % 2][:, :].unsqueeze(1), xT[f][:, c, :], W[:, c, ds(e, 1), :],
                                                    start=(c == 0), stop=(c == DC - 1))
                        last.then_inc(multiplied, 1)
                    pe.wait_ge(x_in[k], r * 16 + 16)
                    for f in range(NB):
                        turn(f)
                        if f:
                            multiply(f - 1)
                    multiply(NB - 1)


def build(nc, io):
    with ExitStack() as ctx:
        mem = Memory(nc, ctx, "all")
        keep = {"X": mem.sb("X", [P, NT, D]), "ident": mem.sb("ident", [P, P]), "identb": mem.sb("identb", [P, P], bf16),
                "mean": mem.sb("mean", [P, NT]), "rstd": mem.sb("rstd", [P, NT])}
        st = mem.sb("stats", [P, NT, 6])

        def stage(name, f, *args):
            with ExitStack() as sub:
                own = Memory(nc, sub, name)
                f(nc, own, *args)
                if name in ("in", "n1", "n2", "bd"):
                    own.clear()
        stage("in", load_and_constants, io, keep, st)
        keep["xg"] = [nc.dram_tensor(f"rows_in{hf}", (HPT * P, D), fp32).ap() for hf in range(2)]
        stage("n1", finish_rstd, keep, st, TPB, 1)
        stage("la", linear_attention, io, keep, st)
        stage("n2", finish_rstd, keep, st, NT, 2)
        stage("sm", soft_mixture, io, keep, st)
        keep["qk"] = nc.dram_tensor("rotated_qk", (B * G, TPB, P, P), fp32).ap()
        keep["v"] = nc.dram_tensor("values", (B * G, TPB, P, 4 * VW), fp32).ap()
        keep["ao"] = nc.dram_tensor("head_outputs", (B * G * (N // 512), 4, P, 4 * HD), fp32).ap()
        keep["yg"] = [nc.dram_tensor(f"rows_out{hf}", (HPT * P, D), fp32).ap() for hf in range(2)]
        keep["wt"] = mem.sb("wt", [P, 2, NT])
        keep["dest"] = mem.sb("dest", [P, 2, NT], mybir.dt.int32)
        keep["which"] = mem.sb("which", [1, 2 * HPT], mybir.dt.int32)
        keep["nmax"] = mem.sb("nmax", [P, B * G, TPB * 4])
        stage("n3", finish_rstd, keep, st, NT, 1)
        keep["need_max"] = mem.sb("need_max", [1, 1], mybir.dt.int32)
        with ExitStack() as sub:
            nn = Memory(nc, sub, "qk").sb("nn", [P, NT, 3 * H])
            stage("qk", project_qkv, io, keep, nn)
            stage("bd", bound_scores, io, keep, nn)
        stage("mx", row_maxima, io, keep)
        stage("at", attention, io, keep)
        stage("pr", project_out, io, keep, st)
        stage("n4", finish_rstd, keep, st, NT, 1)
        stage("rt", route, io, keep)
        stage("ex", experts, io, keep)


_OUTS = [((4, 2048, 256), 'float32')]


def kernel(**inputs):
    import numpy as _np
    import concourse.bacc as _bacc
    from concourse import mybir as _mybir
    from concourse.bass_utils import run_bass_kernel_spmd as _run

    nc = _bacc.Bacc("TRN2", target_bir_lowering=False, num_devices=1)
    c = _np.ascontiguousarray
    i = {k: _np.asarray(v) for k, v in inputs.items()}
    laid = {
        "x": c(i["L0_attn_x"]),
        "qkvT": c(i["L0_attn_qkv_w"].T), "qkv_b": c(i["L0_attn_qkv_b"]),
        "projT": c(i["L0_attn_proj_w"].T), "proj_b": c(i["L0_attn_proj_b"]),
        "pmT": c(i["L0_attn_projection_matrix"].T),
        "gamma": c(i["L0_ffn_ln_gamma"]), "beta": c(i["L0_ffn_ln_beta"]),
        "mu": c(i["L0_ffn_mu"].reshape(256, 256)), "scale": c(i["L0_ffn_scale"]),
        "w1": c(i["L0_ffn_w1"]), "b1": c(i["L0_ffn_b1"]), "w2": c(i["L0_ffn_w2"]), "b2": c(i["L0_ffn_b2"]),
        "WqT": c(i["L1_attn_Wq"].T), "WkT": c(i["L1_attn_Wk"].T), "WvT": c(i["L1_attn_Wv"].T),
        "WoT": c(i["L1_attn_Wo"].T),
        "routerT": c(i["L1_ffn_router_w"].T), "we": c(i["L1_ffn_expert_weights"]),
    }
    laid.update(tables())
    io, arrays = {}, {}
    for name, a in laid.items():
        arrays[f"in_{name}"] = a
        io[name] = nc.dram_tensor(f"in_{name}", a.shape, _mybir.dt.from_np(a.dtype), kind="ExternalInput").ap()
    for n, (shape, dtype) in enumerate(_OUTS):
        io["out"] = nc.dram_tensor(f"out_{n}_dram", shape, _mybir.dt.from_np(_np.dtype(dtype)), kind="ExternalOutput").ap()
    build(nc, io)
    r = _run(nc, [arrays], core_ids=[0])
    return r.results[0]["out_0_dram"]
```
